# Optimizing a Trainium2 kernel written in Bass

```python
import numpy as np
import jax
import jax.numpy as jnp

def _softmax(x, axis=-1):
    return jax.nn.softmax(x, axis=axis)

def _gelu(x):
    return jax.nn.gelu(x, approximate=True)

def _silu(x):
    return jax.nn.silu(x)

def _sigmoid(x):
    return jax.nn.sigmoid(x)

def _layernorm(x, axis=-1, eps=1e-05):
    m = jnp.mean(x, axis=axis, keepdims=True)
    v = jnp.var(x, axis=axis, keepdims=True)
    return (x - m) / jnp.sqrt(v + eps)

def _scatter_add(tgt, idx, src, axis=0):
    return tgt.at[idx].add(src)

def _segment_sum(src, seg, n):
    return jax.ops.segment_sum(src, seg, n)
kernel_name = 'mk_prb_d2_jaxref_r8_c255a3'

def setup_inputs(seed: int=0):
    np.random.seed(seed)
    _w = jnp.asarray

    def _L0_attn_setup():
        import jax, jax.numpy as jnp
        import numpy as np
        B, S, HID = (4, 512, 256)
        H, NB = (16, 4)
        D = HID // H
        EPS = 1e-06

        def elu_plus_one(x):
            return jax.nn.elu(x) + 1.0

        def _reference_tuple_inner(hidden_states, Wq, Wk, Wv, Wo, bank_weights, memories, memory_norms):
            b, s, _ = hidden_states.shape

            def proj(W):
                return (hidden_states @ W.T).reshape(b, s, H, D).transpose(0, 2, 1, 3)
            q, k, v = (proj(Wq), proj(Wk), proj(Wv))
            sigma_q = elu_plus_one(q)
            a_unnorm = jnp.einsum('bhsd,nhde->nbhse', sigma_q, memories)
            norm = jnp.einsum('bhsd,nhd->nbhs', sigma_q, memory_norms)
            a = a_unnorm / jnp.clip(norm, EPS, None)[..., None]
            active = (memory_norms.sum(axis=(1, 2)) >= EPS).astype(a.dtype)
            a = a * active[:, None, None, None, None]
            weights = jax.nn.softmax(bank_weights, axis=-1)
            combined = jnp.einsum('nbhse,hn->bhse', a, weights)
            sigma_k = elu_plus_one(k)
            mem0, norm0 = (memories[0], memory_norms[0])
            retr = jnp.einsum('bhsd,hde->bhse', sigma_k, mem0)
            knorm = jnp.clip(jnp.einsum('bhsd,hd->bhs', sigma_k, norm0), EPS, None)
            delta_v = v - retr / knorm[..., None]
            mem_update = jnp.einsum('bhsd,bhse->hde', sigma_k, delta_v) / (b * s)
            new_mem0 = jax.lax.stop_gradient(mem0 + mem_update)
            new_norm0 = jax.lax.stop_gradient(norm0 + sigma_k.sum(axis=(0, 2)) / b)
            out = combined.transpose(0, 2, 1, 3).reshape(b, s, HID) @ Wo.T
            return (out, new_mem0, new_norm0)
        key = jax.random.key(seed)
        ks = jax.random.split(key, 8)
        return {'hidden_states': jax.random.normal(ks[0], (B, S, HID), jnp.float32), 'Wq': jax.random.normal(ks[1], (HID, HID), jnp.float32) * 0.02, 'Wk': jax.random.normal(ks[2], (HID, HID), jnp.float32) * 0.02, 'Wv': jax.random.normal(ks[3], (HID, HID), jnp.float32) * 0.02, 'Wo': jax.random.normal(ks[4], (HID, HID), jnp.float32) * 0.02, 'bank_weights': jax.random.normal(ks[5], (H, NB), jnp.float32) * 0.02, 'memories': jax.random.uniform(ks[6], (NB, H, D, D), jnp.float32), 'memory_norms': jax.random.uniform(ks[7], (NB, H, D), jnp.float32)}
    _L0_attn_in = _L0_attn_setup()

    def _L0_ffn_setup():
        import jax, jax.numpy as jnp
        import numpy as np
        BF16 = jnp.bfloat16
        E4M3 = jnp.float8_e4m3fn
        FEATURES = 256
        HIDDEN = 1024
        B, S = (4, 256)

        def _qdot(x, w, out_dtype=BF16):
            return jnp.dot(x.astype(E4M3), w.astype(E4M3), preferred_element_type=out_dtype)
        key = jax.random.key(seed)
        k1, k2, k3 = jax.random.split(key, 3)
        x = jax.random.normal(k1, (B, S, FEATURES), dtype=BF16)
        w_gating = jax.random.normal(k2, (2, FEATURES, HIDDEN), dtype=jnp.float32) / np.sqrt(FEATURES)
        w_linear = jax.random.normal(k3, (HIDDEN, FEATURES), dtype=jnp.float32) / np.sqrt(HIDDEN)
        return {'x': x, 'w_gating': w_gating, 'w_linear': w_linear}
    _L0_ffn_in = _L0_ffn_setup()

    def _L1_attn_setup():
        import jax, jax.numpy as jnp
        import numpy as np
        H = 16
        NOPE = 128
        ROPE = 64
        VD = 128
        KVR = 64
        QKD = NOPE + ROPE
        EPS = 1e-06

        def rms_norm(x, w):
            nrm = jax.lax.rsqrt(jnp.mean(x.astype(jnp.float32) ** 2, axis=-1, keepdims=True) + EPS)
            return (x.astype(jnp.float32) * nrm).astype(x.dtype) * w

        def rope_cos_sin(T, dim, base=10000.0):
            inv = 1.0 / base ** (jnp.arange(0, dim, 2, dtype=jnp.float32) / dim)
            f = jnp.outer(jnp.arange(T, dtype=jnp.float32), inv)
            emb = jnp.concatenate([f, f], axis=-1)
            return (jnp.cos(emb), jnp.sin(emb))

        def rotate_half(x):
            x1, x2 = jnp.split(x, 2, axis=-1)
            return jnp.concatenate([-x2, x1], axis=-1)

        def apply_rope(x, cos, sin):
            return x * cos[None, None] + rotate_half(x) * sin[None, None]
        key = jax.random.key(seed)
        ks = jax.random.split(key, 6)
        B, T, D = (2, 256, 256)
        s = 0.02
        return {'x': jax.random.normal(ks[0], (B, T, D), jnp.float32), 'wq': jax.random.normal(ks[1], (D, H * QKD), jnp.float32) * s, 'wkv_a': jax.random.normal(ks[2], (D, KVR + ROPE), jnp.float32) * s, 'wkv_b': jax.random.normal(ks[3], (KVR, H * (NOPE + VD)), jnp.float32) * s, 'wo': jax.random.normal(ks[4], (H * VD, D), jnp.float32) * s, 'kv_norm_w': jnp.ones((KVR,), jnp.float32)}
    _L1_attn_in = _L1_attn_setup()

    def _L1_ffn_setup():
        import jax, jax.numpy as jnp
        import numpy as np
        B, L, D = (2, 128, 256)
        E, TOP_K, RANK, DFF = (8, 2, 8, 688)

        def _lora(x, A, Bm, scale):
            return x @ A @ Bm * scale

        def _expert_lora(x, A, Bm, w, scale):
            xA = jnp.einsum('bld,edr->bler', x, A)
            xAB = jnp.einsum('bler,erd->bled', xA, Bm) * scale
            return (xAB * w).sum(axis=2)
        key = jax.random.key(seed)
        ks = jax.random.split(key, 18)
        r = lambda k, s, sc: jax.random.normal(k, s, dtype=jnp.float32) * sc
        inv_d = 1.0 / np.sqrt(D)
        inv_f = 1.0 / np.sqrt(DFF)
        return {'x': r(ks[0], (B, L, D), 1.0), 'W_router': r(ks[1], (D, E), inv_d), 'W_gate': r(ks[2], (D, DFF), inv_d), 'W_up': r(ks[3], (D, DFF), inv_d), 'W_down': r(ks[4], (DFF, D), inv_f), 'sA_gate': r(ks[5], (D, RANK), inv_d), 'sB_gate': r(ks[6], (RANK, DFF), 0.02), 'sA_up': r(ks[7], (D, RANK), inv_d), 'sB_up': r(ks[8], (RANK, DFF), 0.02), 'sA_down': r(ks[9], (DFF, RANK), inv_f), 'sB_down': r(ks[10], (RANK, D), 0.02), 'A_gate': r(ks[11], (E, D, RANK), inv_d), 'B_gate': r(ks[12], (E, RANK, DFF), 0.02), 'A_up': r(ks[13], (E, D, RANK), inv_d), 'B_up': r(ks[14], (E, RANK, DFF), 0.02), 'A_down': r(ks[15], (E, DFF, RANK), inv_f), 'B_down': r(ks[16], (E, RANK, D), 0.02), 'expert_bias': jnp.zeros((E,), dtype=jnp.float32)}
    _L1_ffn_in = _L1_ffn_setup()
    _d = {'L0_attn_hidden_states': _L0_attn_in['hidden_states'], 'L0_attn_Wq': _L0_attn_in['Wq'], 'L0_attn_Wk': _L0_attn_in['Wk'], 'L0_attn_Wv': _L0_attn_in['Wv'], 'L0_attn_Wo': _L0_attn_in['Wo'], 'L0_attn_bank_weights': _L0_attn_in['bank_weights'], 'L0_attn_memories': _L0_attn_in['memories'], 'L0_attn_memory_norms': _L0_attn_in['memory_norms'], 'L0_ffn_w_gating': _L0_ffn_in['w_gating'], 'L0_ffn_w_linear': _L0_ffn_in['w_linear'], 'L1_attn_wq': _L1_attn_in['wq'], 'L1_attn_wkv_a': _L1_attn_in['wkv_a'], 'L1_attn_wkv_b': _L1_attn_in['wkv_b'], 'L1_attn_wo': _L1_attn_in['wo'], 'L1_attn_kv_norm_w': _L1_attn_in['kv_norm_w'], 'L1_ffn_W_router': _L1_ffn_in['W_router'], 'L1_ffn_W_gate': _L1_ffn_in['W_gate'], 'L1_ffn_W_up': _L1_ffn_in['W_up'], 'L1_ffn_W_down': _L1_ffn_in['W_down'], 'L1_ffn_sA_gate': _L1_ffn_in['sA_gate'], 'L1_ffn_sB_gate': _L1_ffn_in['sB_gate'], 'L1_ffn_sA_up': _L1_ffn_in['sA_up'], 'L1_ffn_sB_up': _L1_ffn_in['sB_up'], 'L1_ffn_sA_down': _L1_ffn_in['sA_down'], 'L1_ffn_sB_down': _L1_ffn_in['sB_down'], 'L1_ffn_A_gate': _L1_ffn_in['A_gate'], 'L1_ffn_B_gate': _L1_ffn_in['B_gate'], 'L1_ffn_A_up': _L1_ffn_in['A_up'], 'L1_ffn_B_up': _L1_ffn_in['B_up'], 'L1_ffn_A_down': _L1_ffn_in['A_down'], 'L1_ffn_B_down': _L1_ffn_in['B_down'], 'L1_ffn_expert_bias': _L1_ffn_in['expert_bias']}
    _x0 = _d['L0_attn_hidden_states']
    _d['L0_attn_hidden_states'] = jax.random.normal(jax.random.fold_in(jax.random.key(seed), 1), (2, 1024, 256), dtype=_x0.dtype)
    del _x0
    return _d

def reference(L0_attn_hidden_states, L0_attn_Wq, L0_attn_Wk, L0_attn_Wv, L0_attn_Wo, L0_attn_bank_weights, L0_attn_memories, L0_attn_memory_norms, L0_ffn_w_gating, L0_ffn_w_linear, L1_attn_wq, L1_attn_wkv_a, L1_attn_wkv_b, L1_attn_wo, L1_attn_kv_norm_w, L1_ffn_W_router, L1_ffn_W_gate, L1_ffn_W_up, L1_ffn_W_down, L1_ffn_sA_gate, L1_ffn_sB_gate, L1_ffn_sA_up, L1_ffn_sB_up, L1_ffn_sA_down, L1_ffn_sB_down, L1_ffn_A_gate, L1_ffn_B_gate, L1_ffn_A_up, L1_ffn_B_up, L1_ffn_A_down, L1_ffn_B_down, L1_ffn_expert_bias):

    def _L0_attn_ref(hidden_states, Wq, Wk, Wv, Wo, bank_weights, memories, memory_norms):
        import jax, jax.numpy as jnp
        import numpy as np
        B, S, HID = (4, 512, 256)
        H, NB = (16, 4)
        D = HID // H
        EPS = 1e-06

        def elu_plus_one(x):
            return jax.nn.elu(x) + 1.0

        def _reference_tuple_inner(hidden_states, Wq, Wk, Wv, Wo, bank_weights, memories, memory_norms):
            b, s, _ = hidden_states.shape

            def proj(W):
                return (hidden_states @ W.T).reshape(b, s, H, D).transpose(0, 2, 1, 3)
            q, k, v = (proj(Wq), proj(Wk), proj(Wv))
            sigma_q = elu_plus_one(q)
            a_unnorm = jnp.einsum('bhsd,nhde->nbhse', sigma_q, memories)
            norm = jnp.einsum('bhsd,nhd->nbhs', sigma_q, memory_norms)
            a = a_unnorm / jnp.clip(norm, EPS, None)[..., None]
            active = (memory_norms.sum(axis=(1, 2)) >= EPS).astype(a.dtype)
            a = a * active[:, None, None, None, None]
            weights = jax.nn.softmax(bank_weights, axis=-1)
            combined = jnp.einsum('nbhse,hn->bhse', a, weights)
            sigma_k = elu_plus_one(k)
            mem0, norm0 = (memories[0], memory_norms[0])
            retr = jnp.einsum('bhsd,hde->bhse', sigma_k, mem0)
            knorm = jnp.clip(jnp.einsum('bhsd,hd->bhs', sigma_k, norm0), EPS, None)
            delta_v = v - retr / knorm[..., None]
            mem_update = jnp.einsum('bhsd,bhse->hde', sigma_k, delta_v) / (b * s)
            new_mem0 = jax.lax.stop_gradient(mem0 + mem_update)
            new_norm0 = jax.lax.stop_gradient(norm0 + sigma_k.sum(axis=(0, 2)) / b)
            out = combined.transpose(0, 2, 1, 3).reshape(b, s, HID) @ Wo.T
            return (out, new_mem0, new_norm0)
        return _reference_tuple_inner(hidden_states, Wq, Wk, Wv, Wo, bank_weights, memories, memory_norms)[0]

    def _L0_ffn_ref(x, w_gating, w_linear):
        import jax, jax.numpy as jnp
        import numpy as np
        BF16 = jnp.bfloat16
        E4M3 = jnp.float8_e4m3fn
        FEATURES = 256
        HIDDEN = 1024
        B, S = (4, 256)

        def _qdot(x, w, out_dtype=BF16):
            return jnp.dot(x.astype(E4M3), w.astype(E4M3), preferred_element_type=out_dtype)
        ff_gate = _qdot(x, w_gating[0])
        gate_value = jax.nn.gelu(ff_gate)
        ff1 = _qdot(x, w_gating[1])
        activations = gate_value * ff1
        outputs = _qdot(activations, w_linear)
        return outputs

    def _L1_attn_ref(x, wq, wkv_a, wkv_b, wo, kv_norm_w):
        import jax, jax.numpy as jnp
        import numpy as np
        H = 16
        NOPE = 128
        ROPE = 64
        VD = 128
        KVR = 64
        QKD = NOPE + ROPE
        EPS = 1e-06

        def rms_norm(x, w):
            nrm = jax.lax.rsqrt(jnp.mean(x.astype(jnp.float32) ** 2, axis=-1, keepdims=True) + EPS)
            return (x.astype(jnp.float32) * nrm).astype(x.dtype) * w

        def rope_cos_sin(T, dim, base=10000.0):
            inv = 1.0 / base ** (jnp.arange(0, dim, 2, dtype=jnp.float32) / dim)
            f = jnp.outer(jnp.arange(T, dtype=jnp.float32), inv)
            emb = jnp.concatenate([f, f], axis=-1)
            return (jnp.cos(emb), jnp.sin(emb))

        def rotate_half(x):
            x1, x2 = jnp.split(x, 2, axis=-1)
            return jnp.concatenate([-x2, x1], axis=-1)

        def apply_rope(x, cos, sin):
            return x * cos[None, None] + rotate_half(x) * sin[None, None]
        B, T, D = x.shape
        q = (x @ wq).reshape(B, T, H, QKD)
        q_nope, q_rope = (q[..., :NOPE], q[..., NOPE:])
        kvc = x @ wkv_a
        kv_latent = rms_norm(kvc[..., :KVR], kv_norm_w)
        k_rope_raw = kvc[..., KVR:]
        cos, sin = rope_cos_sin(T, ROPE)
        q_rope = apply_rope(jnp.transpose(q_rope, (0, 2, 1, 3)), cos, sin)
        k_rope = apply_rope(k_rope_raw[:, None], cos, sin)
        kv_full = (kv_latent @ wkv_b).reshape(B, T, H, NOPE + VD)
        k_nope = jnp.transpose(kv_full[..., :NOPE], (0, 2, 1, 3))
        v = jnp.transpose(kv_full[..., NOPE:], (0, 2, 1, 3))
        k = jnp.concatenate([k_nope, jnp.broadcast_to(k_rope, (B, H, T, ROPE))], axis=-1)
        qf = jnp.concatenate([jnp.transpose(q_nope, (0, 2, 1, 3)), q_rope], axis=-1)
        scale = QKD ** (-0.5)
        att = jnp.einsum('bhqd,bhkd->bhqk', qf, k) * scale
        causal = jnp.triu(jnp.full((T, T), -jnp.inf, jnp.float32), k=1)
        att = att + causal[None, None]
        att = jax.nn.softmax(att.astype(jnp.float32), axis=-1).astype(x.dtype)
        y = jnp.einsum('bhqk,bhkd->bhqd', att, v)
        y = jnp.transpose(y, (0, 2, 1, 3)).reshape(B, T, H * VD)
        return y @ wo

    def _L1_ffn_ref(x, W_router, W_gate, W_up, W_down, sA_gate, sB_gate, sA_up, sB_up, sA_down, sB_down, A_gate, B_gate, A_up, B_up, A_down, B_down, expert_bias):
        import jax, jax.numpy as jnp
        import numpy as np
        B, L, D = (2, 128, 256)
        E, TOP_K, RANK, DFF = (8, 2, 8, 688)

        def _lora(x, A, Bm, scale):
            return x @ A @ Bm * scale

        def _expert_lora(x, A, Bm, w, scale):
            xA = jnp.einsum('bld,edr->bler', x, A)
            xAB = jnp.einsum('bler,erd->bled', xA, Bm) * scale
            return (xAB * w).sum(axis=2)
        scale = 1.0 / RANK
        logits = x @ W_router
        scores = jax.nn.sigmoid(logits)
        biased = scores + expert_bias
        _, topk_idx = jax.lax.top_k(biased, TOP_K)
        topk_scores = jnp.take_along_axis(scores, topk_idx, axis=-1)
        topk_w = topk_scores / (topk_scores.sum(-1, keepdims=True) + 1e-08)
        one_hot = jax.nn.one_hot(topk_idx, E, dtype=x.dtype)
        expert_weights = (one_hot * topk_w[..., None]).sum(axis=2)
        w = expert_weights[..., None]
        gate = x @ W_gate + _lora(x, sA_gate, sB_gate, scale) + _expert_lora(x, A_gate, B_gate, w, scale)
        up = x @ W_up + _lora(x, sA_up, sB_up, scale) + _expert_lora(x, A_up, B_up, w, scale)
        hidden = jax.nn.silu(gate) * up
        out = hidden @ W_down + _lora(hidden, sA_down, sB_down, scale) + _expert_lora(hidden, A_down, B_down, w, scale)
        return out
    x = L0_attn_hidden_states
    xn = _layernorm(x, axis=-1)
    x = x + _L0_attn_ref(xn, L0_attn_Wq, L0_attn_Wk, L0_attn_Wv, L0_attn_Wo, L0_attn_bank_weights, L0_attn_memories, L0_attn_memory_norms) + _L0_ffn_ref(xn, L0_ffn_w_gating, L0_ffn_w_linear)
    xn = _layernorm(x, axis=-1)
    x = x + _L1_attn_ref(xn, L1_attn_wq, L1_attn_wkv_a, L1_attn_wkv_b, L1_attn_wo, L1_attn_kv_norm_w) + _L1_ffn_ref(xn, L1_ffn_W_router, L1_ffn_W_gate, L1_ffn_W_up, L1_ffn_W_down, L1_ffn_sA_gate, L1_ffn_sB_gate, L1_ffn_sA_up, L1_ffn_sB_up, L1_ffn_sA_down, L1_ffn_sB_down, L1_ffn_A_gate, L1_ffn_B_gate, L1_ffn_A_up, L1_ffn_B_up, L1_ffn_A_down, L1_ffn_B_down, L1_ffn_expert_bias)
    return x

_drawn_inputs = setup_inputs


def setup_inputs(seed=0):
    import zlib

    import numpy as np

    out = dict(_drawn_inputs(seed))
    spreads = {'L1_attn_kv_norm_w': (1.0, 0.6), 'L1_ffn_expert_bias': (0.0, 0.8)}
    factors = {'L0_attn_Wq': 6.456,
     'L0_attn_bank_weights': 24.937,
     'L1_attn_wq': 8.0,
     'L1_ffn_W_router': 8.0,
     'L1_ffn_sA_gate': 8.0,
     'L1_ffn_sB_gate': 8.0,
     'L1_ffn_sA_up': 8.0,
     'L1_ffn_sB_up': 8.0,
     'L1_ffn_sA_down': 8.0,
     'L1_ffn_sB_down': 8.0,
     'L1_ffn_A_gate': 8.0,
     'L1_ffn_B_gate': 8.0,
     'L1_ffn_A_up': 8.0,
     'L1_ffn_B_up': 8.0,
     'L1_ffn_A_down': 8.0,
     'L1_ffn_B_down': 8.0}
    for name, (base, spread) in spreads.items():
        noise = np.random.default_rng([zlib.crc32(name.encode()), seed]).standard_normal(out[name].shape)
        drawn = base * np.exp(spread * noise) if base else spread * noise
        out[name] = jnp.asarray(drawn.astype(out[name].dtype))
    for name, factor in factors.items():
        out[name] = (out[name] * factor).astype(out[name].dtype)
    return out
```

```python
import concourse.bass as bass
from concourse import mybir
from contextlib import ExitStack

B, T, D = 2, 1024, 256
H0, D0, NB = 16, 16, 4
HID = 1024
H, NOPE, ROPE, VD, KVR = 16, 128, 64, 128, 64
E, RANK, DFF = 8, 8, 688
CH = 512
NC = T // CH
TPC = CH // 128
KD = D // 128
FM = [(m * 128, min(128, DFF - m * 128)) for m in range((DFF + 127) // 128)]
NM = len(FM)
SCALE = (NOPE + ROPE) ** -0.5
LN_EPS, MEM_EPS, RMS_EPS = 1e-5, 1e-6, 1e-6
MASKED = -1e30
GELU_C, GELU_S = 0.044677734375, 0.796875

C_ID, C_MASK, C_SEL = 0, 128, 256
C_TRI = C_SEL + 8 * 128
C_BLK = C_TRI + 64
C_COS = C_BLK + 64
C_SIN = C_COS + 8 * 64
C_END = C_SIN + 8 * 64

DVE_LINKS = 58


def fused_two_layers(nc, x_in, const_in, wq0_in, wo0_in, mem_in, mnorm_in, mrow_in, bw_in, bwself_in,
                     wg_in, wl_in, wqT_in, wkT_in, wqr_in, wvT_in, wo_in, wkva_in, kvw_in,
                     ra_in, wgu_in, wd_in, lora_in, bgu_in, ad_in, bd_in, ebias_in, out):
    fp32, bf16, fp8 = mybir.dt.float32, mybir.dt.bfloat16, mybir.dt.float8e4
    ALU, ACT, AX = mybir.AluOpType, mybir.ActivationFunctionType, mybir.AxisListType

    ctx = ExitStack()
    with ctx:
        def sb(name, shape, dt=fp32):
            return ctx.enter_context(nc.sbuf_tensor(name, shape, dt))

        def sem(name):
            return ctx.enter_context(nc.semaphore(name))

        xg = sb("xg", [128, NC, TPC, D])
        const = sb("const", [128, C_END])
        ident = const[:, C_ID:C_ID + 128]
        sel = const[:, C_SEL:C_TRI].rearrange("p (j c) -> p j c", j=8)
        tri = const[:, C_TRI:C_BLK].rearrange("p (e f) -> p e f", e=E)
        blk = const[:, C_BLK:C_COS]
        cos = const[:, C_COS:C_SIN].rearrange("p (t r) -> p t r", t=8)
        sin = const[:, C_SIN:C_END].rearrange("p (t r) -> p t r", t=8)
        identb = sb("identb", [128, 128], bf16)
        maskb = sb("maskb", [128, 128], bf16)
        wq0 = sb("wq0", [128, KD, D])
        wo0 = sb("wo0", [128, KD, D])
        mem = sb("mem", [128, 8, 128])
        mnorm = sb("mnorm", [128, KD, 64])
        mrow = sb("mrow", [64, D0])
        bw = sb("bw", [64, NB])
        bwself = sb("bwself", [64, 1])
        bankw = sb("bankw", [64, 1])
        bsm = sb("bsm", [64, 16])
        wg8 = sb("wg8", [128, KD, 2, HID], fp8)
        wl8 = sb("wl8", [128, HID // 128, D], fp8)
        WQH = sb("WQH", [128, KD, H, 128], bf16)
        WQL = sb("WQL", [128, KD, H, 128], bf16)
        GH = sb("GH", [128, H, D], bf16)
        GL = sb("GL", [128, H, D], bf16)
        KVH = sb("KVH", [128, KD, 128], bf16)
        KVL = sb("KVL", [128, KD, 128], bf16)
        kvw = sb("kvw", [128, KVR])
        ra = sb("ra", [128, KD, 136])
        GUH = sb("GUH", [128, KD, 2, DFF], bf16)
        GUL = sb("GUL", [128, KD, 2, DFF], bf16)
        WDH = sb("WDH", [128, NM, D], bf16)
        WDL = sb("WDL", [128, NM, D], bf16)
        BGH = sb("BGH", [128, DFF], bf16)
        BGL = sb("BGL", [128, DFF], bf16)
        ADH = sb("ADH", [128, NM, 64], bf16)
        ADL = sb("ADL", [128, NM, 64], bf16)
        BDH = sb("BDH", [64, D], bf16)
        BDL = sb("BDL", [64, D], bf16)
        ebias = sb("ebias", [128, E])
        KTH = sb("KTH", [128, T], bf16)
        KTL = sb("KTL", [128, T], bf16)
        LAT = sb("LAT", [128, T // 128, 128], bf16)
        XH = sb("XH", [128, KD, CH], bf16)
        XL = sb("XL", [128, KD, CH], bf16)
        nhalf = sb("nhalf", [128, TPC])
        stats = sb("stats", [128, TPC, 6])
        mv = sb("mv", [128, TPC, 2])
        ve = sb("ve", [128, TPC])
        rstd = sb("rstd", [128, TPC])
        nm = sb("nm", [128, 8])
        rs = sb("rs", [128, 8])
        rl = sb("rl", [128, 8])

        ARENA = 25700
        arena = sb("arena", [128, ARENA])

        class Cut:
            def __init__(self):
                self.at = 0

            def take(self, words, dt=fp32):
                a = arena[:, self.at:self.at + words]
                self.at += words
                assert self.at <= ARENA, self.at
                return a if dt == fp32 else a.bitcast(dt)

        cut = Cut()
        r_wqT = cut.take(H * D).rearrange("p (h d) -> p h d", h=H)
        r_wkT = cut.take(H * 64).rearrange("p (h d) -> p h d", h=H)
        r_wqr = cut.take(KD * H * 64).rearrange("p (k h d) -> p k h d", k=KD, h=H)
        r_wvT = cut.take(H * 64).rearrange("p (h d) -> p h d", h=H)
        r_wo = cut.take(H * D).rearrange("p (h d) -> p h d", h=H)
        r_kva = cut.take(KD * 128).rearrange("p (k d) -> p k d", k=KD)
        r_gu = cut.take(KD * 2 * DFF).rearrange("p (k g d) -> p k g d", k=KD, g=2)
        r_wd = cut.take(NM * D).rearrange("p (m d) -> p m d", m=NM)
        r_lora = cut.take(DFF + D)
        r_bgu = cut.take(DFF)
        r_ad = cut.take(NM * 64).rearrange("p (m d) -> p m d", m=NM)
        r_bd = cut.take(D)
        r_wg = cut.take(KD * 2 * HID).rearrange("p (k g d) -> p k g d", k=KD, g=2)
        r_wl = cut.take(8 * D).rearrange("p (k d) -> p k d", k=8)

        cut = Cut()
        xn = cut.take(TPC * D).rearrange("p (t d) -> p t d", t=TPC)
        xnT = cut.take(KD * CH).rearrange("p (k n) -> p k n", k=KD)
        xq8 = cut.take(KD * CH // 4, fp8).rearrange("p (k n) -> p k n", k=KD)
        ex = cut.take(KD * CH).rearrange("p (k n) -> p k n", k=KD)
        sig = cut.take(KD * CH).rearrange("p (k n) -> p k n", k=KD)
        sn = cut.take(2 * CH).rearrange("p (b n) -> p b n", b=2)
        rnorm = cut.take(CH)
        gcp = cut.take(4 * CH, bf16).rearrange("p (b g n) -> p b g n", b=4, g=2)
        ucp = cut.take(4 * CH, bf16).rearrange("p (b g n) -> p b g n", b=4, g=2)
        inner = cut.take(2 * CH, bf16).rearrange("p (b g n) -> p b g n", b=2, g=2)
        tanhg = cut.take(2 * CH, bf16).rearrange("p (b g n) -> p b g n", b=2, g=2)
        act8 = cut.take(8 * CH // 4, fp8).rearrange("p (k n) -> p k n", k=8)
        combT = cut.take(KD * CH).rearrange("p (k n) -> p k n", k=KD)
        fb = cut.take(TPC * D // 2, bf16).rearrange("p (t d) -> p t d", t=TPC)
        th = cut.take(TPC * E).rearrange("p (t e) -> p t e", t=TPC)
        bi = cut.take(TPC * E).rearrange("p (t e) -> p t e", t=TPC)
        cmp1 = cut.take(TPC * 64).rearrange("p (t e f) -> p t e f", t=TPC, e=E)
        cmp2 = cut.take(TPC * 64).rearrange("p (t e f) -> p t e f", t=TPC, e=E)
        rank = cut.take(TPC * E).rearrange("p (t e) -> p t e", t=TPC)
        wex = cut.take(TPC * E).rearrange("p (t e) -> p t e", t=TPC)
        den = cut.take(TPC)
        xaw = cut.take(TPC * 128).rearrange("p (t c) -> p t c", t=TPC)
        ZH = cut.take(CH // 2, bf16)
        ZL = cut.take(CH // 2, bf16)
        kvs = cut.take(TPC * 128).rearrange("p (t c) -> p t c", t=TPC)
        ktok = cut.take(TPC * 128).rearrange("p (t c) -> p t c", t=TPC)
        ksq = cut.take(TPC * 64).rearrange("p (t c) -> p t c", t=TPC)
        kr1 = cut.take(TPC * 64).rearrange("p (t c) -> p t c", t=TPC)
        kr2 = cut.take(TPC * 64).rearrange("p (t c) -> p t c", t=TPC)
        kss = cut.take(TPC)
        knr = cut.take(TPC)
        tt = cut.take(2 * CH).rearrange("p (b n) -> p b n", b=2)
        a1 = cut.take(2 * CH).rearrange("p (b n) -> p b n", b=2)
        hf = cut.take(2 * CH).rearrange("p (b n) -> p b n", b=2)
        HH = cut.take(NM * CH // 2, bf16).rearrange("p (m n) -> p m n", m=NM)
        HL = cut.take(NM * CH // 2, bf16).rearrange("p (m n) -> p m n", m=NM)
        zw = cut.take(TPC * 64).rearrange("p (t c) -> p t c", t=TPC)
        Z2H = cut.take(CH // 2, bf16)
        Z2L = cut.take(CH // 2, bf16)

        cut = Cut()
        QTH = cut.take(H * CH // 2, bf16).rearrange("p (h n) -> p h n", h=H)
        QTL = cut.take(H * CH // 2, bf16).rearrange("p (h n) -> p h n", h=H)
        P = cut.take(2 * TPC * T).rearrange("p (b t n) -> p b t n", b=2, t=TPC)
        qtok = cut.take(2 * 512).rearrange("p (b h c) -> p b h c", b=2, h=4)
        qr1 = cut.take(2 * 256).rearrange("p (b h c) -> p b h c", b=2, h=4)
        qr2 = cut.take(2 * 256).rearrange("p (b h c) -> p b h c", b=2, h=4)
        PH = cut.take(CH, bf16).rearrange("p (b n) -> p b n", b=2)
        PL = cut.take(CH, bf16).rearrange("p (b n) -> p b n", b=2)

        ps = ctx.enter_context(nc.psum_tensor("ps", [128, 8, 512], fp32))

        def token_major(bank, t):
            return ps[:, bank + t // 2, (t % 2) * 256:(t % 2) * 256 + D]

        def token_major_all(bank):
            return ps[:, bank:bank + 2, :].rearrange("p b (t d) -> p (b t) d", t=2)

        loads = ["const", "small", "l0", "wg", "wl", "wq", "wv", "kva", "gu", "wd", "tail"]
        ld = {n: sem("loaded_" + n) for n in loads}
        x_loaded = [sem(f"x_loaded{c}") for c in range(NC)]
        prep_mm = sem("prep_mm")
        prep_hi = sem("prep_hi")
        prep_lo = sem("prep_lo")
        prep_dve = sem("prep_dve")
        prep_act = sem("prep_act")
        prep_done = sem("prep_done")
        half_set = sem("half_set")
        passed = sem("passed")
        link = sem("dve_link")
        names = """var_ready rstd_ready xn_ready xT_ready xnT_ready xq8_ready xsplit_ready q_ready e_ready sig_ready
        gu_ready gate_copied up_copied sq_ready inner_ready tanh_ready act8_ready norm_ready r_ready rbc_ready sn_ready comb_done
        combT_ready y0_ready y1_ready fb_ready ra_ready th_ready kvc_ready kvs_ready kss_ready knr_ready ktok_ready
        kT_ready kth_ready ktl_ready xaw_ready xawT_ready zh_ready zl_ready m_ready tt_ready hf_ready hh_ready hs_ready
        z_ready zw_ready z2T_ready z2h_ready z2l_ready y2_ready x2_ready
        qp_ready qn_ready qr_ready qrope_parts qt_ready qth_ready qtl_ready
        s_ready max_ready exp_done rl_ready pn_ready pt_ready pth_ready ptl_ready pv_done cth_ready ctl_ready
        o_ready out_ready""".split()
        S = {n: sem(n) for n in names}
        stored = sem("stored")

        block = ctx.enter_context(nc.Block())

        def row(c):
            return slice(c * CH, (c + 1) * CH)

        def plain(eng):
            eng.sem_inc(passed, 1)

        @block.sync
        def _(sp):
            def load(dst, src, name):
                sp.dma_start(dst, src).then_inc(ld[name], 16)

            def x_rows(b, c):
                return x_in[b, row(c), :].rearrange("(t p) d -> p t d", p=128)

            def out_rows(b, c):
                return out[b, row(c), :].rearrange("(t p) d -> p t d", p=128)

            load(const[:, :], const_in, "const")
            for c in range(NC):
                sp.dma_start(xg[:, c], x_rows(0, c)).then_inc(x_loaded[c], 16)
            load(r_wg.rearrange("p k g n -> p k (g n)"), wg_in.rearrange("(k p) g n -> p k (g n)", p=128), "wg")
            load(r_wl, wl_in.rearrange("(k p) n -> p k n", p=128), "wl")
            load(r_wqT, wqT_in, "wq")
            load(r_wkT, wkT_in, "wq")
            load(r_wqr.rearrange("p k h n -> p k (h n)"), wqr_in.rearrange("(k p) h n -> p k (h n)", p=128), "wq")
            for b in range(B):
                for c in range(NC):
                    sp.wait_ge(S["out_ready"], b * NC + c + 1)
                    sp.dma_start(out_rows(b, c), xg[:, c]).then_inc(stored, 16)
                    if b + 1 < B:
                        sp.wait_ge(stored, 16 * (b * NC + c + 1))
                        sp.dma_start(xg[:, c], x_rows(b + 1, c)).then_inc(x_loaded[c], 16)
            sp.wait_ge(stored, 16 * B * NC)

        @block.gpsimd
        def _(pool):
            def load(dst, src, name):
                pool.dma_start(dst, src).then_inc(ld[name], 16)

            nc.gpsimd.memset(nhalf[:, :], -0.5).then_inc(half_set, 1)
            load(r_wvT, wvT_in, "wv")
            load(r_wo, wo_in.rearrange("(h p) n -> p h n", p=128), "wv")
            pool.wait_ge(half_set, 1)
            with pool.Fori(0, B) as b:
                for c in range(NC):
                    n = b * NC + c
                    for l in range(2):
                        pool.wait_ge(S["var_ready"], n * 2 + l + 1)
                        nc.gpsimd.tensor_tensor(rstd[:, :], ve[:, :], nhalf[:, :], ALU.pow) \
                            .then_inc(S["rstd_ready"], 1)
                    pool.wait_ge(S["kss_ready"], n + 1)
                    nc.gpsimd.tensor_tensor(knr, kss, nhalf[:, :], ALU.pow).then_inc(S["knr_ready"], 1)
                    for m, (_, w) in enumerate(FM):
                        i = n * NM + m
                        pool.wait_ge(S["hf_ready"], i + 1)
                        plain(pool)
                        nc.gpsimd.tensor_copy(HH[0:w, m], hf[0:w, m % 2]).then_inc(S["hh_ready"], 1)
                        pool.wait_ge(S["hh_ready"], i + 1)
                        nc.gpsimd.tensor_tensor(HL[0:w, m], hf[0:w, m % 2], HH[0:w, m], ALU.subtract) \
                            .then_inc(S["hs_ready"], 1)

        BANKS = [("wq", i) for i in range(4)] + [("g", i) for i in range(8)] \
            + [("gu", i) for i in range(4)] + [("wd", i) for i in range(NM // 2)]

        def bank_of(i):
            return 2 * (i % 4)

        @block.scalar
        def _(act):
            def load(dst, src, name):
                act.dma_start(dst, src).then_inc(ld[name], 16)

            load(mrow[:, :], mrow_in, "small")
            load(bw[:, :], bw_in, "small")
            load(bwself[:, :], bwself_in, "small")
            load(wq0[:, :, :], wq0_in.rearrange("(k p) n -> p k n", p=128), "l0")
            load(wo0[:, :, :], wo0_in.rearrange("(k p) n -> p k n", p=128), "l0")
            load(mem[:, :, :], mem_in, "l0")
            load(mnorm[:, :, :], mnorm_in, "l0")
            load(r_kva, wkva_in.rearrange("(k p) n -> p k n", p=128), "kva")
            load(kvw[:, :], kvw_in.partition_broadcast(128), "kva")
            load(ebias[:, :], ebias_in.partition_broadcast(128), "kva")
            load(ra[:, :, :], ra_in.rearrange("(k p) n -> p k n", p=128), "kva")
            load(r_gu.rearrange("p k g n -> p k (g n)"), wgu_in.rearrange("(k p) g n -> p k (g n)", p=128), "gu")
            load(r_lora[0:72, :], lora_in, "gu")
            load(r_wd[:, 0:NM - 1, :], wd_in[0:(NM - 1) * 128, :].rearrange("(m p) n -> p m n", p=128), "wd")
            load(r_wd[0:FM[-1][1], NM - 1, :], wd_in[(NM - 1) * 128:DFF, :], "wd")
            load(r_bgu, bgu_in, "tail")
            load(r_ad[:, 0:NM - 1, :], ad_in[0:(NM - 1) * 128, :].rearrange("(m p) n -> p m n", p=128), "tail")
            load(r_ad[0:FM[-1][1], NM - 1, :], ad_in[(NM - 1) * 128:DFF, :], "tail")
            load(r_bd[0:64, :], bd_in, "tail")

            act.wait_ge(prep_dve, 2)
            nc.scalar.activation(bsm[:, 4:8], bw[:, :], ACT.Exp, bias=bsm[:, 0:1]).then_inc(prep_act, 1)
            nc.scalar.activation(bsm[:, 8:9], bwself[:, :], ACT.Exp, bias=bsm[:, 0:1]).then_inc(prep_act, 1)
            act.wait_ge(ld["wq"], 48)
            for k in range(KD):
                nc.scalar.activation(WQH[:, k, :, 64:128], r_wqr[:, k], ACT.Copy, scale=SCALE) \
                    .then_inc(prep_act, 1)
            for i, (kind, j) in enumerate(BANKS):
                src = ps[:, bank_of(i)]
                if kind == "wq":
                    act.wait_ge(prep_mm, i + 2)
                    k, hh = j // 2, j % 2
                    nc.scalar.activation(WQH[:, k, 8 * hh:8 * hh + 8, 0:64],
                                         src.rearrange("p (h d) -> p h d", h=8), ACT.Copy, scale=SCALE) \
                        .then_inc(prep_hi, 1)
                elif kind == "g":
                    act.wait_ge(prep_mm, i + 2)
                    nc.scalar.copy(GH[:, 2 * j:2 * j + 2, :], src.rearrange("p (h d) -> p h d", h=2)) \
                        .then_inc(prep_hi, 1)
                elif kind == "gu":
                    act.wait_ge(prep_lo, 2 * i + 1)
                    k, g = j // 2, j % 2
                    nc.scalar.copy(GUH[:, k, g, :], r_gu[:, k, g, :]).then_inc(prep_hi, 1)
                else:
                    act.wait_ge(prep_lo, 2 * i + 1)
                    if j < NM // 2 - 1:
                        nc.scalar.copy(WDH[:, 2 * j:2 * j + 2, :], r_wd[:, 2 * j:2 * j + 2, :]).then_inc(prep_hi, 1)
                    else:
                        w = FM[-1][1]
                        nc.scalar.copy(WDH[:, 2 * j, :], r_wd[:, 2 * j, :])
                        nc.scalar.copy(WDH[0:w, 2 * j + 1, :], r_wd[0:w, 2 * j + 1, :]).then_inc(prep_hi, 1)

            def chunk(b, c):
                n = b * NC + c
                act.wait_ge(S["xT_ready"], 2 * n + 1)
                nc.scalar.copy(xnT, ps[:, 0:2, :]).then_inc(S["xnT_ready"], 1)
                act.wait_ge(S["q_ready"], n + 1)
                nc.scalar.activation(ex, ps[:, 6:8, :], ACT.Exp).then_inc(S["e_ready"], 1)
                for q in range(5):
                    i = n * 4 + q
                    if q < 4:
                        act.wait_ge(S["gu_ready"], i + 1)
                        nc.scalar.copy(gcp[:, q], ps[:, 2:4, :]).then_inc(S["gate_copied"], 1)
                        nc.scalar.copy(ucp[:, q], ps[:, 4:6, :]).then_inc(S["up_copied"], 1)
                        act.wait_ge(S["gate_copied"], i + 1)
                        if q >= 2:
                            act.wait_ge(S["tanh_ready"], i - 1)
                        nc.scalar.activation(inner[:, q % 2], gcp[:, q], ACT.Square).then_inc(S["sq_ready"], 1)
                    if q >= 1:
                        act.wait_ge(S["inner_ready"], i)
                        if q >= 3:
                            act.wait_ge(S["act8_ready"], i - 2)
                        nc.scalar.activation(tanhg[:, (q - 1) % 2], inner[:, (q - 1) % 2], ACT.Tanh) \
                            .then_inc(S["tanh_ready"], 1)
                act.wait_ge(S["comb_done"], 8 * n + 8)
                nc.scalar.copy(combT, ps[:, 6:8, :]).then_inc(S["combT_ready"], 1)
                act.wait_ge(S["y0_ready"], n + 1)
                nc.scalar.copy(fb, token_major_all(2)).then_inc(S["fb_ready"], 1)
                act.wait_ge(S["xT_ready"], 2 * n + 2)
                nc.scalar.copy(xnT, ps[:, 0:2, :]).then_inc(S["xnT_ready"], 1)
                act.wait_ge(S["ra_ready"], n + 1)
                nc.scalar.activation(th, token_major_all(6)[:, :, 0:E], ACT.Tanh, scale=0.5) \
                    .then_inc(S["th_ready"], 1)
                act.wait_ge(S["kvc_ready"], n + 1)
                nc.scalar.copy(kvs, ps[:, 0, :].rearrange("p (t c) -> p t c", t=TPC)).then_inc(S["kvs_ready"], 1)
                act.wait_ge(S["xawT_ready"], n + 1)
                nc.scalar.copy(ZH, ps[:, 1, :]).then_inc(S["zh_ready"], 1)
                act.wait_ge(S["kT_ready"], n + 1)
                nc.scalar.copy(KTH[:, row(c)], ps[:, 6, :]).then_inc(S["kth_ready"], 1)
                for m, (_, w) in enumerate(FM):
                    i = n * NM + m
                    act.wait_ge(S["m_ready"], i + 1)
                    if m >= 2:
                        act.wait_ge(S["hf_ready"], i - 1)
                    nc.scalar.activation(tt[0:w, m % 2], ps[0:w, 2 + 2 * (m % 2), :], ACT.Tanh, scale=0.5) \
                        .then_inc(S["tt_ready"], 1)
                act.wait_ge(S["z2T_ready"], n + 1)
                nc.scalar.copy(Z2H[0:64, :], ps[0:64, 0, :]).then_inc(S["z2h_ready"], 1)

                def nope(i):
                    u = n * 16 + i
                    act.wait_ge(S["qp_ready"], u + 1)
                    if i >= 2:
                        act.wait_ge(S["qt_ready"], u - 1)
                    nc.scalar.copy(qtok[:, i % 2, :, 0:64],
                                   ps[:, i % 2, :].rearrange("p (h c) -> p h c", h=4)[:, :, 0:64]) \
                        .then_inc(S["qn_ready"], 1)

                def q_high(i):
                    u, t, q = n * 16 + i, i // 4, i % 4
                    act.wait_ge(S["qt_ready"], u + 1)
                    nc.scalar.copy(QTH[:, 4 * q:4 * q + 4, t * 128:t * 128 + 128],
                                   ps[:, 2 + i % 2, :].rearrange("p (h c) -> p h c", h=4)) \
                        .then_inc(S["qth_ready"], 1)

                for i in range(17):
                    if i < 16:
                        nope(i)
                    if i >= 1:
                        q_high(i - 1)

                NJ = TPC * (c + 1)

                def jn(h, j):
                    return b * (16 * 12) + c * 64 + h * NJ + j

                def p_high(h, par, j, first=False):
                    w0 = max(0, j - TPC * c) * 128
                    i = jn(h, j)
                    act.wait_ge(S["pt_ready"], i + 1)
                    if not (first and j < 2):
                        act.wait_ge(S["pv_done"], i - 1)
                    nc.scalar.copy(PH[:, j % 2, w0:CH], ps[:, 4 + j % 2, w0:CH]).then_inc(S["pth_ready"], 1)

                def exps(h, par, t):
                    w = (TPC * c + t + 1) * 128
                    i = ((b * NC + c) * 16 + h) * 4 + t
                    act.wait_ge(S["max_ready"], i + 1)
                    nc.scalar.activation(P[:, par, t, 0:w], ps[:, 2 * (t % 2):2 * (t % 2) + 2, :]
                                         .rearrange("p b n -> p (b n)")[:, 0:w], ACT.Exp,
                                         bias=nm[:, 4 * par + t:4 * par + t + 1],
                                         accum_out=rs[:, 4 * par + t:4 * par + t + 1]).then_inc(S["exp_done"], 1)

                def context_high(h, par):
                    act.wait_ge(S["pv_done"], jn(h, NJ - 1) + 1)
                    nc.scalar.copy(QTH[:, h, :] if isinstance(h, int) else
                                   QTH[:, bass.ds(h, 1), :].rearrange("p a n -> p (a n)"),
                                   ps[:, 6 + par, :]).then_inc(S["cth_ready"], 1)

                def step(h, par, first=False):
                    for t in range(TPC):
                        for j in range((c + 1) * t, (c + 1) * (t + 1)):
                            p_high(h - 1, 1 - par, j, first)
                        if t == 0 and not first:
                            act.wait_ge(S["pv_done"], jn(h - 1, 0))
                        exps(h, par, t)
                    context_high(h - 1, 1 - par)

                for t in range(TPC):
                    exps(0, 0, t)
                step(1, 1, first=True)
                with act.Fori(1, H // 2) as hp:
                    step(hp * 2, 0)
                    step(hp * 2 + 1, 1)
                for j in range(NJ):
                    p_high(H - 1, 1, j)
                context_high(H - 1, 1)

            with act.Fori(0, B) as b:
                for c in range(NC):
                    chunk(b, c)

        @block.vector
        def _(dve):
            v = nc.vector
            count = [0]

            def own(ins):
                count[0] += 1
                ins.then_inc(prep_dve, 1)
                dve.wait_ge(prep_dve, count[0])

            dve.wait_ge(ld["small"], 48)
            own(v.tensor_reduce(bsm[:, 0:1], bw[:, :], AX.X, ALU.max, negate=True))
            own(v.tensor_reduce(bsm[:, 1:2], mrow[:, :], AX.X, ALU.add))
            dve.wait_ge(prep_act, 2)
            own(v.tensor_reduce(bsm[:, 2:3], bsm[:, 4:8], AX.X, ALU.add))
            own(v.reciprocal(bsm[:, 3:4], bsm[:, 2:3]))
            own(v.tensor_tensor(bsm[:, 9:10], bsm[:, 8:9], bsm[:, 3:4], ALU.mult))
            dve.wait_ge(prep_mm, 1)
            own(v.tensor_scalar(bankw[:, :], ps[0:64, 7, 0:1], MEM_EPS, bsm[:, 9:10], ALU.is_ge, ALU.mult))
            dve.wait_ge(ld["const"], 16)
            v.tensor_copy(identb[:, :], ident)
            v.tensor_copy(maskb[:, :], const[:, C_MASK:C_MASK + 128])
            dve.wait_ge(ld["wg"], 16)
            v.tensor_copy(wg8[:, :, :, :], r_wg, saturate=True)
            dve.wait_ge(ld["wl"], 16)
            v.tensor_copy(wl8[:, :, :], r_wl, saturate=True)
            dve.wait_ge(prep_act, 4)
            for k in range(KD):
                v.scalar_tensor_tensor(WQL[:, k, :, 64:128], r_wqr[:, k], SCALE, WQH[:, k, :, 64:128],
                                       ALU.mult, ALU.subtract)
            dve.wait_ge(ld["kva"], 64)
            dve.wait_ge(ld["tail"], 64)
            w = FM[-1][1]
            v.tensor_copy(KVH[:, :, :], r_kva)
            v.tensor_copy(BGH[:, :], r_bgu)
            v.tensor_copy(ADH[:, 0:NM - 1, :], r_ad[:, 0:NM - 1, :])
            v.tensor_copy(ADH[0:w, NM - 1, :], r_ad[0:w, NM - 1, :])
            own(v.tensor_copy(BDH[:, :], r_bd[0:64, :]))
            v.tensor_tensor(KVL[:, :, :], r_kva, KVH[:, :, :], ALU.subtract)
            v.tensor_tensor(BGL[:, :], r_bgu, BGH[:, :], ALU.subtract)
            v.tensor_tensor(ADL[:, 0:NM - 1, :], r_ad[:, 0:NM - 1, :], ADH[:, 0:NM - 1, :], ALU.subtract)
            v.tensor_tensor(ADL[0:w, NM - 1, :], r_ad[0:w, NM - 1, :], ADH[0:w, NM - 1, :], ALU.subtract)
            own(v.tensor_tensor(BDL[:, :], r_bd[0:64, :], BDH[:, :], ALU.subtract))
            for i, (kind, j) in enumerate(BANKS):
                src = ps[:, bank_of(i)]
                if kind == "wq":
                    k, hh = j // 2, j % 2
                    dve.wait_ge(prep_hi, i + 1)
                    v.scalar_tensor_tensor(WQL[:, k, 8 * hh:8 * hh + 8, 0:64],
                                           src.rearrange("p (h d) -> p h d", h=8), SCALE,
                                           WQH[:, k, 8 * hh:8 * hh + 8, 0:64], ALU.mult, ALU.subtract) \
                        .then_inc(prep_lo, 2)
                elif kind == "g":
                    dve.wait_ge(prep_hi, i + 1)
                    v.tensor_tensor(GL[:, 2 * j:2 * j + 2, :], src.rearrange("p (h d) -> p h d", h=2),
                                    GH[:, 2 * j:2 * j + 2, :], ALU.subtract).then_inc(prep_lo, 2)
                elif kind == "gu":
                    k, g = j // 2, j % 2
                    dve.wait_ge(prep_mm, i + 2)
                    two = ps[:, bank_of(i):bank_of(i) + 2, :].rearrange("p b n -> p (b n)")[:, 0:DFF]
                    v.scalar_tensor_tensor(r_gu[:, k, g, :], two, 1.0 / RANK, r_gu[:, k, g, :],
                                           ALU.mult, ALU.add).then_inc(prep_lo, 1)
                    dve.wait_ge(prep_hi, i + 1)
                    v.tensor_tensor(GUL[:, k, g, :], r_gu[:, k, g, :], GUH[:, k, g, :], ALU.subtract) \
                        .then_inc(prep_lo, 1)
                else:
                    dve.wait_ge(prep_mm, i + 2)
                    rows = [128, 128 if j < NM // 2 - 1 else FM[-1][1]]
                    for a in range(2):
                        m = 2 * j + a
                        ins = v.scalar_tensor_tensor(r_wd[0:rows[a], m, :], src[0:rows[a], a * D:a * D + D],
                                                     1.0 / RANK, r_wd[0:rows[a], m, :], ALU.mult, ALU.add)
                    ins.then_inc(prep_lo, 1)
                    dve.wait_ge(prep_hi, i + 1)
                    for a in range(2):
                        m = 2 * j + a
                        ins = v.tensor_tensor(WDL[0:rows[a], m, :], r_wd[0:rows[a], m, :],
                                              WDH[0:rows[a], m, :], ALU.subtract)
                    ins.then_inc(prep_lo, 1)
            v.memset(stats[:, :, :], 0.0).then_inc(prep_done, 1)
            dve.wait_ge(prep_done, 1)

            def chunk(b, c):
                n = b * NC + c
                k_link = [0]

                def linked(ins):
                    k_link[0] += 1
                    ins.then_inc(link, 1)
                    dve.wait_ge(link, n * DVE_LINKS + k_link[0])

                def layernorm(l):
                    i = 2 * n + l
                    for t in range(TPC):
                        ins = v.bn_stats(stats[:, t, :], xg[:, c, t, :])
                    linked(ins)
                    plain(dve)
                    for t in range(TPC):
                        ins = v.bn_aggr(mv[:, t, :], stats[:, t, :])
                    linked(ins)
                    v.tensor_scalar(ve[:, :], mv[:, :, 1], LN_EPS, None, ALU.add).then_inc(S["var_ready"], 1)
                    dve.wait_ge(S["rstd_ready"], i + 1)
                    for t in range(TPC):
                        ins = v.tensor_scalar(xn[:, t, :], xg[:, c, t, :], mv[:, t, 0:1], rstd[:, t:t + 1],
                                              ALU.subtract, ALU.mult)
                    ins.then_inc(S["xn_ready"], 1)
                    dve.wait_ge(S["xnT_ready"], i + 1)

                dve.wait_ge(x_loaded[c], b * 16 + 16)
                layernorm(0)
                plain(dve)
                v.tensor_copy(xq8, ps[:, 0:2, :], saturate=True).then_inc(S["xq8_ready"], 1)
                dve.wait_ge(S["e_ready"], n + 1)
                linked(v.tensor_scalar(ex, ex, 1.0, None, ALU.min))
                for g in range(KD):
                    ins = v.scalar_tensor_tensor(sig[:, g], ps[:, 6 + g, :], 1.0, ex[:, g], ALU.add, ALU.max)
                ins.then_inc(S["sig_ready"], 1)

                def gelu_inner(q):
                    dve.wait_ge(S["sq_ready"], n * 4 + q + 1)
                    t = inner[:, q % 2]
                    linked(v.tensor_tensor(t, t, gcp[:, q], ALU.mult))
                    linked(v.tensor_scalar(t, t, GELU_C, None, ALU.mult))
                    linked(v.tensor_tensor(t, t, gcp[:, q], ALU.add))
                    v.tensor_scalar(t, t, GELU_S, None, ALU.mult).then_inc(S["inner_ready"], 1)

                def gelu_outer(q):
                    dve.wait_ge(S["tanh_ready"], n * 4 + q + 1)
                    t = tanhg[:, q % 2]
                    linked(v.tensor_scalar(t, t, 1.0, 0.5, ALU.add, ALU.mult))
                    linked(v.tensor_tensor(t, t, gcp[:, q], ALU.mult))
                    linked(v.tensor_tensor(t, t, ucp[:, q], ALU.mult))
                    plain(dve)
                    v.tensor_copy(act8[:, 2 * q:2 * q + 2], t, saturate=True).then_inc(S["act8_ready"], 1)

                gelu_inner(0)
                gelu_inner(1)
                gelu_outer(0)
                dve.wait_ge(S["norm_ready"], n + 1)
                linked(v.tensor_scalar(rnorm[0:64, :], ps[0:64, 0, :], MEM_EPS, None, ALU.max))
                linked(v.reciprocal(rnorm[0:64, :], rnorm[0:64, :]))
                v.tensor_scalar(rnorm[0:64, :], rnorm[0:64, :], bankw[:, 0:1], None, ALU.mult) \
                    .then_inc(S["r_ready"], 1)
                for q in range(2, 4):
                    gelu_inner(q)
                    gelu_outer(q - 1)
                gelu_outer(3)
                for j in range(8):
                    i = n * 8 + j
                    dve.wait_ge(S["rbc_ready"], i + 1)
                    if j >= 2:
                        dve.wait_ge(S["comb_done"], i - 1)
                    v.tensor_tensor(sn[:, j % 2], sig[:, j // 4], ps[:, j % 2, :], ALU.mult) \
                        .then_inc(S["sn_ready"], 1)
                dve.wait_ge(S["y1_ready"], n + 1)
                linked(v.tensor_tensor(xg[:, c], xg[:, c], token_major_all(4), ALU.add))
                dve.wait_ge(S["fb_ready"], n + 1)
                linked(v.tensor_tensor(xg[:, c], xg[:, c], fb, ALU.add))

                layernorm(1)
                linked(v.tensor_copy(XH[:, :, :], ps[:, 0:2, :]))
                v.tensor_tensor(XL[:, :, :], ps[:, 0:2, :], XH[:, :, :], ALU.subtract) \
                    .then_inc(S["xsplit_ready"], 1)
                dve.wait_ge(S["th_ready"], n + 1)
                linked(v.tensor_scalar(th, th, 1.0, 0.5, ALU.add, ALU.mult))
                linked(v.tensor_tensor(bi, th, ebias[:, :].unsqueeze(1).broadcast_to([128, TPC, E]), ALU.add))
                mine = bi.unsqueeze(3).broadcast_to([128, TPC, E, E])
                other = bi.unsqueeze(2).broadcast_to([128, TPC, E, E])
                v.tensor_tensor(cmp1, other, mine, ALU.is_gt)
                linked(v.tensor_tensor(cmp2, other, mine, ALU.is_equal))
                linked(v.tensor_tensor(cmp2, cmp2, tri.unsqueeze(1).broadcast_to([128, TPC, E, E]), ALU.mult))
                linked(v.tensor_tensor(cmp1, cmp1, cmp2, ALU.add))
                linked(v.tensor_reduce(rank, cmp1, AX.X, ALU.add))
                linked(v.scalar_tensor_tensor(wex, rank, 2.0, th, ALU.is_lt, ALU.mult))
                linked(v.tensor_reduce(den, wex, AX.X, ALU.add))
                linked(v.tensor_scalar(den, den, 1e-8, None, ALU.add))
                linked(v.reciprocal(den, den))
                linked(v.scalar_tensor_tensor(wex, wex, 1.0 / RANK,
                                              den.unsqueeze(2).broadcast_to([128, TPC, E]), ALU.mult, ALU.mult))
                by_rank = wex.unsqueeze(3).broadcast_to([128, TPC, E, RANK])
                for g in range(2):
                    a = token_major_all(6)[:, :, E + 64 * g:E + 64 * g + 64]
                    ins = v.tensor_tensor(xaw[:, :, 64 * g:64 * g + 64].rearrange("p t (e r) -> p t e r", e=E),
                                          a.rearrange("p t (e r) -> p t e r", e=E), by_rank, ALU.mult)
                ins.then_inc(S["xaw_ready"], 1)
                dve.wait_ge(S["kvs_ready"], n + 1)
                linked(v.tensor_tensor(ksq, kvs[:, :, 0:64], kvs[:, :, 0:64], ALU.mult))
                linked(v.tensor_reduce(kss, ksq, AX.X, ALU.add))
                v.tensor_scalar(kss, kss, 1.0 / KVR, RMS_EPS, ALU.mult, ALU.add).then_inc(S["kss_ready"], 1)
                cs, sn_t = cos[:, TPC * c:TPC * c + TPC, :], sin[:, TPC * c:TPC * c + TPC, :]
                v.tensor_tensor(kr1, kvs[:, :, 64:128], cs, ALU.mult)
                v.tensor_tensor(kr2[:, :, 0:32], kvs[:, :, 96:128], sn_t[:, :, 0:32], ALU.mult)
                linked(v.tensor_tensor(kr2[:, :, 32:64], kvs[:, :, 64:96], sn_t[:, :, 32:64], ALU.mult))
                v.tensor_tensor(ktok[:, :, 64:128], kr1, kr2, ALU.add)
                dve.wait_ge(S["zh_ready"], n + 1)
                v.tensor_tensor(ZL, ps[:, 1, :], ZH, ALU.subtract).then_inc(S["zl_ready"], 1)
                dve.wait_ge(S["knr_ready"], n + 1)
                linked(v.tensor_tensor(ktok[:, :, 0:64], kvs[:, :, 0:64],
                                       knr.unsqueeze(2).broadcast_to([128, TPC, 64]), ALU.mult))
                v.tensor_tensor(ktok[:, :, 0:64], ktok[:, :, 0:64],
                                kvw[:, :].unsqueeze(1).broadcast_to([128, TPC, 64]), ALU.mult) \
                    .then_inc(S["ktok_ready"], 1)
                dve.wait_ge(S["ktok_ready"], n + 1)
                lat = LAT[:, TPC * c:TPC * c + TPC, :]
                linked(v.tensor_copy(lat[:, :, 0:64], ktok[:, :, 0:64]))
                linked(v.tensor_tensor(lat[:, :, 64:128], ktok[:, :, 0:64], lat[:, :, 0:64], ALU.subtract))
                dve.wait_ge(S["kth_ready"], n + 1)
                v.tensor_tensor(KTL[:, row(c)], ps[:, 6, :], KTH[:, row(c)], ALU.subtract) \
                    .then_inc(S["ktl_ready"], 1)
                for m, (_, w) in enumerate(FM):
                    i, p = n * NM + m, m % 2
                    dve.wait_ge(S["tt_ready"], i + 1)
                    linked(v.scalar_tensor_tensor(a1[0:w, p], tt[0:w, p], 1.0, ps[0:w, 2 + 2 * p, :],
                                                  ALU.add, ALU.mult))
                    if m >= 2:
                        dve.wait_ge(S["hs_ready"], i - 1)
                    v.scalar_tensor_tensor(hf[0:w, p], a1[0:w, p], 0.5, ps[0:w, 3 + 2 * p, :],
                                           ALU.mult, ALU.mult).then_inc(S["hf_ready"], 1)
                dve.wait_ge(S["z_ready"], n + 1)
                v.tensor_tensor(zw.rearrange("p t (e r) -> p t e r", e=E),
                                ps[:, 1, 0:TPC * 64].rearrange("p (t e r) -> p t e r", t=TPC, e=E),
                                by_rank, ALU.mult).then_inc(S["zw_ready"], 1)
                dve.wait_ge(S["z2h_ready"], n + 1)
                v.tensor_tensor(Z2L[0:64, :], ps[0:64, 0, :], Z2H[0:64, :], ALU.subtract) \
                    .then_inc(S["z2l_ready"], 1)
                dve.wait_ge(S["y2_ready"], n + 1)
                linked(v.tensor_tensor(xg[:, c], xg[:, c], token_major_all(6), ALU.add))

                def rope(i):
                    u, t, p = n * 16 + i, i // 4, i % 2
                    src = ps[:, p, :].rearrange("p (h c) -> p h c", h=4)
                    cs = cos[:, TPC * c + t, :].unsqueeze(1).broadcast_to([128, 4, 64])
                    sa = sin[:, TPC * c + t, 0:32].unsqueeze(1).broadcast_to([128, 4, 32])
                    sb_ = sin[:, TPC * c + t, 32:64].unsqueeze(1).broadcast_to([128, 4, 32])
                    dve.wait_ge(S["qn_ready"], u + 1)
                    v.tensor_tensor(qr1[:, p], src[:, :, 64:128], cs, ALU.mult)
                    v.tensor_tensor(qr2[:, p, :, 0:32], src[:, :, 96:128], sa, ALU.mult)
                    v.tensor_tensor(qr2[:, p, :, 32:64], src[:, :, 64:96], sb_, ALU.mult) \
                        .then_inc(S["qrope_parts"], 1)
                    if i >= 2:
                        dve.wait_ge(S["qt_ready"], u - 1)
                    dve.wait_ge(S["qrope_parts"], u + 1)
                    v.tensor_tensor(qtok[:, p, :, 64:128], qr1[:, p], qr2[:, p], ALU.add) \
                        .then_inc(S["qr_ready"], 1)

                def q_low(i):
                    u, t, q = n * 16 + i, i // 4, i % 4
                    dve.wait_ge(S["qth_ready"], u + 1)
                    v.tensor_tensor(QTL[:, 4 * q:4 * q + 4, t * 128:t * 128 + 128],
                                    ps[:, 2 + i % 2, :].rearrange("p (h c) -> p h c", h=4),
                                    QTH[:, 4 * q:4 * q + 4, t * 128:t * 128 + 128], ALU.subtract) \
                        .then_inc(S["qtl_ready"], 1)

                for i in range(17):
                    if i < 16:
                        rope(i)
                    if i >= 1:
                        q_low(i - 1)

                NJ = TPC * (c + 1)

                def jn(h, j):
                    return b * (16 * 12) + c * 64 + h * NJ + j

                def row_max(h, par, t):
                    w = (TPC * c + t + 1) * 128
                    i = ((b * NC + c) * 16 + h) * 4 + t
                    dve.wait_ge(S["s_ready"], i + 1)
                    v.tensor_reduce(nm[:, 4 * par + t:4 * par + t + 1],
                                    ps[:, 2 * (t % 2):2 * (t % 2) + 2, :].rearrange("p b n -> p (b n)")[:, 0:w],
                                    AX.X, ALU.max, negate=True).then_inc(S["max_ready"], 1)

                def normalise(h, par, t):
                    w = (TPC * c + t + 1) * 128
                    i = ((b * NC + c) * 16 + h) * 4 + t
                    s = slice(4 * par + t, 4 * par + t + 1)
                    dve.wait_ge(S["exp_done"], i + 1)
                    v.reciprocal(rl[:, s], rs[:, s]).then_inc(S["rl_ready"], 1)
                    dve.wait_ge(S["rl_ready"], i + 1)
                    v.tensor_scalar(P[:, par, t, 0:w], P[:, par, t, 0:w], rl[:, s], None, ALU.mult) \
                        .then_inc(S["pn_ready"], 1)

                def p_low(h, j):
                    w0 = max(0, j - TPC * c) * 128
                    dve.wait_ge(S["pth_ready"], jn(h, j) + 1)
                    v.tensor_tensor(PL[:, j % 2, w0:CH], ps[:, 4 + j % 2, w0:CH], PH[:, j % 2, w0:CH],
                                    ALU.subtract).then_inc(S["ptl_ready"], 1)

                def context_low(h, par):
                    i = n * 16 + h
                    dve.wait_ge(S["cth_ready"], i + 1)
                    at = (lambda q: q[:, h, :]) if isinstance(h, int) else \
                        (lambda q: q[:, bass.ds(h, 1), :].rearrange("p a n -> p (a n)"))
                    v.tensor_tensor(at(QTL), ps[:, 6 + par, :], at(QTH), ALU.subtract) \
                        .then_inc(S["ctl_ready"], 1)

                def step(h, par):
                    for t in range(TPC):
                        row_max(h, par, t)
                        if t == 0:
                            normalise(h - 1, 1 - par, TPC - 1)
                        else:
                            normalise(h, par, t - 1)
                        for j in range((c + 1) * t, (c + 1) * (t + 1)):
                            p_low(h - 1, j)
                    context_low(h - 1, 1 - par)

                for t in range(TPC):
                    row_max(0, 0, t)
                    if t:
                        normalise(0, 0, t - 1)
                step(1, 1)
                with dve.Fori(1, H // 2) as hp:
                    step(hp * 2, 0)
                    step(hp * 2 + 1, 1)
                normalise(H - 1, 1, TPC - 1)
                for j in range(NJ):
                    p_low(H - 1, j)
                context_low(H - 1, 1)
                dve.wait_ge(S["o_ready"], n + 1)
                v.tensor_tensor(xg[:, c], xg[:, c], token_major_all(4), ALU.add).then_inc(S["out_ready"], 1)
                assert k_link[0] == DVE_LINKS, k_link[0]

            with dve.Fori(0, B) as b:
                for c in range(NC):
                    chunk(b, c)

        @block.tensor
        def _(pe):
            mm = nc.tensor.matmul

            pe.wait_ge(ld["const"], 16)
            pe.wait_ge(prep_dve, 2)
            mm(ps[0:64, 7, 0:1], blk[0:64, :], bsm[:, 1:2], start=True, stop=True).then_inc(prep_mm, 1)
            waited = {"wq": ("wq", 48), "g": ("wv", 32), "gu": ("gu", 32), "wd": ("wd", 32)}
            for i, (kind, j) in enumerate(BANKS):
                name, value = waited[kind]
                pe.wait_ge(ld[name], value)
                if i == 3:
                    pe.wait_ge(prep_dve, 6)
                if i >= 4:
                    pe.wait_ge(prep_lo, 2 * (i - 4) + 2)
                dst = ps[:, bank_of(i), :]
                if kind == "wq":
                    k, hh = j // 2, j % 2
                    for a in range(8):
                        h = 8 * hh + a
                        last = mm(dst[:, 64 * a:64 * a + 64], r_wqT[:, h, 128 * k:128 * k + 128], r_wkT[:, h, :],
                                  start=True, stop=True)
                elif kind == "g":
                    for a in range(2):
                        h = 2 * j + a
                        for r in range(2):
                            last = mm(ps[64 * r:64 * r + 64, bank_of(i), a * D:a * D + D], r_wvT[:, h, :],
                                      r_wo[:, h, :], start=True, stop=True)
                elif kind == "gu":
                    k, g = j // 2, j % 2
                    sa = r_lora[32 * g:32 * g + RANK, 128 * k:128 * k + 128]
                    for n0, n1 in ((0, 512), (512, DFF)):
                        last = mm(ps[:, bank_of(i) + n0 // 512, 0:n1 - n0], sa,
                                  r_lora[32 * g:32 * g + RANK, D + n0:D + n1], start=True, stop=True)
                else:
                    for a in range(2):
                        m0, w = FM[2 * j + a]
                        last = mm(dst[0:w, a * D:a * D + D], r_lora[64:64 + RANK, m0:m0 + w],
                                  r_lora[64:64 + RANK, DFF:DFF + D], start=True, stop=True)
                last.then_inc(prep_mm, 1)
            pe.wait_ge(prep_done, 1)
            pe.wait_ge(ld["l0"], 64)
            pe.wait_ge(ld["kva"], 64)

            def split3(ps_out, pairs, start=True, stop=True):
                for i, ((lh, ll), (rh, rl_)) in enumerate(pairs):
                    mm(ps_out, lh, rh, start=start and i == 0, stop=False)
                    mm(ps_out, lh, rl_, start=False, stop=False)
                    last = mm(ps_out, ll, rh, start=False, stop=stop and i == len(pairs) - 1)
                return last

            def chunk(b, c):
                n = b * NC + c

                def transposes(l):
                    pe.wait_ge(S["xn_ready"], 2 * n + l + 1)
                    for k in range(KD):
                        for t in range(TPC):
                            last = nc.tensor.transpose(ps[:, k, t * 128:t * 128 + 128],
                                                       xn[:, t, k * 128:k * 128 + 128], ident)
                    last.then_inc(S["xT_ready"], 1)

                transposes(0)
                pe.wait_ge(S["xnT_ready"], 2 * n + 1)
                for g in range(KD):
                    for k in range(KD):
                        last = mm(ps[:, 6 + g, :], wq0[:, k, g * 128:g * 128 + 128], xnT[:, k, :],
                                  start=k == 0, stop=k == KD - 1)
                last.then_inc(S["q_ready"], 1)

                def ffn0(q):
                    i = n * 4 + q
                    if q >= 1:
                        pe.wait_ge(S["up_copied"], i)
                    plain(pe)
                    for g in range(2):
                        for a in range(2):
                            h = 2 * q + a
                            for k in range(KD):
                                last = mm(ps[:, 2 + 2 * g + a, :], wg8[:, k, g, h * 128:h * 128 + 128],
                                          xq8[:, k, :], start=k == 0, stop=k == KD - 1)
                    last.then_inc(S["gu_ready"], 1)

                pe.wait_ge(S["xq8_ready"], n + 1)
                for q in range(2):
                    ffn0(q)
                pe.wait_ge(S["sig_ready"], n + 1)
                for k in range(KD):
                    last = mm(ps[0:64, 0, :], mnorm[:, k, :], sig[:, k], start=k == 0, stop=k == KD - 1)
                last.then_inc(S["norm_ready"], 1)
                for q in range(2, 4):
                    ffn0(q)
                pe.wait_ge(S["r_ready"], n + 1)

                def combine(j):
                    g, bank = j // 4, j % 4
                    pe.wait_ge(S["sn_ready"], n * 8 + j + 1)
                    mm(ps[:, 6 + g, :], mem[:, j, :], sn[:, j % 2], start=bank == 0, stop=bank == 3) \
                        .then_inc(S["comb_done"], 1)

                for j in range(9):
                    if j < 8:
                        if j >= 2:
                            pe.wait_ge(S["sn_ready"], n * 8 + j - 1)
                        mm(ps[:, j % 2, :], sel[0:64, j, :], rnorm[0:64, :], start=True, stop=True) \
                            .then_inc(S["rbc_ready"], 1)
                    if j >= 1:
                        combine(j - 1)
                pe.wait_ge(S["act8_ready"], n * 4 + 4)
                plain(pe)
                for t in range(TPC):
                    for k in range(8):
                        last = mm(token_major(2, t), act8[:, k, t * 128:t * 128 + 128], wl8[:, k, :],
                                  start=k == 0, stop=k == 7)
                last.then_inc(S["y0_ready"], 1)
                pe.wait_ge(S["combT_ready"], n + 1)
                for t in range(TPC):
                    for k in range(KD):
                        last = mm(token_major(4, t), combT[:, k, t * 128:t * 128 + 128], wo0[:, k, :],
                                  start=k == 0, stop=k == KD - 1)
                last.then_inc(S["y1_ready"], 1)

                transposes(1)
                pe.wait_ge(S["xnT_ready"], 2 * n + 2)
                for t in range(TPC):
                    for k in range(KD):
                        last = mm(token_major(6, t)[:, 0:136], xnT[:, k, t * 128:t * 128 + 128], ra[:, k, :],
                                  start=k == 0, stop=k == KD - 1)
                last.then_inc(S["ra_ready"], 1)
                pe.wait_ge(S["xsplit_ready"], n + 1)
                for t in range(TPC):
                    tok = slice(t * 128, t * 128 + 128)
                    last = split3(ps[:, 0, tok], [((XH[:, k, tok], XL[:, k, tok]), (KVH[:, k, :], KVL[:, k, :]))
                                                  for k in range(KD)])
                last.then_inc(S["kvc_ready"], 1)

                def gate_up(m):
                    m0, w = FM[m]
                    if m >= 2:
                        pe.wait_ge(S["hf_ready"], n * NM + m - 1)
                    for g in range(2):
                        split3(ps[0:w, 2 + 2 * (m % 2) + g, :],
                               [((GUH[:, k, g, m0:m0 + w], GUL[:, k, g, m0:m0 + w]), (XH[:, k, :], XL[:, k, :]))
                                for k in range(KD)], stop=False)

                def gate_up_experts(m):
                    m0, w = FM[m]
                    for g in range(2):
                        r = slice(64 * g, 64 * g + 64)
                        last = split3(ps[0:w, 2 + 2 * (m % 2) + g, :],
                                      [((BGH[r, m0:m0 + w], BGL[r, m0:m0 + w]), (ZH[r, :], ZL[r, :]))], start=False)
                    last.then_inc(S["m_ready"], 1)

                gate_up(0)
                gate_up(1)
                pe.wait_ge(S["xaw_ready"], n + 1)
                for t in range(TPC):
                    last = nc.tensor.transpose(ps[:, 1, t * 128:t * 128 + 128], xaw[:, t, :], ident)
                last.then_inc(S["xawT_ready"], 1)
                pe.wait_ge(S["zl_ready"], n + 1)
                gate_up_experts(0)
                gate_up_experts(1)
                pe.wait_ge(S["ktok_ready"], n + 1)
                for t in range(TPC):
                    last = nc.tensor.transpose(ps[:, 6, t * 128:t * 128 + 128], ktok[:, t, :], ident)
                last.then_inc(S["kT_ready"], 1)
                for m in range(2, NM):
                    gate_up(m)
                    gate_up_experts(m)
                pe.wait_ge(S["hs_ready"], n * NM + NM)
                for t in range(TPC):
                    tok = slice(t * 128, t * 128 + 128)
                    last = split3(ps[:, 1, t * 64:t * 64 + 64],
                                  [((HH[0:w, m, tok], HL[0:w, m, tok]), (ADH[0:w, m, :], ADL[0:w, m, :]))
                                   for m, (_, w) in enumerate(FM)])
                last.then_inc(S["z_ready"], 1)
                pe.wait_ge(S["zw_ready"], n + 1)
                plain(pe)
                for t in range(TPC):
                    last = nc.tensor.transpose(ps[0:64, 0, t * 128:t * 128 + 128], zw[:, t, :], ident)
                last.then_inc(S["z2T_ready"], 1)
                pe.wait_ge(S["ktl_ready"], n + 1)
                for t in range(TPC):
                    tok = slice(t * 128, t * 128 + 128)
                    split3(token_major(6, t),
                           [((HH[0:w, m, tok], HL[0:w, m, tok]), (WDH[0:w, m, :], WDL[0:w, m, :]))
                            for m, (_, w) in enumerate(FM)], stop=False)
                    if t == 0:
                        pe.wait_ge(S["z2l_ready"], n + 1)
                    last = split3(token_major(6, t),
                                  [((Z2H[0:64, tok], Z2L[0:64, tok]), (BDH[:, :], BDL[:, :]))], start=False)
                last.then_inc(S["y2_ready"], 1)

                def project(i):
                    u, t, q = n * 16 + i, i // 4, i % 4
                    tok = slice(t * 128, t * 128 + 128)
                    if i >= 2:
                        pe.wait_ge(S["qn_ready"], u - 1)
                        pe.wait_ge(S["qr_ready"], u - 1)
                    split3(ps[:, i % 2, :],
                           [((XH[:, k, tok], XL[:, k, tok]),
                             (WQH[:, k, 4 * q:4 * q + 4, :].rearrange("p h c -> p (h c)"),
                              WQL[:, k, 4 * q:4 * q + 4, :].rearrange("p h c -> p (h c)")))
                            for k in range(KD)]).then_inc(S["qp_ready"], 1)

                def turn(i):
                    u, p = n * 16 + i, i % 2
                    pe.wait_ge(S["qn_ready"], u + 1)
                    pe.wait_ge(S["qr_ready"], u + 1)
                    if i >= 2:
                        pe.wait_ge(S["qtl_ready"], u - 1)
                    for a in range(4):
                        last = nc.tensor.transpose(ps[:, 2 + p, a * 128:a * 128 + 128], qtok[:, p, a, :], ident)
                    last.then_inc(S["qt_ready"], 1)

                for i in range(17):
                    if i < 16:
                        project(i)
                    if i >= 1:
                        turn(i - 1)
                pe.wait_ge(S["qtl_ready"], n * 16 + 16)

                NJ = TPC * (c + 1)

                def jn(h, j):
                    return b * (16 * 12) + c * 64 + h * NJ + j

                def query(q, h, t):
                    if isinstance(h, int):
                        return q[:, h, t * 128:t * 128 + 128]
                    return q[:, bass.ds(h, 1), t * 128:t * 128 + 128].rearrange("p a n -> p (a n)")

                def scores(h, t):
                    i = ((b * NC + c) * 16 + h) * 4 + t
                    if not (isinstance(h, int) and h == 0 and t < 2):
                        pe.wait_ge(S["exp_done"], i - 1)
                    w = (TPC * c + t + 1) * 128
                    parts = [(0, min(w, 512))] + ([(512, w)] if w > 512 else [])
                    qh, ql = query(QTH, h, t), query(QTL, h, t)
                    for lhs, rhs, kind in ((qh, KTH, 0), (qh, KTL, 1), (ql, KTH, 2)):
                        for a, z in parts:
                            mm(ps[:, 2 * (t % 2) + a // 512, 0:z - a], lhs, rhs[:, a:z],
                               start=kind == 0, stop=kind == 2 and z < w)
                    d = (w - 128) % 512
                    mm(ps[:, 2 * (t % 2) + (w - 128) // 512, d:d + 128], identb[:, :], maskb[:, :],
                       start=False, stop=True).then_inc(S["s_ready"], 1)

                def turn_p(h, par, j):
                    t0 = max(0, j - TPC * c)
                    if j == 0:
                        pe.wait_ge(S["pn_ready"], (n * 16 + h) * 4 + TPC)
                    if not (isinstance(h, int) and h == 0 and j < 2):
                        pe.wait_ge(S["ptl_ready"], jn(h, j) - 1)
                    for t in range(t0, TPC):
                        last = nc.tensor.transpose(ps[:, 4 + j % 2, t * 128:t * 128 + 128],
                                                   P[:, par, t, j * 128:j * 128 + 128], ident)
                    last.then_inc(S["pt_ready"], 1)

                def values(h, par, j):
                    w0 = max(0, j - TPC * c) * 128
                    if j == 0 and not (isinstance(h, int) and h < 2):
                        pe.wait_ge(S["ctl_ready"], n * 16 + h - 1)
                    pe.wait_ge(S["ptl_ready"], jn(h, j) + 1)
                    mm(ps[:, 6 + par, w0:CH], LAT[:, j, :], PH[:, j % 2, w0:CH], start=j == 0, stop=False)
                    mm(ps[:, 6 + par, w0:CH], LAT[:, j, :], PL[:, j % 2, w0:CH], start=False, stop=j == NJ - 1) \
                        .then_inc(S["pv_done"], 1)

                def step(h, par):
                    for t in range(TPC):
                        scores(h, t)
                        for j in range((c + 1) * t, (c + 1) * (t + 1)):
                            turn_p(h - 1, 1 - par, j)
                            if j:
                                values(h - 1, 1 - par, j - 1)
                    values(h - 1, 1 - par, NJ - 1)

                for t in range(TPC):
                    scores(0, t)
                step(1, 1)
                with pe.Fori(1, H // 2) as hp:
                    step(hp * 2, 0)
                    step(hp * 2 + 1, 1)
                for j in range(NJ):
                    turn_p(H - 1, 1, j)
                    if j:
                        values(H - 1, 1, j - 1)
                values(H - 1, 1, NJ - 1)
                pe.wait_ge(S["ctl_ready"], n * 16 + H)
                for t in range(TPC):
                    tok = slice(t * 128, t * 128 + 128)
                    last = split3(token_major(4, t), [((QTH[:, h, tok], QTL[:, h, tok]), (GH[:, h, :], GL[:, h, :]))
                                                      for h in range(H)])
                last.then_inc(S["o_ready"], 1)

            with pe.Fori(0, B) as b:
                for c in range(NC):
                    chunk(b, c)


def _constants(np):
    k = np.zeros((128, C_END), np.float32)
    k[:, C_ID:C_ID + 128] = np.eye(128, dtype=np.float32)
    q, key = np.arange(128)[:, None], np.arange(128)[None, :]
    k[:, C_MASK:C_MASK + 128] = np.where(key > q, np.float32(MASKED), np.float32(0))
    sel = np.zeros((64, KD, NB, 128), np.float32)
    for g in range(KD):
        for n in range(NB):
            for h in range(8):
                sel[n * H0 + g * 8 + h, g, n, h * D0:(h + 1) * D0] = 1
    k[0:64, C_SEL:C_TRI] = sel.reshape(64, -1)
    e = np.arange(E)
    k[:, C_TRI:C_BLK] = (e[None, :] < e[:, None]).astype(np.float32).reshape(1, 64)
    r = np.arange(64) // H0
    k[0:64, C_BLK:C_COS] = (r[:, None] == r[None, :]).astype(np.float32)
    inv = (np.float32(1) / np.float32(10000.0) ** (np.arange(0, ROPE, 2, dtype=np.float32) / np.float32(ROPE)))
    f = np.outer(np.arange(T, dtype=np.float32), inv.astype(np.float32)).astype(np.float32)
    cos = np.cos(f.astype(np.float64)).astype(np.float32)
    sin = np.sin(f.astype(np.float64)).astype(np.float32)
    cos = np.concatenate([cos, cos], 1).reshape(T // 128, 128, ROPE).transpose(1, 0, 2)
    sin = np.concatenate([-sin, sin], 1).reshape(T // 128, 128, ROPE).transpose(1, 0, 2)
    k[:, C_COS:C_SIN] = cos.reshape(128, -1)
    k[:, C_SIN:C_END] = sin.reshape(128, -1)
    return k


def kernel(**inputs):
    import numpy as np
    import concourse.bacc as bacc
    from concourse.bass_utils import run_bass_kernel_spmd

    i = {n: np.asarray(a) for n, a in inputs.items()}
    mems, norms = i["L0_attn_memories"], i["L0_attn_memory_norms"]
    mem = np.zeros((128, KD, NB, 128), np.float32)
    mnorm = np.zeros((128, KD, NB, H0), np.float32)
    for g in range(KD):
        for n in range(NB):
            for h in range(8):
                r = slice(h * D0, (h + 1) * D0)
                mem[r, g, n, r] = mems[n, g * 8 + h]
                mnorm[r, g, n, g * 8 + h] = norms[n, g * 8 + h]
    bank = i["L0_attn_bank_weights"]
    wq = i["L1_attn_wq"].reshape(D, H, NOPE + ROPE)
    wkv = i["L1_attn_wkv_b"].reshape(KVR, H, NOPE + VD)
    a_gate = i["L1_ffn_A_gate"].transpose(1, 0, 2).reshape(D, E * RANK)
    a_up = i["L1_ffn_A_up"].transpose(1, 0, 2).reshape(D, E * RANK)
    lora = np.zeros((72, DFF + D), np.float32)
    for g, (a, bm) in enumerate((("sA_gate", "sB_gate"), ("sA_up", "sB_up"), ("sA_down", "sB_down"))):
        a, bm = i["L1_ffn_" + a].T, i["L1_ffn_" + bm]
        lora[32 * g:32 * g + RANK, 0:a.shape[1]] = a
        lora[32 * g:32 * g + RANK, a.shape[1]:] = bm
    arrays = {
        "x": i["L0_attn_hidden_states"],
        "const": _constants(np),
        "wq0": i["L0_attn_Wq"].T,
        "wo0": i["L0_attn_Wo"].T,
        "mem": mem.reshape(128, 8, 128),
        "mnorm": mnorm.reshape(128, KD, 64),
        "mrow": norms.reshape(64, D0),
        "bw": np.tile(bank, (NB, 1)),
        "bwself": bank.T.reshape(64, 1),
        "wg": i["L0_ffn_w_gating"].transpose(1, 0, 2),
        "wl": i["L0_ffn_w_linear"],
        "wqT": wq[:, :, 0:NOPE].transpose(2, 1, 0),
        "wkT": wkv[:, :, 0:NOPE].transpose(2, 1, 0),
        "wqr": wq[:, :, NOPE:],
        "wvT": wkv[:, :, NOPE:].transpose(2, 1, 0),
        "wo": i["L1_attn_wo"],
        "wkva": i["L1_attn_wkv_a"],
        "kvw": i["L1_attn_kv_norm_w"],
        "ra": np.concatenate([i["L1_ffn_W_router"], a_gate, a_up], 1),
        "wgu": np.stack([i["L1_ffn_W_gate"], i["L1_ffn_W_up"]], 1),
        "wd": i["L1_ffn_W_down"],
        "lora": lora,
        "bgu": np.concatenate([i["L1_ffn_B_gate"].reshape(64, DFF), i["L1_ffn_B_up"].reshape(64, DFF)], 0),
        "ad": i["L1_ffn_A_down"].transpose(1, 0, 2).reshape(DFF, 64),
        "bd": i["L1_ffn_B_down"].reshape(64, D),
        "ebias": i["L1_ffn_expert_bias"],
    }
    nc = bacc.Bacc("TRN2", target_bir_lowering=False, num_devices=1)
    ins, args = {}, []
    for name, a in arrays.items():
        a = np.ascontiguousarray(a)
        ins[name + "_dram"] = a
        args.append(nc.dram_tensor(name + "_dram", a.shape, mybir.dt.from_np(a.dtype), kind="ExternalInput").ap())
    args.append(nc.dram_tensor("out_dram", (B, T, D), mybir.dt.float32, kind="ExternalOutput").ap())
    fused_two_layers(nc, *args)
    r = run_bass_kernel_spmd(nc, [ins], core_ids=[0])
    return r.results[0]["out_dram"]
```

```python
import concourse.bass as bass
from concourse import mybir
from contextlib import ExitStack

B, T, D = 2, 1024, 256
H0, D0, NB = 16, 16, 4
HID = 1024
H, NOPE, ROPE, VD, KVR = 16, 128, 64, 128, 64
E, RANK, DFF = 8, 8, 688
CH = 512
NC = T // CH
TPC = CH // 128
KD = D // 128
FM = [(m * 128, min(128, DFF - m * 128)) for m in range((DFF + 127) // 128)]
NM = len(FM)
SCALE = (NOPE + ROPE) ** -0.5
LN_EPS, MEM_EPS, RMS_EPS = 1e-5, 1e-6, 1e-6
MASKED = -1e30
ACT_TILES = (0, 1)
RINGS, LAGS = (4, 2), (2, 1)
TURN_BANKS = ((4, 5, 1, 3), (4, 5))
GELU_C, GELU_S = 0.044677734375, 0.796875

C_ID, C_MASK, C_SEL = 0, 128, 256
C_TRI = C_SEL + 8 * 128
C_BLK = C_TRI + 64
C_COS = C_BLK + 64
C_SIN = C_COS + 8 * 64
C_END = C_SIN + 8 * 64



def fused_two_layers(nc, x_in, const_in, wq0_in, wo0_in, mem_in, mnorm_in, mrow_in, bw_in, bwself_in,
                     wg_in, wl_in, wqT_in, wkT_in, wqr_in, wvT_in, wo_in, wkva_in, kvw_in,
                     ra_in, wgu_in, wd_in, lora_in, bgu_in, ad_in, bd_in, ebias_in, out):
    fp32, bf16, fp8 = mybir.dt.float32, mybir.dt.bfloat16, mybir.dt.float8e4
    ALU, ACT, AX = mybir.AluOpType, mybir.ActivationFunctionType, mybir.AxisListType

    ctx = ExitStack()
    with ctx:
        def sb(name, shape, dt=fp32):
            return ctx.enter_context(nc.sbuf_tensor(name, shape, dt))

        def sem(name):
            return ctx.enter_context(nc.semaphore(name))

        xg = sb("xg", [128, NC, TPC, D])
        const = sb("const", [128, C_END])
        ident = const[:, C_ID:C_ID + 128]
        sel = const[:, C_SEL:C_TRI].rearrange("p (j c) -> p j c", j=8)
        tri = const[:, C_TRI:C_BLK].rearrange("p (e f) -> p e f", e=E)
        blk = const[:, C_BLK:C_COS]
        cos = const[:, C_COS:C_SIN].rearrange("p (t r) -> p t r", t=8)
        sin = const[:, C_SIN:C_END].rearrange("p (t r) -> p t r", t=8)
        identb = sb("identb", [128, 128], bf16)
        maskb = sb("maskb", [128, 128], bf16)
        selb = sb("selb", [128, 8, 128], bf16)
        wq0 = sb("wq0", [128, KD, D])
        wo0 = sb("wo0", [128, KD, D])
        mem = sb("mem", [128, 8, 128])
        mnorm = sb("mnorm", [128, KD, 64])
        mrow = sb("mrow", [64, D0])
        bw = sb("bw", [64, NB])
        bwself = sb("bwself", [64, 1])
        bankw = sb("bankw", [64, 1])
        bsm = sb("bsm", [64, 16])
        wg8 = sb("wg8", [128, KD, 2, HID], fp8)
        wl8 = sb("wl8", [128, HID // 128, D], fp8)
        WQH = sb("WQH", [128, KD, H, 128], bf16)
        WQL = sb("WQL", [128, KD, H, 128], bf16)
        GH = sb("GH", [128, H, D], bf16)
        GL = sb("GL", [128, H, D], bf16)
        KVH = sb("KVH", [128, KD, 128], bf16)
        KVL = sb("KVL", [128, KD, 128], bf16)
        kvw = sb("kvw", [128, KVR])
        ra = sb("ra", [128, KD, 136])
        GUH = sb("GUH", [128, KD, 2, DFF], bf16)
        GUL = sb("GUL", [128, KD, 2, DFF], bf16)
        WDH = sb("WDH", [128, NM, D], bf16)
        WDL = sb("WDL", [128, NM, D], bf16)
        BGH = sb("BGH", [128, DFF], bf16)
        BGL = sb("BGL", [128, DFF], bf16)
        ADH = sb("ADH", [128, NM, 64], bf16)
        ADL = sb("ADL", [128, NM, 64], bf16)
        BDH = sb("BDH", [64, D], bf16)
        BDL = sb("BDL", [64, D], bf16)
        ebias = sb("ebias", [128, E])
        KTH = sb("KTH", [128, T], bf16)
        KTL = sb("KTL", [128, T], bf16)
        LAT = sb("LAT", [128, T // 128, 128], bf16)
        XH = sb("XH", [128, KD, CH], bf16)
        XL = sb("XL", [128, KD, CH], bf16)
        nhalf = sb("nhalf", [128, TPC])
        stats = sb("stats", [128, TPC, 6])
        mv = sb("mv", [128, TPC, 2])
        ve = sb("ve", [128, TPC])
        rstd = sb("rstd", [128, TPC])
        nm = sb("nm", [128, 8])
        rs = sb("rs", [128, 8])
        rl = sb("rl", [128, 8])

        ARENA = 25700
        arena = sb("arena", [128, ARENA])

        class Cut:
            def __init__(self):
                self.at = 0

            def take(self, words, dt=fp32):
                a = arena[:, self.at:self.at + words]
                self.at += words
                assert self.at <= ARENA, self.at
                return a if dt == fp32 else a.bitcast(dt)

        cut = Cut()
        r_wqT = cut.take(H * D).rearrange("p (h d) -> p h d", h=H)
        r_wkT = cut.take(H * 64).rearrange("p (h d) -> p h d", h=H)
        r_wqr = cut.take(KD * H * 64).rearrange("p (k h d) -> p k h d", k=KD, h=H)
        r_wvT = cut.take(H * 64).rearrange("p (h d) -> p h d", h=H)
        r_wo = cut.take(H * D).rearrange("p (h d) -> p h d", h=H)
        r_kva = cut.take(KD * 128).rearrange("p (k d) -> p k d", k=KD)
        r_gu = cut.take(KD * 2 * DFF).rearrange("p (k g d) -> p k g d", k=KD, g=2)
        r_wd = cut.take(NM * D).rearrange("p (m d) -> p m d", m=NM)
        r_lora = cut.take(DFF + D)
        r_bgu = cut.take(DFF)
        r_ad = cut.take(NM * 64).rearrange("p (m d) -> p m d", m=NM)
        r_bd = cut.take(D)
        r_wg = cut.take(KD * 2 * HID).rearrange("p (k g d) -> p k g d", k=KD, g=2)
        r_wl = cut.take(8 * D).rearrange("p (k d) -> p k d", k=8)

        cut = Cut()
        QTH = cut.take(H * CH // 2, bf16).rearrange("p (h n) -> p h n", h=H)
        QTL = cut.take(H * CH // 2, bf16).rearrange("p (h n) -> p h n", h=H)
        P = cut.take(2 * TPC * T).rearrange("p (b t n) -> p b t n", b=2, t=TPC)
        qtok = cut.take(2 * 512).rearrange("p (b h c) -> p b h c", b=2, h=4)
        qr1 = cut.take(2 * 256).rearrange("p (b h c) -> p b h c", b=2, h=4)
        qr2 = cut.take(2 * 256).rearrange("p (b h c) -> p b h c", b=2, h=4)
        PH = cut.take(2 * CH, bf16).rearrange("p (b n) -> p b n", b=4)
        PL = cut.take(2 * CH, bf16).rearrange("p (b n) -> p b n", b=4)

        cut = Cut()
        cut.at = H * CH
        ex = cut.take(KD * CH).rearrange("p (k n) -> p k n", k=KD)
        sig = cut.take(KD * CH).rearrange("p (k n) -> p k n", k=KD)
        sn = cut.take(2 * CH).rearrange("p (b n) -> p b n", b=2)
        rnorm = cut.take(CH)
        rsplit = cut.take(CH // 2, bf16)
        gcp = cut.take(4 * CH, bf16).rearrange("p (b g n) -> p b g n", b=4, g=2)
        ucp = cut.take(4 * CH, bf16).rearrange("p (b g n) -> p b g n", b=4, g=2)
        inner = cut.take(2 * CH, bf16).rearrange("p (b g n) -> p b g n", b=2, g=2)
        tanhg = cut.take(2 * CH, bf16).rearrange("p (b g n) -> p b g n", b=2, g=2)
        act8 = cut.take(8 * CH // 4, fp8).rearrange("p (k n) -> p k n", k=8)
        combT = cut.take(KD * CH).rearrange("p (k n) -> p k n", k=KD)
        fb = cut.take(TPC * D // 2, bf16).rearrange("p (t d) -> p t d", t=TPC)
        xq8 = cut.take(KD * CH // 4, fp8).rearrange("p (k n) -> p k n", k=KD)
        l0_low = cut.at
        xn = cut.take(TPC * D).rearrange("p (t d) -> p t d", t=TPC)
        xnT = cut.take(KD * CH).rearrange("p (k n) -> p k n", k=KD)

        cut = Cut()
        th = cut.take(TPC * E).rearrange("p (t e) -> p t e", t=TPC)
        bi = cut.take(TPC * E).rearrange("p (t e) -> p t e", t=TPC)
        cmp1 = cut.take(TPC * 64).rearrange("p (t e f) -> p t e f", t=TPC, e=E)
        cmp2 = cut.take(TPC * 64).rearrange("p (t e f) -> p t e f", t=TPC, e=E)
        rank = cut.take(TPC * E).rearrange("p (t e) -> p t e", t=TPC)
        wex = cut.take(TPC * E).rearrange("p (t e) -> p t e", t=TPC)
        den = cut.take(TPC)
        xaw = cut.take(TPC * 128).rearrange("p (t c) -> p t c", t=TPC)
        ZH = cut.take(CH // 2, bf16)
        ZL = cut.take(CH // 2, bf16)
        kvs = cut.take(TPC * 128).rearrange("p (t c) -> p t c", t=TPC)
        ktok = cut.take(TPC * 128).rearrange("p (t c) -> p t c", t=TPC)
        ksq = cut.take(TPC * 64).rearrange("p (t c) -> p t c", t=TPC)
        kr1 = cut.take(TPC * 64).rearrange("p (t c) -> p t c", t=TPC)
        kr2 = cut.take(TPC * 64).rearrange("p (t c) -> p t c", t=TPC)
        kss = cut.take(TPC)
        knr = cut.take(TPC)
        tt = cut.take(2 * CH).rearrange("p (b n) -> p b n", b=2)
        a1 = cut.take(2 * CH).rearrange("p (b n) -> p b n", b=2)
        hf = cut.take(2 * CH).rearrange("p (b n) -> p b n", b=2)
        HH = cut.take(NM * CH // 2, bf16).rearrange("p (m n) -> p m n", m=NM)
        HL = cut.take(NM * CH // 2, bf16).rearrange("p (m n) -> p m n", m=NM)
        zw = cut.take(TPC * 64).rearrange("p (t c) -> p t c", t=TPC)
        Z2H = cut.take(CH // 2, bf16)
        Z2L = cut.take(CH // 2, bf16)
        assert cut.at <= l0_low

        ps = ctx.enter_context(nc.psum_tensor("ps", [128, 8, 512], fp32))

        def token_major(bank, t):
            return ps[:, bank + t // 2, (t % 2) * 256:(t % 2) * 256 + D]

        def token_major_all(bank):
            return ps[:, bank:bank + 2, :].rearrange("p b (t d) -> p (b t) d", t=2)

        loads = ["const", "small", "l0", "wg", "wl", "wq", "wv", "kva", "gu", "wd", "tail"]
        ld = {n: sem("loaded_" + n) for n in loads}
        x_loaded = [sem(f"x_loaded{c}") for c in range(NC)]
        prep_mm = sem("prep_mm")
        prep_hi = sem("prep_hi")
        prep_lo = sem("prep_lo")
        prep_dve = sem("prep_dve")
        prep_act = sem("prep_act")
        prep_done = sem("prep_done")
        half_set = sem("half_set")
        link = sem("dve_link")
        names = """var_ready rstd_ready xn_ready xT_ready xnT_ready xq8_ready xsplit_ready q_ready e_ready sig_ready
        gu_ready gate_copied up_copied sq_ready inner_ready tanh_ready act8_ready norm_ready rh_ready r_ready rbc_ready sn_ready comb_done
        combT_ready y0_ready y1_ready fb_ready ra_ready th_ready kvc_ready kvs_ready kss_ready knr_ready ktok_ready
        kT_ready kth_ready ktl_ready xaw_ready xawT_ready zh_ready zl_ready m_ready tt_ready hf_ready hh_ready hs_ready
        z_ready zw_ready z2T_ready z2h_ready z2l_ready y2_ready x2_ready
        qp_ready qn_ready qr_ready qrope_parts qt_ready qth_ready qtl_ready
        s_ready max_ready exp_done rl_ready pn_act pn_dve pt_ready pth_ready ptl_ready pv_done cth_ready ctl_ready
        o_ready out_added""".split()
        S = {n: sem(n) for n in names}
        stored = sem("stored")

        block = ctx.enter_context(nc.Block())

        def row(c):
            return slice(c * CH, (c + 1) * CH)

        @block.sync
        def _(sp):
            def load(dst, src, name):
                sp.dma_start(dst, src).then_inc(ld[name], 16)

            def x_rows(b, c):
                return x_in[b, row(c), :].rearrange("(t p) d -> p t d", p=128)

            def out_rows(b, c):
                return out[b, row(c), :].rearrange("(t p) d -> p t d", p=128)

            load(const[:, :], const_in, "const")
            for c in range(NC):
                sp.dma_start(xg[:, c], x_rows(0, c)).then_inc(x_loaded[c], 16)
            load(r_wg.rearrange("p k g n -> p k (g n)"), wg_in.rearrange("(k p) g n -> p k (g n)", p=128), "wg")
            load(r_wl, wl_in.rearrange("(k p) n -> p k n", p=128), "wl")
            load(r_wqT, wqT_in, "wq")
            load(r_wkT, wkT_in, "wq")
            load(r_wqr.rearrange("p k h n -> p k (h n)"), wqr_in.rearrange("(k p) h n -> p k (h n)", p=128), "wq")
            for b in range(B):
                for c in range(NC):
                    sp.wait_ge(S["out_added"], (b * NC + c + 1) * TPC)
                    sp.dma_start(out_rows(b, c), xg[:, c]).then_inc(stored, 16)
                    if b + 1 < B:
                        sp.wait_ge(stored, 16 * (b * NC + c + 1))
                        sp.dma_start(xg[:, c], x_rows(b + 1, c)).then_inc(x_loaded[c], 16)
            sp.wait_ge(stored, 16 * B * NC)

        @block.gpsimd
        def _(pool):
            def load(dst, src, name):
                pool.dma_start(dst, src).then_inc(ld[name], 16)

            nc.gpsimd.memset(nhalf[:, :], -0.5).then_inc(half_set, 1)
            load(r_wvT, wvT_in, "wv")
            load(r_wo, wo_in.rearrange("(h p) n -> p h n", p=128), "wv")
            pool.wait_ge(half_set, 1)
            for n in range(B * NC):
                for l in range(2):
                    pool.wait_ge(S["var_ready"], n * 2 + l + 1)
                    nc.gpsimd.tensor_tensor(rstd[:, :], ve[:, :], nhalf[:, :], ALU.pow) \
                        .then_inc(S["rstd_ready"], 1)
                pool.wait_ge(S["kss_ready"], n + 1)
                nc.gpsimd.tensor_tensor(knr, kss, nhalf[:, :], ALU.pow).then_inc(S["knr_ready"], 1)

        BANKS = [("wq", i) for i in range(4)] + [("g", i) for i in range(8)] \
            + [("gu", i) for i in range(4)] + [("wd", i) for i in range(NM // 2)]

        def bank_of(i):
            return 2 * (i % 4)

        @block.scalar
        def _(act):
            def load(dst, src, name):
                act.dma_start(dst, src).then_inc(ld[name], 16)

            load(mrow[:, :], mrow_in, "small")
            load(bw[:, :], bw_in, "small")
            load(bwself[:, :], bwself_in, "small")
            load(wq0[:, :, :], wq0_in.rearrange("(k p) n -> p k n", p=128), "l0")
            load(wo0[:, :, :], wo0_in.rearrange("(k p) n -> p k n", p=128), "l0")
            load(mem[:, :, :], mem_in, "l0")
            load(mnorm[:, :, :], mnorm_in, "l0")
            load(r_kva, wkva_in.rearrange("(k p) n -> p k n", p=128), "kva")
            load(kvw[:, :], kvw_in.partition_broadcast(128), "kva")
            load(ebias[:, :], ebias_in.partition_broadcast(128), "kva")
            load(ra[:, :, :], ra_in.rearrange("(k p) n -> p k n", p=128), "kva")
            load(r_gu.rearrange("p k g n -> p k (g n)"), wgu_in.rearrange("(k p) g n -> p k (g n)", p=128), "gu")
            load(r_lora[0:72, :], lora_in, "gu")
            load(r_wd[:, 0:NM - 1, :], wd_in[0:(NM - 1) * 128, :].rearrange("(m p) n -> p m n", p=128), "wd")
            load(r_wd[0:FM[-1][1], NM - 1, :], wd_in[(NM - 1) * 128:DFF, :], "wd")
            load(r_bgu, bgu_in, "tail")
            load(r_ad[:, 0:NM - 1, :], ad_in[0:(NM - 1) * 128, :].rearrange("(m p) n -> p m n", p=128), "tail")
            load(r_ad[0:FM[-1][1], NM - 1, :], ad_in[(NM - 1) * 128:DFF, :], "tail")
            load(r_bd[0:64, :], bd_in, "tail")

            act.wait_ge(prep_dve, 2)
            nc.scalar.activation(bsm[:, 4:8], bw[:, :], ACT.Exp, bias=bsm[:, 0:1]).then_inc(prep_act, 1)
            nc.scalar.activation(bsm[:, 8:9], bwself[:, :], ACT.Exp, bias=bsm[:, 0:1]).then_inc(prep_act, 1)
            act.wait_ge(ld["wq"], 48)
            for k in range(KD):
                nc.scalar.activation(WQH[:, k, :, 64:128], r_wqr[:, k], ACT.Copy, scale=SCALE) \
                    .then_inc(prep_act, 1)
            for i, (kind, j) in enumerate(BANKS):
                src = ps[:, bank_of(i)]
                if kind == "wq":
                    act.wait_ge(prep_mm, i + 2)
                    k, hh = j // 2, j % 2
                    nc.scalar.activation(WQH[:, k, 8 * hh:8 * hh + 8, 0:64],
                                         src.rearrange("p (h d) -> p h d", h=8), ACT.Copy, scale=SCALE) \
                        .then_inc(prep_hi, 1)
                elif kind == "g":
                    act.wait_ge(prep_mm, i + 2)
                    nc.scalar.copy(GH[:, 2 * j:2 * j + 2, :], src.rearrange("p (h d) -> p h d", h=2)) \
                        .then_inc(prep_hi, 1)
                elif kind == "gu":
                    act.wait_ge(prep_lo, 2 * i + 1)
                    k, g = j // 2, j % 2
                    nc.scalar.copy(GUH[:, k, g, :], r_gu[:, k, g, :]).then_inc(prep_hi, 1)
                else:
                    act.wait_ge(prep_lo, 2 * i + 1)
                    if j < NM // 2 - 1:
                        nc.scalar.copy(WDH[:, 2 * j:2 * j + 2, :], r_wd[:, 2 * j:2 * j + 2, :]).then_inc(prep_hi, 1)
                    else:
                        w = FM[-1][1]
                        nc.scalar.copy(WDH[:, 2 * j, :], r_wd[:, 2 * j, :])
                        nc.scalar.copy(WDH[0:w, 2 * j + 1, :], r_wd[0:w, 2 * j + 1, :]).then_inc(prep_hi, 1)

            def layer0(n):
                act.wait_ge(S["xT_ready"], 2 * n + 1)
                nc.scalar.copy(xnT, ps[:, 6:8, :]).then_inc(S["xnT_ready"], 1)
                act.wait_ge(S["q_ready"], n + 1)
                nc.scalar.activation(ex, ps[:, 6:8, :], ACT.Exp).then_inc(S["e_ready"], 1)
                for q in range(5):
                    i = n * 4 + q
                    if q < 4:
                        act.wait_ge(S["gu_ready"], i + 1)
                        nc.scalar.copy(gcp[:, q], ps[:, 2:4, :]).then_inc(S["gate_copied"], 1)
                        nc.scalar.copy(ucp[:, q], ps[:, 4:6, :]).then_inc(S["up_copied"], 1)
                        act.wait_ge(S["gate_copied"], i + 1)
                        if q >= 2:
                            act.wait_ge(S["tanh_ready"], i - 1)
                        nc.scalar.activation(inner[:, q % 2], gcp[:, q], ACT.Square).then_inc(S["sq_ready"], 1)
                    if q >= 1:
                        act.wait_ge(S["inner_ready"], i)
                        if q >= 3:
                            act.wait_ge(S["act8_ready"], i - 2)
                        nc.scalar.activation(tanhg[:, (q - 1) % 2], inner[:, (q - 1) % 2], ACT.Tanh) \
                            .then_inc(S["tanh_ready"], 1)
                act.wait_ge(S["comb_done"], 8 * n + 8)
                nc.scalar.copy(combT, ps[:, 6:8, :]).then_inc(S["combT_ready"], 1)
                act.wait_ge(S["y0_ready"], n + 1)
                nc.scalar.copy(fb, token_major_all(2)).then_inc(S["fb_ready"], 1)

            def layer1(n):
                b, c = n // NC, n % NC
                act.wait_ge(S["xT_ready"], 2 * n + 2)
                nc.scalar.copy(xnT, ps[:, 6:8, :]).then_inc(S["xnT_ready"], 1)
                act.wait_ge(S["ra_ready"], n + 1)
                nc.scalar.activation(th, token_major_all(0)[:, :, 0:E], ACT.Tanh, scale=0.5) \
                    .then_inc(S["th_ready"], 1)
                act.wait_ge(S["kvc_ready"], n + 1)
                nc.scalar.copy(kvs, ps[:, 6, :].rearrange("p (t c) -> p t c", t=TPC)).then_inc(S["kvs_ready"], 1)
                act.wait_ge(S["xawT_ready"], n + 1)
                nc.scalar.copy(ZH, ps[:, 1, :]).then_inc(S["zh_ready"], 1)

                def gate_tanh(m):
                    i, w = n * NM + m, FM[m][1]
                    act.wait_ge(S["m_ready"], i + 1)
                    if m >= 2:
                        act.wait_ge(S["hf_ready"], i - 1)
                    nc.scalar.activation(tt[0:w, m % 2], ps[0:w, 2 + 2 * (m % 2), :], ACT.Tanh, scale=0.5) \
                        .then_inc(S["tt_ready"], 1)

                def hidden_high(m):
                    w = FM[m][1]
                    act.wait_ge(S["hf_ready"], n * NM + m + 1)
                    nc.scalar.copy(HH[0:w, m], hf[0:w, m % 2]).then_inc(S["hh_ready"], 1)

                gate_tanh(0)
                gate_tanh(1)
                act.wait_ge(S["kT_ready"], n + 1)
                nc.scalar.copy(KTH[:, row(c)], ps[:, 7, :]).then_inc(S["kth_ready"], 1)
                hidden_high(0)
                hidden_high(1)
                for m in range(2, NM):
                    gate_tanh(m)
                    hidden_high(m)
                act.wait_ge(S["z2T_ready"], n + 1)
                nc.scalar.copy(Z2H[0:64, :], ps[0:64, 0, :]).then_inc(S["z2h_ready"], 1)

                def nope(i):
                    u = n * 16 + i
                    act.wait_ge(S["qp_ready"], u + 1)
                    if i >= 2:
                        act.wait_ge(S["qt_ready"], u - 1)
                    nc.scalar.copy(qtok[:, i % 2, :, 0:64],
                                   ps[:, i % 2, :].rearrange("p (h c) -> p h c", h=4)[:, :, 0:64]) \
                        .then_inc(S["qn_ready"], 1)

                def q_high(i):
                    u, t, q = n * 16 + i, i // 4, i % 4
                    act.wait_ge(S["qt_ready"], u + 1)
                    nc.scalar.copy(QTH[:, 4 * q:4 * q + 4, t * 128:t * 128 + 128],
                                   ps[:, 2 + i % 2, :].rearrange("p (h c) -> p h c", h=4)) \
                        .then_inc(S["qth_ready"], 1)

                for i in range(17):
                    if i < 16:
                        nope(i)
                    if i >= 1:
                        q_high(i - 1)

                NJ = TPC * (c + 1)

                def slice_of(t):
                    return range((c + 1) * t, (c + 1) * (t + 1))

                RING, LAG = RINGS[c], LAGS[c]

                def jn(h, j):
                    return b * (16 * 12) + c * 64 + h * NJ + j

                def p_high(h, par, j, first=False):
                    w0 = max(0, j - TPC * c) * 128
                    i = jn(h, j)
                    act.wait_ge(S["pt_ready"], i + 1)
                    if not (first and j < RING):
                        act.wait_ge(S["pv_done"], i - RING + 1)
                    nc.scalar.copy(PH[:, j % RING, w0:CH], ps[:, TURN_BANKS[c][j % RING], w0:CH]) \
                        .then_inc(S["pth_ready"], 1)

                def exps(h, par, t):
                    w = (TPC * c + t + 1) * 128
                    i = ((b * NC + c) * 16 + h) * 4 + t
                    act.wait_ge(S["max_ready"], i + 1)
                    nc.scalar.activation(P[:, par, t, 0:w], ps[:, 2 * (t % 2):2 * (t % 2) + 2, :]
                                         .rearrange("p b n -> p (b n)")[:, 0:w], ACT.Exp,
                                         bias=nm[:, 4 * par + t:4 * par + t + 1],
                                         accum_out=rs[:, 4 * par + t:4 * par + t + 1]).then_inc(S["exp_done"], 1)

                def normalise(h, par, t):
                    w = (TPC * c + t + 1) * 128
                    i = ((b * NC + c) * 16 + h) * 4 + t
                    act.wait_ge(S["rl_ready"], i + 1)
                    nc.scalar.activation(P[:, par, t, 0:w], P[:, par, t, 0:w], ACT.Copy,
                                         scale=rl[:, 4 * par + t:4 * par + t + 1]).then_inc(S["pn_act"], 1)

                def context_high(h, par):
                    act.wait_ge(S["pv_done"], jn(h, NJ - 1) + 1)
                    nc.scalar.copy(QTH[:, h, :] if isinstance(h, int) else
                                   QTH[:, bass.ds(h, 1), :].rearrange("p a n -> p (a n)"),
                                   ps[:, 6 + par, :]).then_inc(S["cth_ready"], 1)

                def step(h, par, first=False):
                    for t in range(TPC):
                        if t == LAG - 1 and not first:
                            context_high(h - 2, par)
                        for j in slice_of(t):
                            p_high(h - 1, 1 - par, j, first)
                        if t == 0 and not first:
                            act.wait_ge(S["pt_ready"], jn(h - 1, 0))
                        exps(h, par, t)
                        if t - 1 in ACT_TILES:
                            normalise(h, par, t - 1)

                for t in range(TPC):
                    exps(0, 0, t)
                    if t - 1 in ACT_TILES:
                        normalise(0, 0, t - 1)
                step(1, 1, first=True)
                with act.Fori(1, H // 2) as hp:
                    step(hp * 2, 0)
                    step(hp * 2 + 1, 1)
                context_high(H - 2, 0)
                for j in range(NJ):
                    p_high(H - 1, 1, j)
                context_high(H - 1, 1)

            layer0(0)
            for n in range(B * NC):
                layer1(n)
                if n + 1 < B * NC:
                    layer0(n + 1)

        @block.vector
        def _(dve):
            v = nc.vector
            count = [0]

            def own(ins):
                count[0] += 1
                ins.then_inc(prep_dve, 1)
                dve.wait_ge(prep_dve, count[0])

            dve.wait_ge(ld["small"], 48)
            own(v.tensor_reduce(bsm[:, 0:1], bw[:, :], AX.X, ALU.max, negate=True))
            own(v.tensor_reduce(bsm[:, 1:2], mrow[:, :], AX.X, ALU.add))
            dve.wait_ge(prep_act, 2)
            own(v.tensor_reduce(bsm[:, 2:3], bsm[:, 4:8], AX.X, ALU.add))
            own(v.reciprocal(bsm[:, 3:4], bsm[:, 2:3]))
            own(v.tensor_tensor(bsm[:, 9:10], bsm[:, 8:9], bsm[:, 3:4], ALU.mult))
            dve.wait_ge(prep_mm, 1)
            own(v.tensor_scalar(bankw[:, :], ps[0:64, 7, 0:1], MEM_EPS, bsm[:, 9:10], ALU.is_ge, ALU.mult))
            dve.wait_ge(ld["const"], 16)
            v.tensor_copy(identb[:, :], ident)
            v.tensor_copy(selb[:, :, :], sel)
            v.tensor_copy(maskb[:, :], const[:, C_MASK:C_MASK + 128])
            dve.wait_ge(ld["wg"], 16)
            v.tensor_copy(wg8[:, :, :, :], r_wg, saturate=True)
            dve.wait_ge(ld["wl"], 16)
            v.tensor_copy(wl8[:, :, :], r_wl, saturate=True)
            dve.wait_ge(prep_act, 4)
            for k in range(KD):
                v.scalar_tensor_tensor(WQL[:, k, :, 64:128], r_wqr[:, k], SCALE, WQH[:, k, :, 64:128],
                                       ALU.mult, ALU.subtract)
            dve.wait_ge(ld["kva"], 64)
            dve.wait_ge(ld["tail"], 64)
            w = FM[-1][1]
            v.tensor_copy(KVH[:, :, :], r_kva)
            v.tensor_copy(BGH[:, :], r_bgu)
            v.tensor_copy(ADH[:, 0:NM - 1, :], r_ad[:, 0:NM - 1, :])
            v.tensor_copy(ADH[0:w, NM - 1, :], r_ad[0:w, NM - 1, :])
            own(v.tensor_copy(BDH[:, :], r_bd[0:64, :]))
            v.tensor_tensor(KVL[:, :, :], r_kva, KVH[:, :, :], ALU.subtract)
            v.tensor_tensor(BGL[:, :], r_bgu, BGH[:, :], ALU.subtract)
            v.tensor_tensor(ADL[:, 0:NM - 1, :], r_ad[:, 0:NM - 1, :], ADH[:, 0:NM - 1, :], ALU.subtract)
            v.tensor_tensor(ADL[0:w, NM - 1, :], r_ad[0:w, NM - 1, :], ADH[0:w, NM - 1, :], ALU.subtract)
            own(v.tensor_tensor(BDL[:, :], r_bd[0:64, :], BDH[:, :], ALU.subtract))
            for i, (kind, j) in enumerate(BANKS):
                src = ps[:, bank_of(i)]
                if kind == "wq":
                    k, hh = j // 2, j % 2
                    dve.wait_ge(prep_hi, i + 1)
                    v.scalar_tensor_tensor(WQL[:, k, 8 * hh:8 * hh + 8, 0:64],
                                           src.rearrange("p (h d) -> p h d", h=8), SCALE,
                                           WQH[:, k, 8 * hh:8 * hh + 8, 0:64], ALU.mult, ALU.subtract) \
                        .then_inc(prep_lo, 2)
                elif kind == "g":
                    dve.wait_ge(prep_hi, i + 1)
                    v.tensor_tensor(GL[:, 2 * j:2 * j + 2, :], src.rearrange("p (h d) -> p h d", h=2),
                                    GH[:, 2 * j:2 * j + 2, :], ALU.subtract).then_inc(prep_lo, 2)
                elif kind == "gu":
                    k, g = j // 2, j % 2
                    dve.wait_ge(prep_mm, i + 2)
                    two = ps[:, bank_of(i):bank_of(i) + 2, :].rearrange("p b n -> p (b n)")[:, 0:DFF]
                    v.scalar_tensor_tensor(r_gu[:, k, g, :], two, 1.0 / RANK, r_gu[:, k, g, :],
                                           ALU.mult, ALU.add).then_inc(prep_lo, 1)
                    dve.wait_ge(prep_hi, i + 1)
                    v.tensor_tensor(GUL[:, k, g, :], r_gu[:, k, g, :], GUH[:, k, g, :], ALU.subtract) \
                        .then_inc(prep_lo, 1)
                else:
                    dve.wait_ge(prep_mm, i + 2)
                    rows = [128, 128 if j < NM // 2 - 1 else FM[-1][1]]
                    for a in range(2):
                        m = 2 * j + a
                        ins = v.scalar_tensor_tensor(r_wd[0:rows[a], m, :], src[0:rows[a], a * D:a * D + D],
                                                     1.0 / RANK, r_wd[0:rows[a], m, :], ALU.mult, ALU.add)
                    ins.then_inc(prep_lo, 1)
                    dve.wait_ge(prep_hi, i + 1)
                    for a in range(2):
                        m = 2 * j + a
                        ins = v.tensor_tensor(WDL[0:rows[a], m, :], r_wd[0:rows[a], m, :],
                                              WDH[0:rows[a], m, :], ALU.subtract)
                    ins.then_inc(prep_lo, 1)
            v.memset(stats[:, :, :], 0.0).then_inc(prep_done, 1)
            dve.wait_ge(prep_done, 1)

            k_link = [0]

            def linked(ins):
                k_link[0] += 1
                ins.then_inc(link, 1)
                dve.wait_ge(link, k_link[0])

            def layernorm(n, l):
                i, c = 2 * n + l, n % NC
                for t in range(TPC):
                    ins = v.bn_stats(stats[:, t, :], xg[:, c, t, :])
                linked(ins)
                for t in range(TPC):
                    ins = v.bn_aggr(mv[:, t, :], stats[:, t, :])
                linked(ins)
                v.tensor_scalar(ve[:, :], mv[:, :, 1], LN_EPS, None, ALU.add).then_inc(S["var_ready"], 1)
                dve.wait_ge(S["rstd_ready"], i + 1)
                for t in range(TPC):
                    ins = v.tensor_scalar(xn[:, t, :], xg[:, c, t, :], mv[:, t, 0:1], rstd[:, t:t + 1],
                                          ALU.subtract, ALU.mult)
                ins.then_inc(S["xn_ready"], 1)

            def add_output(n, t):
                dve.wait_ge(S["o_ready"], n * TPC + t + 1)
                v.tensor_tensor(xg[:, n % NC, t], xg[:, n % NC, t], ps[:, t % 2, 0:D], ALU.add) \
                    .then_inc(S["out_added"], 1)

            def layer0(n, prev):
                def output(t):
                    if prev is not None:
                        add_output(prev, t)

                c = n % NC
                dve.wait_ge(x_loaded[c], (n // NC) * 16 + 16)
                layernorm(n, 0)
                dve.wait_ge(S["xnT_ready"], 2 * n + 1)
                v.tensor_copy(xq8, ps[:, 6:8, :], saturate=True).then_inc(S["xq8_ready"], 1)
                output(0)
                dve.wait_ge(S["e_ready"], n + 1)
                linked(v.tensor_scalar(ex, ex, 1.0, None, ALU.min))
                for g in range(KD):
                    ins = v.scalar_tensor_tensor(sig[:, g], ps[:, 6 + g, :], 1.0, ex[:, g], ALU.add, ALU.max)
                ins.then_inc(S["sig_ready"], 1)

                def gelu_inner(q):
                    dve.wait_ge(S["sq_ready"], n * 4 + q + 1)
                    t = inner[:, q % 2]
                    linked(v.tensor_tensor(t, t, gcp[:, q], ALU.mult))
                    linked(v.tensor_scalar(t, t, GELU_C, None, ALU.mult))
                    linked(v.tensor_tensor(t, t, gcp[:, q], ALU.add))
                    v.tensor_scalar(t, t, GELU_S, None, ALU.mult).then_inc(S["inner_ready"], 1)

                def gelu_outer(q):
                    dve.wait_ge(S["tanh_ready"], n * 4 + q + 1)
                    t = tanhg[:, q % 2]
                    linked(v.tensor_scalar(t, t, 1.0, 0.5, ALU.add, ALU.mult))
                    linked(v.tensor_tensor(t, t, gcp[:, q], ALU.mult))
                    linked(v.tensor_tensor(t, t, ucp[:, q], ALU.mult))
                    v.tensor_copy(act8[:, 2 * q:2 * q + 2], t, saturate=True).then_inc(S["act8_ready"], 1)

                def weigh(j):
                    i = n * 8 + j
                    dve.wait_ge(S["rbc_ready"], i + 1)
                    if j >= 2:
                        dve.wait_ge(S["comb_done"], i - 1)
                    v.tensor_tensor(sn[:, j % 2], sig[:, j // 4], ps[:, 2 + j % 4, :], ALU.mult) \
                        .then_inc(S["sn_ready"], 1)

                gelu_inner(0)
                dve.wait_ge(S["norm_ready"], n + 1)
                linked(v.tensor_scalar(rnorm[0:64, :], ps[0:64, 6, :], MEM_EPS, None, ALU.max))
                linked(v.reciprocal(rnorm[0:64, :], rnorm[0:64, :]))
                linked(v.tensor_scalar(rnorm[0:64, :], rnorm[0:64, :], bankw[:, 0:1], None, ALU.mult))
                linked(v.tensor_copy(rsplit[0:64, :], rnorm[0:64, :]))
                v.tensor_tensor(rsplit[64:128, :], rnorm[0:64, :], rsplit[0:64, :], ALU.subtract) \
                    .then_inc(S["r_ready"], 1)
                gelu_inner(1)
                gelu_outer(0)
                output(1)
                gelu_inner(2)
                gelu_outer(1)
                for j in range(4):
                    weigh(j)
                gelu_inner(3)
                gelu_outer(2)
                gelu_outer(3)
                for j in range(4, 8):
                    weigh(j)
                output(2)
                dve.wait_ge(S["fb_ready"], n + 1)
                dve.wait_ge(S["y1_ready"], n + 1)
                linked(v.tensor_tensor(xg[:, c], xg[:, c], token_major_all(4), ALU.add))
                linked(v.tensor_tensor(xg[:, c], xg[:, c], fb, ALU.add))
                layernorm(n, 1)
                output(3)

            def layer1(n):
                b, c = n // NC, n % NC
                dve.wait_ge(S["xnT_ready"], 2 * n + 2)
                linked(v.tensor_copy(XH[:, :, :], ps[:, 6:8, :]))
                v.tensor_tensor(XL[:, :, :], ps[:, 6:8, :], XH[:, :, :], ALU.subtract) \
                    .then_inc(S["xsplit_ready"], 1)
                dve.wait_ge(S["th_ready"], n + 1)
                linked(v.tensor_scalar(th, th, 1.0, 0.5, ALU.add, ALU.mult))
                linked(v.tensor_tensor(bi, th, ebias[:, :].unsqueeze(1).broadcast_to([128, TPC, E]), ALU.add))
                mine = bi.unsqueeze(3).broadcast_to([128, TPC, E, E])
                other = bi.unsqueeze(2).broadcast_to([128, TPC, E, E])
                v.tensor_tensor(cmp1, other, mine, ALU.is_gt)
                linked(v.tensor_tensor(cmp2, other, mine, ALU.is_equal))
                linked(v.tensor_tensor(cmp2, cmp2, tri.unsqueeze(1).broadcast_to([128, TPC, E, E]), ALU.mult))
                linked(v.tensor_tensor(cmp1, cmp1, cmp2, ALU.add))
                linked(v.tensor_reduce(rank, cmp1, AX.X, ALU.add))
                linked(v.scalar_tensor_tensor(wex, rank, 2.0, th, ALU.is_lt, ALU.mult))
                linked(v.tensor_reduce(den, wex, AX.X, ALU.add))
                linked(v.tensor_scalar(den, den, 1e-8, None, ALU.add))
                linked(v.reciprocal(den, den))
                linked(v.scalar_tensor_tensor(wex, wex, 1.0 / RANK,
                                              den.unsqueeze(2).broadcast_to([128, TPC, E]), ALU.mult, ALU.mult))
                by_rank = wex.unsqueeze(3).broadcast_to([128, TPC, E, RANK])
                for g in range(2):
                    a = token_major_all(0)[:, :, E + 64 * g:E + 64 * g + 64]
                    ins = v.tensor_tensor(xaw[:, :, 64 * g:64 * g + 64].rearrange("p t (e r) -> p t e r", e=E),
                                          a.rearrange("p t (e r) -> p t e r", e=E), by_rank, ALU.mult)
                ins.then_inc(S["xaw_ready"], 1)
                dve.wait_ge(S["kvs_ready"], n + 1)
                linked(v.tensor_tensor(ksq, kvs[:, :, 0:64], kvs[:, :, 0:64], ALU.mult))
                linked(v.tensor_reduce(kss, ksq, AX.X, ALU.add))
                v.tensor_scalar(kss, kss, 1.0 / KVR, RMS_EPS, ALU.mult, ALU.add).then_inc(S["kss_ready"], 1)
                cs, sn_t = cos[:, TPC * c:TPC * c + TPC, :], sin[:, TPC * c:TPC * c + TPC, :]
                v.tensor_tensor(kr1, kvs[:, :, 64:128], cs, ALU.mult)
                v.tensor_tensor(kr2[:, :, 0:32], kvs[:, :, 96:128], sn_t[:, :, 0:32], ALU.mult)
                linked(v.tensor_tensor(kr2[:, :, 32:64], kvs[:, :, 64:96], sn_t[:, :, 32:64], ALU.mult))
                v.tensor_tensor(ktok[:, :, 64:128], kr1, kr2, ALU.add)
                dve.wait_ge(S["zh_ready"], n + 1)
                v.tensor_tensor(ZL, ps[:, 1, :], ZH, ALU.subtract).then_inc(S["zl_ready"], 1)
                dve.wait_ge(S["knr_ready"], n + 1)
                linked(v.tensor_tensor(ktok[:, :, 0:64], kvs[:, :, 0:64],
                                       knr.unsqueeze(2).broadcast_to([128, TPC, 64]), ALU.mult))
                v.tensor_tensor(ktok[:, :, 0:64], ktok[:, :, 0:64],
                                kvw[:, :].unsqueeze(1).broadcast_to([128, TPC, 64]), ALU.mult) \
                    .then_inc(S["ktok_ready"], 1)
                dve.wait_ge(S["ktok_ready"], n + 1)

                def hidden(m):
                    i, p, w = n * NM + m, m % 2, FM[m][1]
                    dve.wait_ge(S["tt_ready"], i + 1)
                    linked(v.scalar_tensor_tensor(a1[0:w, p], tt[0:w, p], 1.0, ps[0:w, 2 + 2 * p, :],
                                                  ALU.add, ALU.mult))
                    v.scalar_tensor_tensor(hf[0:w, p], a1[0:w, p], 0.5, ps[0:w, 3 + 2 * p, :],
                                           ALU.mult, ALU.mult).then_inc(S["hf_ready"], 1)

                def hidden_low(m):
                    w = FM[m][1]
                    dve.wait_ge(S["hh_ready"], n * NM + m + 1)
                    v.tensor_tensor(HL[0:w, m], hf[0:w, m % 2], HH[0:w, m], ALU.subtract) \
                        .then_inc(S["hs_ready"], 1)

                hidden(0)
                hidden(1)
                lat = LAT[:, TPC * c:TPC * c + TPC, :]
                linked(v.tensor_copy(lat[:, :, 0:64], ktok[:, :, 0:64]))
                linked(v.tensor_tensor(lat[:, :, 64:128], ktok[:, :, 0:64], lat[:, :, 0:64], ALU.subtract))
                dve.wait_ge(S["kth_ready"], n + 1)
                v.tensor_tensor(KTL[:, row(c)], ps[:, 7, :], KTH[:, row(c)], ALU.subtract) \
                    .then_inc(S["ktl_ready"], 1)
                hidden_low(0)
                hidden_low(1)
                for m in range(2, NM):
                    hidden(m)
                    hidden_low(m)
                dve.wait_ge(S["z_ready"], n + 1)
                v.tensor_tensor(zw.rearrange("p t (e r) -> p t e r", e=E),
                                ps[:, 1, 0:TPC * 64].rearrange("p (t e r) -> p t e r", t=TPC, e=E),
                                by_rank, ALU.mult).then_inc(S["zw_ready"], 1)
                dve.wait_ge(S["z2h_ready"], n + 1)
                v.tensor_tensor(Z2L[0:64, :], ps[0:64, 0, :], Z2H[0:64, :], ALU.subtract) \
                    .then_inc(S["z2l_ready"], 1)
                dve.wait_ge(S["y2_ready"], n + 1)
                linked(v.tensor_tensor(xg[:, c], xg[:, c], token_major_all(6), ALU.add))

                def rope(i):
                    u, t, p = n * 16 + i, i // 4, i % 2
                    src = ps[:, p, :].rearrange("p (h c) -> p h c", h=4)
                    cs = cos[:, TPC * c + t, :].unsqueeze(1).broadcast_to([128, 4, 64])
                    sa = sin[:, TPC * c + t, 0:32].unsqueeze(1).broadcast_to([128, 4, 32])
                    sb_ = sin[:, TPC * c + t, 32:64].unsqueeze(1).broadcast_to([128, 4, 32])
                    dve.wait_ge(S["qn_ready"], u + 1)
                    v.tensor_tensor(qr1[:, p], src[:, :, 64:128], cs, ALU.mult)
                    v.tensor_tensor(qr2[:, p, :, 0:32], src[:, :, 96:128], sa, ALU.mult)
                    v.tensor_tensor(qr2[:, p, :, 32:64], src[:, :, 64:96], sb_, ALU.mult) \
                        .then_inc(S["qrope_parts"], 1)
                    if i >= 2:
                        dve.wait_ge(S["qt_ready"], u - 1)
                    dve.wait_ge(S["qrope_parts"], u + 1)
                    v.tensor_tensor(qtok[:, p, :, 64:128], qr1[:, p], qr2[:, p], ALU.add) \
                        .then_inc(S["qr_ready"], 1)

                def q_low(i):
                    u, t, q = n * 16 + i, i // 4, i % 4
                    dve.wait_ge(S["qth_ready"], u + 1)
                    v.tensor_tensor(QTL[:, 4 * q:4 * q + 4, t * 128:t * 128 + 128],
                                    ps[:, 2 + i % 2, :].rearrange("p (h c) -> p h c", h=4),
                                    QTH[:, 4 * q:4 * q + 4, t * 128:t * 128 + 128], ALU.subtract) \
                        .then_inc(S["qtl_ready"], 1)

                for i in range(17):
                    if i < 16:
                        rope(i)
                    if i >= 1:
                        q_low(i - 1)

                NJ = TPC * (c + 1)

                def slice_of(t):
                    return range((c + 1) * t, (c + 1) * (t + 1))

                RING, LAG = RINGS[c], LAGS[c]

                def jn(h, j):
                    return b * (16 * 12) + c * 64 + h * NJ + j

                def row_max(h, par, t):
                    w = (TPC * c + t + 1) * 128
                    i = ((b * NC + c) * 16 + h) * 4 + t
                    dve.wait_ge(S["s_ready"], i + 1)
                    v.tensor_reduce(nm[:, 4 * par + t:4 * par + t + 1],
                                    ps[:, 2 * (t % 2):2 * (t % 2) + 2, :].rearrange("p b n -> p (b n)")[:, 0:w],
                                    AX.X, ALU.max, negate=True).then_inc(S["max_ready"], 1)

                def normalise(h, par, t):
                    w = (TPC * c + t + 1) * 128
                    i = ((b * NC + c) * 16 + h) * 4 + t
                    s = slice(4 * par + t, 4 * par + t + 1)
                    dve.wait_ge(S["exp_done"], i + 1)
                    v.reciprocal(rl[:, s], rs[:, s]).then_inc(S["rl_ready"], 1)
                    if t in ACT_TILES:
                        return
                    dve.wait_ge(S["rl_ready"], i + 1)
                    v.tensor_scalar(P[:, par, t, 0:w], P[:, par, t, 0:w], rl[:, s], None, ALU.mult) \
                        .then_inc(S["pn_dve"], 1)

                def p_low(h, j):
                    w0 = max(0, j - TPC * c) * 128
                    dve.wait_ge(S["pth_ready"], jn(h, j) + 1)
                    v.tensor_tensor(PL[:, j % RING, w0:CH], ps[:, TURN_BANKS[c][j % RING], w0:CH],
                                    PH[:, j % RING, w0:CH], ALU.subtract).then_inc(S["ptl_ready"], 1)

                def context_low(h, par):
                    i = n * 16 + h
                    dve.wait_ge(S["cth_ready"], i + 1)
                    at = (lambda q: q[:, h, :]) if isinstance(h, int) else \
                        (lambda q: q[:, bass.ds(h, 1), :].rearrange("p a n -> p (a n)"))
                    v.tensor_tensor(at(QTL), ps[:, 6 + par, :], at(QTH), ALU.subtract) \
                        .then_inc(S["ctl_ready"], 1)

                def step(h, par, first=False):
                    normalise(h - 1, 1 - par, TPC - 1)
                    for t in range(TPC):
                        row_max(h, par, t)
                        if t:
                            normalise(h, par, t - 1)
                        if t == LAG - 1 and not first:
                            context_low(h - 2, par)
                        for j in slice_of(t):
                            p_low(h - 1, j)

                for t in range(TPC):
                    row_max(0, 0, t)
                    if t:
                        normalise(0, 0, t - 1)
                step(1, 1, first=True)
                with dve.Fori(1, H // 2) as hp:
                    step(hp * 2, 0)
                    step(hp * 2 + 1, 1)
                normalise(H - 1, 1, TPC - 1)
                context_low(H - 2, 0)
                for j in range(NJ):
                    p_low(H - 1, j)
                context_low(H - 1, 1)

            layer0(0, None)
            for n in range(B * NC):
                layer1(n)
                if n + 1 < B * NC:
                    layer0(n + 1, n)
            for t in range(TPC):
                add_output(B * NC - 1, t)

        @block.tensor
        def _(pe):
            mm = nc.tensor.matmul

            pe.wait_ge(ld["const"], 16)
            pe.wait_ge(prep_dve, 2)
            mm(ps[0:64, 7, 0:1], blk[0:64, :], bsm[:, 1:2], start=True, stop=True).then_inc(prep_mm, 1)
            waited = {"wq": ("wq", 48), "g": ("wv", 32), "gu": ("gu", 32), "wd": ("wd", 32)}
            for i, (kind, j) in enumerate(BANKS):
                name, value = waited[kind]
                pe.wait_ge(ld[name], value)
                if i == 3:
                    pe.wait_ge(prep_dve, 6)
                if i >= 4:
                    pe.wait_ge(prep_lo, 2 * (i - 4) + 2)
                dst = ps[:, bank_of(i), :]
                if kind == "wq":
                    k, hh = j // 2, j % 2
                    for a in range(8):
                        h = 8 * hh + a
                        last = mm(dst[:, 64 * a:64 * a + 64], r_wqT[:, h, 128 * k:128 * k + 128], r_wkT[:, h, :],
                                  start=True, stop=True)
                elif kind == "g":
                    for a in range(2):
                        h = 2 * j + a
                        for r in range(2):
                            last = mm(ps[64 * r:64 * r + 64, bank_of(i), a * D:a * D + D], r_wvT[:, h, :],
                                      r_wo[:, h, :], start=True, stop=True)
                elif kind == "gu":
                    k, g = j // 2, j % 2
                    sa = r_lora[32 * g:32 * g + RANK, 128 * k:128 * k + 128]
                    for n0, n1 in ((0, 512), (512, DFF)):
                        last = mm(ps[:, bank_of(i) + n0 // 512, 0:n1 - n0], sa,
                                  r_lora[32 * g:32 * g + RANK, D + n0:D + n1], start=True, stop=True)
                else:
                    for a in range(2):
                        m0, w = FM[2 * j + a]
                        last = mm(dst[0:w, a * D:a * D + D], r_lora[64:64 + RANK, m0:m0 + w],
                                  r_lora[64:64 + RANK, DFF:DFF + D], start=True, stop=True)
                last.then_inc(prep_mm, 1)
            pe.wait_ge(prep_done, 1)
            pe.wait_ge(ld["l0"], 64)
            pe.wait_ge(ld["kva"], 64)

            def split3(ps_out, pairs, start=True, stop=True):
                for i, ((lh, ll), (rh, rl_)) in enumerate(pairs):
                    mm(ps_out, lh, rh, start=start and i == 0, stop=False)
                    mm(ps_out, lh, rl_, start=False, stop=False)
                    last = mm(ps_out, ll, rh, start=False, stop=stop and i == len(pairs) - 1)
                return last

            def transposes(i):
                pe.wait_ge(S["xn_ready"], i + 1)
                for k in range(KD):
                    for t in range(TPC):
                        last = nc.tensor.transpose(ps[:, 6 + k, t * 128:t * 128 + 128],
                                                   xn[:, t, k * 128:k * 128 + 128], ident)
                last.then_inc(S["xT_ready"], 1)

            def output_half(n, i):
                t, half = i // 2, i % 2
                tok = slice(t * 128, t * 128 + 128)
                if i == 0:
                    pe.wait_ge(S["ctl_ready"], (n + 1) * H)
                if half == 0 and t >= 2:
                    pe.wait_ge(S["out_added"], n * TPC + t - 1)
                last = split3(ps[:, t % 2, 0:D], [((QTH[:, h, tok], QTL[:, h, tok]), (GH[:, h, :], GL[:, h, :]))
                                                  for h in range(half * H // 2, (half + 1) * H // 2)],
                              start=half == 0, stop=half == 1)
                if half:
                    last.then_inc(S["o_ready"], 1)

            def layer0(n, prev):
                def output(*halves):
                    if prev is not None:
                        for i in halves:
                            output_half(prev, i)

                output(0, 1)
                transposes(2 * n)
                output(2)
                pe.wait_ge(S["xnT_ready"], 2 * n + 1)
                pe.wait_ge(S["xq8_ready"], n + 1)
                for g in range(KD):
                    for k in range(KD):
                        last = mm(ps[:, 6 + g, :], wq0[:, k, g * 128:g * 128 + 128], xnT[:, k, :],
                                  start=k == 0, stop=k == KD - 1)
                last.then_inc(S["q_ready"], 1)

                def ffn0(q):
                    i = n * 4 + q
                    if q >= 1:
                        pe.wait_ge(S["up_copied"], i)
                    for g in range(2):
                        for a in range(2):
                            h = 2 * q + a
                            for k in range(KD):
                                last = mm(ps[:, 2 + 2 * g + a, :], wg8[:, k, g, h * 128:h * 128 + 128],
                                          xq8[:, k, :], start=k == 0, stop=k == KD - 1)
                    last.then_inc(S["gu_ready"], 1)

                ffn0(0)
                output(3)
                pe.wait_ge(S["sig_ready"], n + 1)
                for k in range(KD):
                    last = mm(ps[0:64, 6, :], mnorm[:, k, :], sig[:, k], start=k == 0, stop=k == KD - 1)
                last.then_inc(S["norm_ready"], 1)
                ffn0(1)
                ffn0(2)
                output(4)
                ffn0(3)

                def spread(j):
                    if j >= 4:
                        pe.wait_ge(S["sn_ready"], n * 8 + j - 3)
                    mm(ps[:, 2 + j % 4, :], selb[:, j, :], rsplit[:, :], start=True, stop=True) \
                        .then_inc(S["rbc_ready"], 1)

                def combine(j):
                    g, bank = j // 4, j % 4
                    pe.wait_ge(S["sn_ready"], n * 8 + j + 1)
                    mm(ps[:, 6 + g, :], mem[:, j, :], sn[:, j % 2], start=bank == 0, stop=bank == 3) \
                        .then_inc(S["comb_done"], 1)

                pe.wait_ge(S["r_ready"], n + 1)
                pe.wait_ge(S["up_copied"], n * 4 + 4)
                for j in range(4):
                    spread(j)
                for j in range(8):
                    combine(j)
                    if j + 4 < 8:
                        spread(j + 4)
                pe.wait_ge(S["act8_ready"], n * 4 + 4)
                for t in range(TPC):
                    for k in range(8):
                        last = mm(token_major(2, t), act8[:, k, t * 128:t * 128 + 128], wl8[:, k, :],
                                  start=k == 0, stop=k == 7)
                last.then_inc(S["y0_ready"], 1)
                pe.wait_ge(S["combT_ready"], n + 1)
                for t in range(TPC):
                    for k in range(KD):
                        last = mm(token_major(4, t), combT[:, k, t * 128:t * 128 + 128], wo0[:, k, :],
                                  start=k == 0, stop=k == KD - 1)
                last.then_inc(S["y1_ready"], 1)
                output(5, 6, 7)

            def layer1(n):
                b, c = n // NC, n % NC
                transposes(2 * n + 1)
                pe.wait_ge(S["xnT_ready"], 2 * n + 2)
                if n:
                    pe.wait_ge(S["out_added"], n * TPC)
                for t in range(TPC):
                    for k in range(KD):
                        last = mm(token_major(0, t)[:, 0:136], xnT[:, k, t * 128:t * 128 + 128], ra[:, k, :],
                                  start=k == 0, stop=k == KD - 1)
                last.then_inc(S["ra_ready"], 1)
                pe.wait_ge(S["xsplit_ready"], n + 1)
                for t in range(TPC):
                    tok = slice(t * 128, t * 128 + 128)
                    last = split3(ps[:, 6, tok], [((XH[:, k, tok], XL[:, k, tok]), (KVH[:, k, :], KVL[:, k, :]))
                                                  for k in range(KD)])
                last.then_inc(S["kvc_ready"], 1)

                def gate_up(m):
                    m0, w = FM[m]
                    if m >= 2:
                        pe.wait_ge(S["hf_ready"], n * NM + m - 1)
                    for g in range(2):
                        split3(ps[0:w, 2 + 2 * (m % 2) + g, :],
                               [((GUH[:, k, g, m0:m0 + w], GUL[:, k, g, m0:m0 + w]), (XH[:, k, :], XL[:, k, :]))
                                for k in range(KD)], stop=False)

                def gate_up_experts(m):
                    m0, w = FM[m]
                    for g in range(2):
                        r = slice(64 * g, 64 * g + 64)
                        last = split3(ps[0:w, 2 + 2 * (m % 2) + g, :],
                                      [((BGH[r, m0:m0 + w], BGL[r, m0:m0 + w]), (ZH[r, :], ZL[r, :]))], start=False)
                    last.then_inc(S["m_ready"], 1)

                gate_up(0)
                gate_up(1)
                pe.wait_ge(S["xaw_ready"], n + 1)
                for t in range(TPC):
                    last = nc.tensor.transpose(ps[:, 1, t * 128:t * 128 + 128], xaw[:, t, :], ident)
                last.then_inc(S["xawT_ready"], 1)
                pe.wait_ge(S["zl_ready"], n + 1)
                gate_up_experts(0)
                gate_up_experts(1)
                pe.wait_ge(S["ktok_ready"], n + 1)
                for t in range(TPC):
                    last = nc.tensor.transpose(ps[:, 7, t * 128:t * 128 + 128], ktok[:, t, :], ident)
                last.then_inc(S["kT_ready"], 1)
                for m in range(2, NM):
                    gate_up(m)
                    gate_up_experts(m)
                pe.wait_ge(S["hs_ready"], n * NM + NM)
                for t in range(TPC):
                    tok = slice(t * 128, t * 128 + 128)
                    last = split3(ps[:, 1, t * 64:t * 64 + 64],
                                  [((HH[0:w, m, tok], HL[0:w, m, tok]), (ADH[0:w, m, :], ADL[0:w, m, :]))
                                   for m, (_, w) in enumerate(FM)])
                last.then_inc(S["z_ready"], 1)
                pe.wait_ge(S["zw_ready"], n + 1)
                for t in range(TPC):
                    last = nc.tensor.transpose(ps[0:64, 0, t * 128:t * 128 + 128], zw[:, t, :], ident)
                last.then_inc(S["z2T_ready"], 1)
                pe.wait_ge(S["ktl_ready"], n + 1)
                for t in range(TPC):
                    tok = slice(t * 128, t * 128 + 128)
                    split3(token_major(6, t),
                           [((HH[0:w, m, tok], HL[0:w, m, tok]), (WDH[0:w, m, :], WDL[0:w, m, :]))
                            for m, (_, w) in enumerate(FM)], stop=False)
                    if t == 0:
                        pe.wait_ge(S["z2l_ready"], n + 1)
                    last = split3(token_major(6, t),
                                  [((Z2H[0:64, tok], Z2L[0:64, tok]), (BDH[:, :], BDL[:, :]))], start=False)
                last.then_inc(S["y2_ready"], 1)

                def project(i):
                    u, t, q = n * 16 + i, i // 4, i % 4
                    tok = slice(t * 128, t * 128 + 128)
                    if i >= 2:
                        pe.wait_ge(S["qn_ready"], u - 1)
                        pe.wait_ge(S["qr_ready"], u - 1)
                    split3(ps[:, i % 2, :],
                           [((XH[:, k, tok], XL[:, k, tok]),
                             (WQH[:, k, 4 * q:4 * q + 4, :].rearrange("p h c -> p (h c)"),
                              WQL[:, k, 4 * q:4 * q + 4, :].rearrange("p h c -> p (h c)")))
                            for k in range(KD)]).then_inc(S["qp_ready"], 1)

                def turn(i):
                    u, p = n * 16 + i, i % 2
                    pe.wait_ge(S["qn_ready"], u + 1)
                    pe.wait_ge(S["qr_ready"], u + 1)
                    if i >= 2:
                        pe.wait_ge(S["qtl_ready"], u - 1)
                    for a in range(4):
                        last = nc.tensor.transpose(ps[:, 2 + p, a * 128:a * 128 + 128], qtok[:, p, a, :], ident)
                    last.then_inc(S["qt_ready"], 1)

                for i in range(17):
                    if i < 16:
                        project(i)
                    if i >= 1:
                        turn(i - 1)
                pe.wait_ge(S["qtl_ready"], n * 16 + 16)

                NJ = TPC * (c + 1)

                def slice_of(t):
                    return range((c + 1) * t, (c + 1) * (t + 1))

                RING, LAG = RINGS[c], LAGS[c]

                def jn(h, j):
                    return b * (16 * 12) + c * 64 + h * NJ + j

                def query(q, h, t):
                    if isinstance(h, int):
                        return q[:, h, t * 128:t * 128 + 128]
                    return q[:, bass.ds(h, 1), t * 128:t * 128 + 128].rearrange("p a n -> p (a n)")

                def scores(h, t):
                    i = ((b * NC + c) * 16 + h) * 4 + t
                    if not (isinstance(h, int) and h == 0 and t < 2):
                        pe.wait_ge(S["exp_done"], i - 1)
                    w = (TPC * c + t + 1) * 128
                    parts = [(0, min(w, 512))] + ([(512, w)] if w > 512 else [])
                    qh, ql = query(QTH, h, t), query(QTL, h, t)
                    for lhs, rhs, kind in ((qh, KTH, 0), (qh, KTL, 1), (ql, KTH, 2)):
                        for a, z in parts:
                            mm(ps[:, 2 * (t % 2) + a // 512, 0:z - a], lhs, rhs[:, a:z],
                               start=kind == 0, stop=kind == 2 and z < w)
                    d = (w - 128) % 512
                    mm(ps[:, 2 * (t % 2) + (w - 128) // 512, d:d + 128], identb[:, :], maskb[:, :],
                       start=False, stop=True).then_inc(S["s_ready"], 1)

                def turn_p(h, par, j):
                    t0 = max(0, j - TPC * c)
                    if j == 0:
                        pe.wait_ge(S["pn_act"], (n * 16 + h + 1) * len(ACT_TILES))
                        pe.wait_ge(S["pn_dve"], (n * 16 + h + 1) * (TPC - len(ACT_TILES)))
                    if not (isinstance(h, int) and h == 0 and j < RING):
                        pe.wait_ge(S["ptl_ready"], jn(h, j) - RING + 1)
                    for t in range(t0, TPC):
                        last = nc.tensor.transpose(ps[:, TURN_BANKS[c][j % RING], t * 128:t * 128 + 128],
                                                   P[:, par, t, j * 128:j * 128 + 128], ident)
                    last.then_inc(S["pt_ready"], 1)

                def values(h, par, j):
                    w0 = max(0, j - TPC * c) * 128
                    if j == 0 and not (isinstance(h, int) and h < 2):
                        pe.wait_ge(S["ctl_ready"], n * 16 + h - 1)
                    pe.wait_ge(S["ptl_ready"], jn(h, j) + 1)
                    mm(ps[:, 6 + par, w0:CH], LAT[:, j, :], PH[:, j % RING, w0:CH], start=j == 0, stop=False)
                    mm(ps[:, 6 + par, w0:CH], LAT[:, j, :], PL[:, j % RING, w0:CH], start=False, stop=j == NJ - 1) \
                        .then_inc(S["pv_done"], 1)

                def step(h, par, first=False):
                    for t in range(TPC):
                        scores(h, t)
                        if t >= LAG:
                            for j in slice_of(t - LAG):
                                values(h - 1, 1 - par, j)
                        elif not first:
                            for j in slice_of(TPC + t - LAG):
                                values(h - 2, par, j)
                        for j in slice_of(t):
                            turn_p(h - 1, 1 - par, j)

                for t in range(TPC):
                    scores(0, t)
                step(1, 1, first=True)
                with pe.Fori(1, H // 2) as hp:
                    step(hp * 2, 0)
                    step(hp * 2 + 1, 1)
                for t in range(TPC - LAG, TPC):
                    for j in slice_of(t):
                        values(H - 2, 0, j)
                for j in range(NJ):
                    turn_p(H - 1, 1, j)
                    if j:
                        values(H - 1, 1, j - 1)
                values(H - 1, 1, NJ - 1)

            layer0(0, None)
            for n in range(B * NC):
                layer1(n)
                if n + 1 < B * NC:
                    layer0(n + 1, n)
            for i in range(2 * TPC):
                output_half(B * NC - 1, i)


def _constants(np):
    k = np.zeros((128, C_END), np.float32)
    k[:, C_ID:C_ID + 128] = np.eye(128, dtype=np.float32)
    q, key = np.arange(128)[:, None], np.arange(128)[None, :]
    k[:, C_MASK:C_MASK + 128] = np.where(key > q, np.float32(MASKED), np.float32(0))
    sel = np.zeros((64, KD, NB, 128), np.float32)
    for g in range(KD):
        for n in range(NB):
            for h in range(8):
                sel[n * H0 + g * 8 + h, g, n, h * D0:(h + 1) * D0] = 1
    k[:, C_SEL:C_TRI] = np.tile(sel.reshape(64, -1), (2, 1))
    e = np.arange(E)
    k[:, C_TRI:C_BLK] = (e[None, :] < e[:, None]).astype(np.float32).reshape(1, 64)
    r = np.arange(64) // H0
    k[0:64, C_BLK:C_COS] = (r[:, None] == r[None, :]).astype(np.float32)
    inv = (np.float32(1) / np.float32(10000.0) ** (np.arange(0, ROPE, 2, dtype=np.float32) / np.float32(ROPE)))
    f = np.outer(np.arange(T, dtype=np.float32), inv.astype(np.float32)).astype(np.float32)
    cos = np.cos(f.astype(np.float64)).astype(np.float32)
    sin = np.sin(f.astype(np.float64)).astype(np.float32)
    cos = np.concatenate([cos, cos], 1).reshape(T // 128, 128, ROPE).transpose(1, 0, 2)
    sin = np.concatenate([-sin, sin], 1).reshape(T // 128, 128, ROPE).transpose(1, 0, 2)
    k[:, C_COS:C_SIN] = cos.reshape(128, -1)
    k[:, C_SIN:C_END] = sin.reshape(128, -1)
    return k


def kernel(**inputs):
    import numpy as np
    import concourse.bacc as bacc
    from concourse.bass_utils import run_bass_kernel_spmd

    i = {n: np.asarray(a) for n, a in inputs.items()}
    mems, norms = i["L0_attn_memories"], i["L0_attn_memory_norms"]
    mem = np.zeros((128, KD, NB, 128), np.float32)
    mnorm = np.zeros((128, KD, NB, H0), np.float32)
    for g in range(KD):
        for n in range(NB):
            for h in range(8):
                r = slice(h * D0, (h + 1) * D0)
                mem[r, g, n, r] = mems[n, g * 8 + h]
                mnorm[r, g, n, g * 8 + h] = norms[n, g * 8 + h]
    bank = i["L0_attn_bank_weights"]
    wq = i["L1_attn_wq"].reshape(D, H, NOPE + ROPE)
    wkv = i["L1_attn_wkv_b"].reshape(KVR, H, NOPE + VD)
    a_gate = i["L1_ffn_A_gate"].transpose(1, 0, 2).reshape(D, E * RANK)
    a_up = i["L1_ffn_A_up"].transpose(1, 0, 2).reshape(D, E * RANK)
    lora = np.zeros((72, DFF + D), np.float32)
    for g, (a, bm) in enumerate((("sA_gate", "sB_gate"), ("sA_up", "sB_up"), ("sA_down", "sB_down"))):
        a, bm = i["L1_ffn_" + a].T, i["L1_ffn_" + bm]
        lora[32 * g:32 * g + RANK, 0:a.shape[1]] = a
        lora[32 * g:32 * g + RANK, a.shape[1]:] = bm
    arrays = {
        "x": i["L0_attn_hidden_states"],
        "const": _constants(np),
        "wq0": i["L0_attn_Wq"].T,
        "wo0": i["L0_attn_Wo"].T,
        "mem": mem.reshape(128, 8, 128),
        "mnorm": mnorm.reshape(128, KD, 64),
        "mrow": norms.reshape(64, D0),
        "bw": np.tile(bank, (NB, 1)),
        "bwself": bank.T.reshape(64, 1),
        "wg": i["L0_ffn_w_gating"].transpose(1, 0, 2),
        "wl": i["L0_ffn_w_linear"],
        "wqT": wq[:, :, 0:NOPE].transpose(2, 1, 0),
        "wkT": wkv[:, :, 0:NOPE].transpose(2, 1, 0),
        "wqr": wq[:, :, NOPE:],
        "wvT": wkv[:, :, NOPE:].transpose(2, 1, 0),
        "wo": i["L1_attn_wo"],
        "wkva": i["L1_attn_wkv_a"],
        "kvw": i["L1_attn_kv_norm_w"],
        "ra": np.concatenate([i["L1_ffn_W_router"], a_gate, a_up], 1),
        "wgu": np.stack([i["L1_ffn_W_gate"], i["L1_ffn_W_up"]], 1),
        "wd": i["L1_ffn_W_down"],
        "lora": lora,
        "bgu": np.concatenate([i["L1_ffn_B_gate"].reshape(64, DFF), i["L1_ffn_B_up"].reshape(64, DFF)], 0),
        "ad": i["L1_ffn_A_down"].transpose(1, 0, 2).reshape(DFF, 64),
        "bd": i["L1_ffn_B_down"].reshape(64, D),
        "ebias": i["L1_ffn_expert_bias"],
    }
    nc = bacc.Bacc("TRN2", target_bir_lowering=False, num_devices=1)
    ins, args = {}, []
    for name, a in arrays.items():
        a = np.ascontiguousarray(a)
        ins[name + "_dram"] = a
        args.append(nc.dram_tensor(name + "_dram", a.shape, mybir.dt.from_np(a.dtype), kind="ExternalInput").ap())
    args.append(nc.dram_tensor("out_dram", (B, T, D), mybir.dt.float32, kind="ExternalOutput").ap())
    fused_two_layers(nc, *args)
    r = run_bass_kernel_spmd(nc, [ins], core_ids=[0])
    return r.results[0]["out_dram"]
```

```python
import concourse.bass as bass
from concourse import mybir
from contextlib import ExitStack

B, T, D = 2, 1024, 256
H0, D0, NB = 16, 16, 4
HID = 1024
H, NOPE, ROPE, VD, KVR = 16, 128, 64, 128, 64
E, RANK, DFF = 8, 8, 688
CH = 512
NC = T // CH
TPC = CH // 128
KD = D // 128
FM = [(m * 128, min(128, DFF - m * 128)) for m in range((DFF + 127) // 128)]
NM = len(FM)
SCALE = (NOPE + ROPE) ** -0.5
LN_EPS, MEM_EPS, RMS_EPS = 1e-5, 1e-6, 1e-6
MASKED = -1e30
RING = 4
LAG = 3
ROWS_SLOT = (1, 5)
GELU_C, GELU_S = 0.044677734375, 0.796875

C_ID, C_MASK, C_SEL = 0, 128, 256
C_TRI = C_SEL + 8 * 128
C_BLK = C_TRI + 64
C_COS = C_BLK + 64
C_SIN = C_COS + 8 * 64
C_END = C_SIN + 8 * 64



def fused_two_layers(nc, x_in, const_in, wq0_in, wo0_in, mem_in, mnorm_in, mrow_in, bw_in, bwself_in,
                     wg_in, wl_in, wqT_in, wkT_in, wqr_in, wvT_in, wo_in, wkva_in, kvw_in,
                     ra_in, wgu_in, wd_in, lora_in, bgu_in, ad_in, bd_in, ebias_in, out):
    fp32, bf16, fp8 = mybir.dt.float32, mybir.dt.bfloat16, mybir.dt.float8e4
    ALU, ACT, AX = mybir.AluOpType, mybir.ActivationFunctionType, mybir.AxisListType

    ctx = ExitStack()
    with ctx:
        def sb(name, shape, dt=fp32):
            return ctx.enter_context(nc.sbuf_tensor(name, shape, dt))

        def sem(name):
            return ctx.enter_context(nc.semaphore(name))

        xg = sb("xg", [128, NC, TPC, D])
        const = sb("const", [128, C_END])
        ident = const[:, C_ID:C_ID + 128]
        sel = const[:, C_SEL:C_TRI].rearrange("p (j c) -> p j c", j=8)
        tri = const[:, C_TRI:C_BLK].rearrange("p (e f) -> p e f", e=E)
        blk = const[:, C_BLK:C_COS]
        cos = const[:, C_COS:C_SIN].rearrange("p (t r) -> p t r", t=8)
        sin = const[:, C_SIN:C_END].rearrange("p (t r) -> p t r", t=8)
        identb = sb("identb", [128, 128], bf16)
        maskb = sb("maskb", [128, 128], bf16)
        selb = sb("selb", [128, 8, 128], bf16)
        wq0 = sb("wq0", [128, KD, D])
        wo0 = sb("wo0", [128, KD, D])
        mem = sb("mem", [128, 8, 128])
        mnorm = sb("mnorm", [128, KD, 64])
        mrow = sb("mrow", [64, D0])
        bw = sb("bw", [64, NB])
        bwself = sb("bwself", [64, 1])
        bankw = sb("bankw", [128, 1])
        bsm = sb("bsm", [64, 16])
        wg8 = sb("wg8", [128, KD, 2, HID], fp8)
        wl8 = sb("wl8", [128, HID // 128, D], fp8)
        WQH = sb("WQH", [128, KD, H, 128], bf16)
        WQL = sb("WQL", [128, KD, H, 128], bf16)
        GH = sb("GH", [128, H // 2, D], bf16)
        GL = sb("GL", [128, H // 2, D], bf16)
        KVH = sb("KVH", [128, KD, 128], bf16)
        KVL = sb("KVL", [128, KD, 128], bf16)
        kvw = sb("kvw", [128, KVR])
        ra = sb("ra", [128, KD, 136])
        GUH = sb("GUH", [128, KD, 2, DFF], bf16)
        GUL = sb("GUL", [128, KD, 2, DFF], bf16)
        WDH = sb("WDH", [128, NM, D], bf16)
        WDL = sb("WDL", [128, NM, D], bf16)
        BGH = sb("BGH", [128, DFF], bf16)
        BGL = sb("BGL", [128, DFF], bf16)
        ADH = sb("ADH", [128, NM, 64], bf16)
        ADL = sb("ADL", [128, NM, 64], bf16)
        BDH = sb("BDH", [64, D], bf16)
        BDL = sb("BDL", [64, D], bf16)
        ebias = sb("ebias", [128, E])
        KTH = sb("KTH", [128, T], bf16)
        KTL = sb("KTL", [128, T], bf16)
        LAT = sb("LAT", [128, T // 128, 130], bf16)
        XH = sb("XH", [128, KD, CH], bf16)
        XL = sb("XL", [128, KD, CH], bf16)
        nhalf = sb("nhalf", [128, TPC])
        one = sb("one", [128, TPC])
        linv = sb("linv", [128, TPC])
        stats = sb("stats", [128, TPC, 6])
        mv = sb("mv", [128, TPC, 2])
        ve = sb("ve", [128, TPC])
        rstd = sb("rstd", [128, TPC])
        pm = sb("pm", [128, 2, 8])
        nm = sb("nm", [128, TPC])
        nms = sb("nms", [128, 2 * TPC], bf16)
        maxT = sb("maxT", [2 * TPC, 128], bf16)
        tilesel = sb("tilesel", [2 * TPC, TPC, 128], bf16)

        ARENA = 25700
        arena = sb("arena", [128, ARENA])

        class Cut:
            def __init__(self):
                self.at = 0

            def take(self, words, dt=fp32):
                a = arena[:, self.at:self.at + words]
                self.at += words
                assert self.at <= ARENA, self.at
                return a if dt == fp32 else a.bitcast(dt)

        cut = Cut()
        r_wg = cut.take(KD * 2 * HID).rearrange("p (k g d) -> p k g d", k=KD, g=2)
        r_wl = cut.take(8 * D).rearrange("p (k d) -> p k d", k=8)
        r_wkT = cut.take(H * 64).rearrange("p (h d) -> p h d", h=H)
        r_wqr = cut.take(KD * H * 64).rearrange("p (k h d) -> p k h d", k=KD, h=H)
        r_wvT = cut.take(H * 64).rearrange("p (h d) -> p h d", h=H)
        r_wo = cut.take(H * D).rearrange("p (h d) -> p h d", h=H)
        r_kva = cut.take(KD * 128).rearrange("p (k d) -> p k d", k=KD)
        r_gu = cut.take(KD * 2 * DFF).rearrange("p (k g d) -> p k g d", k=KD, g=2)
        r_wd = cut.take(NM * D).rearrange("p (m d) -> p m d", m=NM)
        r_lora = cut.take(DFF + D)
        r_bgu = cut.take(DFF)
        r_ad = cut.take(NM * 64).rearrange("p (m d) -> p m d", m=NM)
        r_bd = cut.take(D)
        r_wqT = cut.take(H * D).rearrange("p (h d) -> p h d", h=H)

        cut = Cut()
        QTH = cut.take(H * CH // 2, bf16).rearrange("p (h n) -> p h n", h=H)
        QTL = cut.take(H * CH // 2, bf16).rearrange("p (h n) -> p h n", h=H)
        P = cut.take(RING * CH).rearrange("p (b n) -> p b n", b=RING)
        qtok = cut.take(4 * 512).rearrange("p (b h c) -> p b h c", b=4, h=4)
        qr1 = cut.take(2 * 256).rearrange("p (b h c) -> p b h c", b=2, h=4)
        qr2 = cut.take(2 * 256).rearrange("p (b h c) -> p b h c", b=2, h=4)
        PH = cut.take(RING * CH // 2, bf16).rearrange("p (b n) -> p b n", b=RING)
        PL = cut.take(RING * CH // 2, bf16).rearrange("p (b n) -> p b n", b=RING)
        cv = cut.take(TPC * 130).rearrange("p (t c) -> p t c", t=TPC)
        csum = cut.take(TPC * KVR).rearrange("p (t c) -> p t c", t=TPC)
        ctok = cut.take(TPC * 128).rearrange("p (t c) -> p t c", t=TPC)

        cut = Cut()
        cut.at = H * CH
        ex = cut.take(KD * CH).rearrange("p (k n) -> p k n", k=KD)
        sig = cut.take(KD * CH).rearrange("p (k n) -> p k n", k=KD)
        sn = cut.take(4 * CH).rearrange("p (b n) -> p b n", b=4)
        rnorm = cut.take(CH // 2)
        rsplit = cut.take(CH // 2, bf16)
        gcp = cut.take(4 * CH, bf16).rearrange("p (b g n) -> p b g n", b=4, g=2)
        ucp = cut.take(4 * CH, bf16).rearrange("p (b g n) -> p b g n", b=4, g=2)
        inner = cut.take(2 * CH, bf16).rearrange("p (b g n) -> p b g n", b=2, g=2)
        tanhg = cut.take(2 * CH, bf16).rearrange("p (b g n) -> p b g n", b=2, g=2)
        act8 = cut.take(8 * CH // 4, fp8).rearrange("p (k n) -> p k n", k=8)
        combT = cut.take(KD * CH).rearrange("p (k n) -> p k n", k=KD)
        fb = cut.take(TPC * D // 2, bf16).rearrange("p (t d) -> p t d", t=TPC)
        xq8 = cut.take(KD * CH // 4, fp8).rearrange("p (k n) -> p k n", k=KD)
        l0_low = cut.at
        xn = cut.take(TPC * D).rearrange("p (t d) -> p t d", t=TPC)
        xnT = cut.take(KD * CH).rearrange("p (k n) -> p k n", k=KD)

        cut = Cut()
        th = cut.take(TPC * E).rearrange("p (t e) -> p t e", t=TPC)
        bi = cut.take(TPC * E).rearrange("p (t e) -> p t e", t=TPC)
        cmp1 = cut.take(TPC * 64).rearrange("p (t e f) -> p t e f", t=TPC, e=E)
        cmp2 = cut.take(TPC * 64).rearrange("p (t e f) -> p t e f", t=TPC, e=E)
        rank = cut.take(TPC * E).rearrange("p (t e) -> p t e", t=TPC)
        wex = cut.take(TPC * E).rearrange("p (t e) -> p t e", t=TPC)
        den = cut.take(TPC)
        xaw = cut.take(TPC * 128).rearrange("p (t c) -> p t c", t=TPC)
        ZH = cut.take(CH // 2, bf16)
        ZL = cut.take(CH // 2, bf16)
        kvs = cut.take(TPC * 128).rearrange("p (t c) -> p t c", t=TPC)
        ktok = cut.take(TPC * 128).rearrange("p (t c) -> p t c", t=TPC)
        ksq = cut.take(TPC * 64).rearrange("p (t c) -> p t c", t=TPC)
        kr1 = cut.take(TPC * 64).rearrange("p (t c) -> p t c", t=TPC)
        kr2 = cut.take(TPC * 64).rearrange("p (t c) -> p t c", t=TPC)
        kss = cut.take(TPC)
        knr = cut.take(TPC)
        tt = cut.take(2 * CH).rearrange("p (b n) -> p b n", b=2)
        a1 = cut.take(2 * CH).rearrange("p (b n) -> p b n", b=2)
        hf = cut.take(2 * CH).rearrange("p (b n) -> p b n", b=2)
        HH = cut.take(NM * CH // 2, bf16).rearrange("p (m n) -> p m n", m=NM)
        HL = cut.take(NM * CH // 2, bf16).rearrange("p (m n) -> p m n", m=NM)
        zw = cut.take(TPC * 64).rearrange("p (t c) -> p t c", t=TPC)
        Z2H = cut.take(CH // 2, bf16)
        Z2L = cut.take(CH // 2, bf16)
        assert cut.at <= l0_low

        ps = ctx.enter_context(nc.psum_tensor("ps", [128, 8, 512], fp32))

        def token_major(bank, t):
            return ps[:, bank + t // 2, (t % 2) * 256:(t % 2) * 256 + D]

        def token_major_all(bank):
            return ps[:, bank:bank + 2, :].rearrange("p b (t d) -> p (b t) d", t=2)

        loads = ["const", "small", "l0", "wg", "wl", "wq", "wqr", "wv", "kva", "gu", "wd", "tail"]
        ld = {n: sem("loaded_" + n) for n in loads}
        x_loaded = [sem(f"x_loaded{c}") for c in range(NC)]
        sums_ready = sem("sums_ready")
        prep_mm = sem("prep_mm")
        prep_hi = sem("prep_hi")
        prep_lo = sem("prep_lo")
        prep_dve = sem("prep_dve")
        prep_act = sem("prep_act")
        prep_sum = sem("prep_sum")
        prep_done = sem("prep_done")
        half_set = sem("half_set")
        link = sem("dve_link")
        names = """var_ready rstd_ready xn_ready xT_ready xnT_ready xq8_ready xsplit_ready q_ready e_ready sig_ready
        gu_ready gate_copied up_copied sq_ready inner_ready tanh_ready act8_ready norm_ready r_ready rbc_ready sn_ready comb_done
        combT_ready y0_ready y1_ready y1_added fb_ready ra_ready th_ready kvc_ready kvs_ready kss_ready knr_ready ktok_ready
        kT_ready kth_ready ktl_ready xaw_ready xawT_ready zh_ready zl_ready m_ready tt_ready hf_ready hh_ready hs_ready
        z_ready zw_ready z2T_ready z2h_ready z2l_ready y2_ready 
        qp_ready qn_ready qc_ready qr_ready qrope_parts qt_ready qth_ready qtl_ready
        rough_ready max_ready nm_ready nmh_ready nms_ready maxT_made maxT_ready st_ready ph_ready pl_ready pv_done
        cv_ready linv_ready csum_ready ctok_ready ct_ready cth_ready ctl_ready
        o_ready out_added""".split()
        S = {n: sem(n) for n in names}
        stored = sem("stored")

        block = ctx.enter_context(nc.Block())

        def output_bank(n, t):
            return (0, 1, 4, 5)[t] if n == B * NC - 1 else t % 2

        def query_step(i):
            return i // TPC, i % TPC

        def first_unit(i, units):
            return [i - 7] if 0 <= i - 7 < units else []

        def row(c):
            return slice(c * CH, (c + 1) * CH)

        @block.sync
        def _(sp):
            def load(dst, src, name):
                sp.dma_start(dst, src).then_inc(ld[name], 16)

            def x_rows(b, c):
                return x_in[b, row(c), :].rearrange("(t p) d -> p t d", p=128)

            def out_rows(b, c):
                return out[b, row(c), :].rearrange("(t p) d -> p t d", p=128)

            load(r_wvT, wvT_in, "wv")
            load(bw[:, :], bw_in, "small")
            load(r_wkT, wkT_in, "wq")
            load(const[:, :], const_in, "const")
            sp.dma_start(xg[:, 0], x_rows(0, 0)).then_inc(x_loaded[0], 16)
            load(r_kva, wkva_in.rearrange("(k p) n -> p k n", p=128), "kva")
            load(ebias[:, :], ebias_in.partition_broadcast(128), "kva")
            load(r_bgu, bgu_in, "tail")
            load(r_ad[0:FM[-1][1], NM - 1, :], ad_in[(NM - 1) * 128:DFF, :], "tail")
            load(r_gu.rearrange("p k g n -> p k (g n)"), wgu_in.rearrange("(k p) g n -> p k (g n)", p=128), "gu")
            load(r_wd[:, 0:NM - 1, :], wd_in[0:(NM - 1) * 128, :].rearrange("(m p) n -> p m n", p=128), "wd")
            load(wq0[:, :, :], wq0_in.rearrange("(k p) n -> p k n", p=128), "l0")
            load(mem[:, :, :], mem_in, "l0")
            load(r_wg.rearrange("p k g n -> p k (g n)"), wg_in.rearrange("(k p) g n -> p k (g n)", p=128), "wg")
            sp.dma_start(xg[:, 1], x_rows(0, 1)).then_inc(x_loaded[1], 16)
            for b in range(B):
                for c in range(NC):
                    sp.wait_ge(S["out_added"], (b * NC + c + 1) * TPC)
                    sp.dma_start(out_rows(b, c), xg[:, c]).then_inc(stored, 16)
                    if b + 1 < B:
                        sp.wait_ge(stored, 16 * (b * NC + c + 1))
                        sp.dma_start(xg[:, c], x_rows(b + 1, c)).then_inc(x_loaded[c], 16)
            sp.wait_ge(stored, 16 * B * NC)

        @block.gpsimd
        def _(pool):
            nc.gpsimd.memset(nhalf[:, :], -0.5)
            nc.gpsimd.memset(one[:, :], 1.0).then_inc(half_set, 1)
            pool.wait_ge(half_set, 1)

            def row_scales(n, l):
                for g in range(2):
                    ts = slice(2 * g, 2 * g + 2)
                    pool.wait_ge(S["var_ready"], (n * 2 + l) * 2 + g + 1)
                    nc.gpsimd.tensor_tensor(rstd[:, ts], ve[:, ts], nhalf[:, ts], ALU.pow) \
                        .then_inc(S["rstd_ready"], 1)

            row_scales(0, 0)
            for n in range(B * NC):
                row_scales(n, 1)
                pool.wait_ge(S["kss_ready"], n + 1)
                nc.gpsimd.tensor_tensor(knr, kss, nhalf[:, :], ALU.pow).then_inc(S["knr_ready"], 1)

                b, c = n // NC, n % NC
                for i in range(16):
                    u, (q, t) = n * 16 + i, query_step(i)
                    cs = cos[:, TPC * c + t, :].unsqueeze(1).broadcast_to([128, 4, 64])
                    if i >= 2:
                        pool.wait_ge(S["qr_ready"], u - 1)
                    pool.wait_ge(S["qn_ready"], u + 1)
                    nc.gpsimd.tensor_tensor(qr1[:, i % 2], qtok[:, i % 4, :, 64:128], cs, ALU.mult) \
                        .then_inc(S["qc_ready"], 1)

                NJ = TPC * (c + 1)

                def jn(h, j):
                    return b * (3 * TPC * H) + c * (TPC * H) + h * NJ + j

                def split_max(h, par):
                    i = n * H + h
                    if c:
                        pool.wait_ge(S["nm_ready"], b * H + h + 1)
                        m = nm[:, :]
                    else:
                        pool.wait_ge(S["max_ready"], jn(h, NJ - 1) + 1)
                        m = pm[:, par, 0:TPC]
                    if not (isinstance(h, int) and h == 0):
                        pool.wait_ge(S["maxT_made"], i)
                    nc.gpsimd.tensor_tensor(nms[:, 0:TPC], m, one[:, :], ALU.mult).then_inc(S["nmh_ready"], 1)
                    pool.wait_ge(S["nmh_ready"], i + 1)
                    nc.gpsimd.tensor_tensor(nms[:, TPC:2 * TPC], m, nms[:, 0:TPC], ALU.subtract) \
                        .then_inc(S["nms_ready"], 1)

                def context(h, par, g, pairs=None):
                    i = (n * H + h) * 2 + g
                    ts = slice(2 * g, 2 * g + 2)
                    pool.wait_ge(S["cv_ready"], i + 1)
                    nc.gpsimd.tensor_tensor(csum[:, ts], cv[:, ts, 0:64], cv[:, ts, 64:128], ALU.add) \
                        .then_inc(S["csum_ready"], 1)
                    if pairs is not None:
                        pool.wait_ge(S["ct_ready"], n * (H // 2) + pairs)
                    pool.wait_ge(S["linv_ready"], i + 1)
                    pool.wait_ge(S["csum_ready"], i + 1)
                    nc.gpsimd.tensor_tensor(ctok[:, ts, 64 * par:64 * par + 64], csum[:, ts],
                                            linv[:, ts].unsqueeze(2).broadcast_to([128, 2, 64]), ALU.mult) \
                        .then_inc(S["ctok_ready"], 1)

                def step(h, par, pairs=None):
                    context(h - 1, 1 - par, 0, pairs)
                    if c:
                        context(h - 1, 1 - par, 1)
                        split_max(h + 1, 1 - par)
                    else:
                        split_max(h + 1, 1 - par)
                        context(h - 1, 1 - par, 1)

                split_max(0, 0)
                if n + 1 < B * NC:
                    row_scales(n + 1, 0)
                split_max(1, 1)
                step(1, 1)
                with pool.Fori(1, H // 2 - 1) as hp:
                    step(hp * 2, 0)
                    step(hp * 2 + 1, 1, pairs=hp)
                step(H - 2, 0)
                for h, pairs in ((H - 2, H // 2 - 1), (H - 1, None)):
                    for g in range(2):
                        context(h, h % 2, g, pairs if g == 0 else None)

        BANKS = [("g", i) for i in range(H // 4)] + [("wq", i) for i in range(4)] \
            + [("gu", i) for i in range(4)] + [("wd", i) for i in range(NM // 2)]

        SUMS = H // 4 + 4

        def bank_of(i):
            return 2 * (i % 4)

        @block.scalar
        def _(act):
            def load(dst, src, name):
                act.dma_start(dst, src).then_inc(ld[name], 16)

            load(r_wo, wo_in.rearrange("(h p) n -> p h n", p=128), "wv")
            load(mrow[:, :], mrow_in, "small")
            load(bwself[:, :], bwself_in, "small")
            load(r_wqT, wqT_in, "wq")
            load(r_wqr.rearrange("p k h n -> p k (h n)"), wqr_in.rearrange("(k p) h n -> p k (h n)", p=128), "wqr")
            load(kvw[:, :], kvw_in.partition_broadcast(128), "kva")
            load(ra[:, :, :], ra_in.rearrange("(k p) n -> p k n", p=128), "kva")
            load(r_ad[:, 0:NM - 1, :], ad_in[0:(NM - 1) * 128, :].rearrange("(m p) n -> p m n", p=128), "tail")
            load(r_bd[0:64, :], bd_in, "tail")
            load(r_lora[0:72, :], lora_in, "gu")
            load(r_wd[0:FM[-1][1], NM - 1, :], wd_in[(NM - 1) * 128:DFF, :], "wd")
            load(wo0[:, :, :], wo0_in.rearrange("(k p) n -> p k n", p=128), "l0")
            load(mnorm[:, :, :], mnorm_in, "l0")
            load(r_wl, wl_in.rearrange("(k p) n -> p k n", p=128), "wl")

            for i, (kind, j) in enumerate(BANKS):
                src = ps[:, bank_of(i)]
                if i == H // 4:
                    act.wait_ge(prep_dve, 2)
                    nc.scalar.activation(bsm[:, 4:8], bw[:, :], ACT.Exp, bias=bsm[:, 0:1]).then_inc(prep_act, 1)
                    nc.scalar.activation(bsm[:, 8:9], bwself[:, :], ACT.Exp, bias=bsm[:, 0:1]).then_inc(prep_act, 1)
                if i == H // 4 + 2:
                    act.wait_ge(ld["wqr"], 16)
                    for k in range(KD):
                        nc.scalar.activation(WQH[:, k, :, 64:128], r_wqr[:, k], ACT.Copy, scale=SCALE) \
                            .then_inc(prep_act, 1)
                if kind == "wq":
                    act.wait_ge(prep_mm, i + 1)
                    k, hh = j // 2, j % 2
                    nc.scalar.activation(WQH[:, k, 8 * hh:8 * hh + 8, 0:64],
                                         src.rearrange("p (h d) -> p h d", h=8), ACT.Copy, scale=SCALE) \
                        .then_inc(prep_hi, 1)
                elif kind == "g":
                    act.wait_ge(prep_mm, i + 1)
                    nc.scalar.copy(GH[:, 2 * j:2 * j + 2, :], src.rearrange("p (h d) -> p h d", h=2)) \
                        .then_inc(prep_hi, 1)
                elif kind == "gu":
                    act.wait_ge(prep_sum, i + 1 - SUMS)
                    k, g = j // 2, j % 2
                    nc.scalar.copy(GUH[:, k, g, :], r_gu[:, k, g, :]).then_inc(prep_hi, 1)
                else:
                    act.wait_ge(prep_sum, i + 1 - SUMS)
                    if j < NM // 2 - 1:
                        nc.scalar.copy(WDH[:, 2 * j:2 * j + 2, :], r_wd[:, 2 * j:2 * j + 2, :]).then_inc(prep_hi, 1)
                    else:
                        w = FM[-1][1]
                        nc.scalar.copy(WDH[:, 2 * j, :], r_wd[:, 2 * j, :])
                        nc.scalar.copy(WDH[0:w, 2 * j + 1, :], r_wd[0:w, 2 * j + 1, :]).then_inc(prep_hi, 1)

            def layer0(n):
                act.wait_ge(S["xT_ready"], 2 * n + 1)
                nc.scalar.copy(xnT, ps[:, 6:8, :]).then_inc(S["xnT_ready"], 1)
                for g in range(KD):
                    act.wait_ge(S["q_ready"], KD * n + g + 1)
                    nc.scalar.activation(ex[:, g], ps[:, 6 + g, :], ACT.Exp).then_inc(S["e_ready"], 1)
                def copies(q):
                    i = n * 4 + q
                    act.wait_ge(S["gu_ready"], i + 1)
                    nc.scalar.copy(gcp[:, q], ps[:, 2:4, :]).then_inc(S["gate_copied"], 1)
                    nc.scalar.copy(ucp[:, q], ps[:, 4:6, :]).then_inc(S["up_copied"], 1)
                    act.wait_ge(S["gate_copied"], i + 1)
                    if q >= 2:
                        act.wait_ge(S["tanh_ready"], i - 1)
                    nc.scalar.activation(inner[:, q % 2], gcp[:, q], ACT.Square).then_inc(S["sq_ready"], 1)

                def tanh(q):
                    i = n * 4 + q
                    act.wait_ge(S["inner_ready"], i + 1)
                    if q >= 2:
                        act.wait_ge(S["act8_ready"], i - 1)
                    nc.scalar.activation(tanhg[:, q % 2], inner[:, q % 2], ACT.Tanh).then_inc(S["tanh_ready"], 1)

                copies(0)
                copies(1)
                tanh(0)
                tanh(1)
                copies(2)
                act.wait_ge(S["comb_done"], 8 * n + 8)
                nc.scalar.copy(combT, ps[:, 6:8, :]).then_inc(S["combT_ready"], 1)
                copies(3)
                tanh(2)
                tanh(3)
                for g in range(2):
                    act.wait_ge(S["y0_ready"], 2 * n + g + 1)
                    nc.scalar.copy(fb[:, 2 * g:2 * g + 2], ps[:, 6 + g, :].rearrange("p (t d) -> p t d", t=2)) \
                        .then_inc(S["fb_ready"], 1)

            def layer1(n):
                b, c = n // NC, n % NC
                act.wait_ge(S["xT_ready"], 2 * n + 2)
                nc.scalar.copy(xnT, ps[:, 6:8, :]).then_inc(S["xnT_ready"], 1)
                act.wait_ge(S["ra_ready"], n + 1)
                nc.scalar.activation(th, token_major_all(0)[:, :, 0:E], ACT.Tanh, scale=0.5) \
                    .then_inc(S["th_ready"], 1)
                act.wait_ge(S["kvc_ready"], n + 1)
                nc.scalar.copy(kvs, ps[:, 6, :].rearrange("p (t c) -> p t c", t=TPC)).then_inc(S["kvs_ready"], 1)
                act.wait_ge(S["xawT_ready"], n + 1)
                nc.scalar.copy(ZH, ps[:, 1, :]).then_inc(S["zh_ready"], 1)

                def gate_tanh(m):
                    i, w = n * NM + m, FM[m][1]
                    act.wait_ge(S["m_ready"], i + 1)
                    if m >= 2:
                        act.wait_ge(S["hf_ready"], i - 1)
                    nc.scalar.activation(tt[0:w, m % 2], ps[0:w, 2 + 2 * (m % 2), :], ACT.Tanh, scale=0.5) \
                        .then_inc(S["tt_ready"], 1)

                def hidden_high(m):
                    w = FM[m][1]
                    act.wait_ge(S["hf_ready"], n * NM + m + 1)
                    nc.scalar.copy(HH[0:w, m], hf[0:w, m % 2]).then_inc(S["hh_ready"], 1)

                gate_tanh(0)
                gate_tanh(1)
                act.wait_ge(S["kT_ready"], n + 1)
                nc.scalar.copy(KTH[:, row(c)], ps[:, 7, :]).then_inc(S["kth_ready"], 1)
                hidden_high(0)
                hidden_high(1)
                for m in range(2, NM):
                    gate_tanh(m)
                    hidden_high(m)
                act.wait_ge(S["z2T_ready"], n + 1)
                nc.scalar.copy(Z2H[0:64, :], ps[0:64, 0, :]).then_inc(S["z2h_ready"], 1)

                def copy_queries(i):
                    u = n * 16 + i
                    act.wait_ge(S["qp_ready"], u + 1)
                    if i >= 4:
                        act.wait_ge(S["qt_ready"], u - 3)
                    nc.scalar.copy(qtok[:, i % 4], ps[:, i % 2, :].rearrange("p (h c) -> p h c", h=4)) \
                        .then_inc(S["qn_ready"], 1)

                def q_high(i):
                    u, (q, t) = n * 16 + i, query_step(i)
                    act.wait_ge(S["qt_ready"], u + 1)
                    nc.scalar.copy(QTH[:, 4 * q:4 * q + 4, t * 128:t * 128 + 128],
                                   ps[:, 2 + i % 2, :].rearrange("p (h c) -> p h c", h=4)) \
                        .then_inc(S["qth_ready"], 1)

                for i in range(18):
                    if i < 16:
                        copy_queries(i)
                    if i >= 2:
                        q_high(i - 2)

                NJ = TPC * (c + 1)

                def jn(h, j):
                    return b * (3 * TPC * H) + c * (TPC * H) + h * NJ + j

                def exps(h, j):
                    w0 = max(0, j - TPC * c) * 128
                    i, p = jn(h, j), j % RING
                    act.wait_ge(S["st_ready"], i + 1)
                    if not (isinstance(h, int) and h == 0 and j < RING):
                        act.wait_ge(S["pv_done"], i - RING + 1)
                    nc.scalar.activation(P[:, p, w0:CH], ps[:, 4 + j % 2, w0:CH], ACT.Exp)
                    nc.scalar.activation(PH[:, p, w0:CH], ps[:, 4 + j % 2, w0:CH], ACT.Exp) \
                        .then_inc(S["ph_ready"], 1)

                def copy_context(h, g):
                    act.wait_ge(S["pv_done"], jn(h, TPC * c + 2 * g + 1) + 1)
                    if not (isinstance(h, int) and h == 0):
                        act.wait_ge(S["ctok_ready"], (n * H + h - 1) * 2 + g + 1)
                    nc.scalar.copy(cv[:, 2 * g:2 * g + 2, 0:129],
                                   ps[:, 6 + g, :].rearrange("p (t c) -> p t c", t=2)[:, :, 0:129]) \
                        .then_inc(S["cv_ready"], 1)

                def context_high(pair):
                    act.wait_ge(S["ct_ready"], n * (H // 2) + pair + 1)
                    nc.scalar.copy(QTH[:, pair, :] if isinstance(pair, int) else
                                   QTH[:, bass.ds(pair, 1), :].rearrange("p a n -> p (a n)"),
                                   ps[:, 3, :]).then_inc(S["cth_ready"], 1)

                def step(h, pair=None, first=False):
                    for j in range(NJ):
                        if j in (0, 2) and not first:
                            copy_context(h - 1, j // 2)
                        if pair is not None and j == 1:
                            context_high(pair)
                        exps(h, j)

                step(0, first=True)
                step(1)
                with act.Fori(1, H // 2 - 1) as hp:
                    step(hp * 2)
                    step(hp * 2 + 1, pair=hp - 1)
                step(H - 2)
                step(H - 1, pair=H // 2 - 2)
                copy_context(H - 1, 0)
                copy_context(H - 1, 1)
                context_high(H // 2 - 1)

            layer0(0)
            for n in range(B * NC):
                layer1(n)
                if n + 1 < B * NC:
                    layer0(n + 1)

        @block.vector
        def _(dve):
            v = nc.vector
            count = [0]

            def own(ins):
                count[0] += 1
                ins.then_inc(prep_dve, 1)
                dve.wait_ge(prep_dve, count[0])

            k_link = [0]

            def linked(ins):
                k_link[0] += 1
                ins.then_inc(link, 1)
                dve.wait_ge(link, k_link[0])

            def row_stats(n, l, before=None):
                c = n % NC
                halves = [range(2 * g, 2 * g + 2) for g in range(2)]
                for g, ts in enumerate(halves):
                    if before:
                        before(g)
                    for t in ts:
                        ins = v.bn_stats(stats[:, t, :], xg[:, c, t, :])
                    if g:
                        linked(ins)
                for ts in halves:
                    for t in ts:
                        ins = v.bn_aggr(mv[:, t, :], stats[:, t, :])
                linked(ins)
                for g in range(2):
                    s = slice(2 * g, 2 * g + 2)
                    v.tensor_scalar(ve[:, s], mv[:, s, 1], LN_EPS, None, ALU.add).then_inc(S["var_ready"], 1)

            def normalise_rows(n, l):
                i, c = 2 * n + l, n % NC
                for g in range(2):
                    dve.wait_ge(S["rstd_ready"], 2 * i + g + 1)
                    for t in (2 * g, 2 * g + 1):
                        ins = v.tensor_scalar(xn[:, t, :], xg[:, c, t, :], mv[:, t, 0:1], rstd[:, t:t + 1],
                                              ALU.subtract, ALU.mult)
                    ins.then_inc(S["xn_ready"], 1)

            def add_adapter(i):
                kind, j = BANKS[i]
                dve.wait_ge(prep_mm, i + 1)
                if kind == "gu":
                    k, g = j // 2, j % 2
                    two = ps[:, bank_of(i):bank_of(i) + 2, :].rearrange("p b n -> p (b n)")[:, 0:DFF]
                    ins = v.scalar_tensor_tensor(r_gu[:, k, g, :], two, 1.0 / RANK, r_gu[:, k, g, :],
                                                 ALU.mult, ALU.add)
                else:
                    for a in range(2):
                        m = 2 * j + a
                        w = FM[m][1]
                        ins = v.scalar_tensor_tensor(r_wd[0:w, m, :], ps[0:w, bank_of(i), a * D:a * D + D],
                                                     1.0 / RANK, r_wd[0:w, m, :], ALU.mult, ALU.add)
                ins.then_inc(prep_sum, 1)

            for i, (kind, j) in enumerate(BANKS):
                src = ps[:, bank_of(i)]
                if i == H // 4:
                    dve.wait_ge(ld["small"], 48)
                    own(v.tensor_reduce(bsm[:, 0:1], bw[:, :], AX.X, ALU.max, negate=True))
                    own(v.tensor_reduce(bsm[:, 1:2], mrow[:, :], AX.X, ALU.add))
                    dve.wait_ge(prep_act, 2)
                    own(v.tensor_reduce(bsm[:, 2:3], bsm[:, 4:8], AX.X, ALU.add))
                    own(v.reciprocal(bsm[:, 3:4], bsm[:, 2:3]))
                    own(v.tensor_tensor(bsm[:, 9:10], bsm[:, 8:9], bsm[:, 3:4], ALU.mult))
                    dve.wait_ge(ld["const"], 16)
                    v.tensor_copy(identb[:, :], ident)
                    v.tensor_copy(maskb[:, :], const[:, C_MASK:C_MASK + 128])
                    v.tensor_copy(selb[:, :, :], sel)
                    v.tensor_tensor(tilesel[:, :, :], const[0:8, C_ID:C_ID + 4].unsqueeze(2).broadcast_to([8, TPC, 128]),
                                    const[0:8, C_ID + 4:C_ID + 8].unsqueeze(2).broadcast_to([8, TPC, 128]), ALU.add)
                    v.memset(LAT[:, :, 128:130], 1.0)
                    dve.wait_ge(x_loaded[0], 16)
                    row_stats(0, 0)
                    dve.wait_ge(sums_ready, 1)
                    own(v.tensor_scalar(bankw[0:64, :], ps[0:64, 7, 0:1], MEM_EPS, bsm[:, 9:10], ALU.is_ge, ALU.mult))
                    v.tensor_copy(bankw[64:128, :], bankw[0:64, :])
                if i == H // 4 + 2:
                    dve.wait_ge(prep_act, 4)
                    for k in range(KD):
                        v.scalar_tensor_tensor(WQL[:, k, :, 64:128], r_wqr[:, k], SCALE, WQH[:, k, :, 64:128],
                                               ALU.mult, ALU.subtract)
                if i == H // 4 + 4:
                    dve.wait_ge(ld["kva"], 64)
                    dve.wait_ge(ld["tail"], 64)
                    w = FM[-1][1]
                    v.tensor_copy(KVH[:, :, :], r_kva)
                    v.tensor_copy(BGH[:, :], r_bgu)
                    v.tensor_copy(ADH[:, 0:NM - 1, :], r_ad[:, 0:NM - 1, :])
                    v.tensor_copy(ADH[0:w, NM - 1, :], r_ad[0:w, NM - 1, :])
                    own(v.tensor_copy(BDH[:, :], r_bd[0:64, :]))
                    v.tensor_tensor(KVL[:, :, :], r_kva, KVH[:, :, :], ALU.subtract)
                    v.tensor_tensor(BGL[:, :], r_bgu, BGH[:, :], ALU.subtract)
                    v.tensor_tensor(ADL[:, 0:NM - 1, :], r_ad[:, 0:NM - 1, :], ADH[:, 0:NM - 1, :], ALU.subtract)
                    v.tensor_tensor(ADL[0:w, NM - 1, :], r_ad[0:w, NM - 1, :], ADH[0:w, NM - 1, :], ALU.subtract)
                    own(v.tensor_tensor(BDL[:, :], r_bd[0:64, :], BDH[:, :], ALU.subtract))
                if kind == "gu" and j == 0:
                    add_adapter(i)
                if kind in ("gu", "wd") and i + 1 < len(BANKS):
                    add_adapter(i + 1)
                if kind == "wq":
                    k, hh = j // 2, j % 2
                    dve.wait_ge(prep_hi, i + 1)
                    v.scalar_tensor_tensor(WQL[:, k, 8 * hh:8 * hh + 8, 0:64],
                                           src.rearrange("p (h d) -> p h d", h=8), SCALE,
                                           WQH[:, k, 8 * hh:8 * hh + 8, 0:64], ALU.mult, ALU.subtract) \
                        .then_inc(prep_lo, 1)
                elif kind == "g":
                    dve.wait_ge(prep_hi, i + 1)
                    v.tensor_tensor(GL[:, 2 * j:2 * j + 2, :], src.rearrange("p (h d) -> p h d", h=2),
                                    GH[:, 2 * j:2 * j + 2, :], ALU.subtract).then_inc(prep_lo, 1)
                elif kind == "gu":
                    k, g = j // 2, j % 2
                    dve.wait_ge(prep_hi, i + 1)
                    v.tensor_tensor(GUL[:, k, g, :], r_gu[:, k, g, :], GUH[:, k, g, :], ALU.subtract) \
                        .then_inc(prep_lo, 1)
                else:
                    dve.wait_ge(prep_hi, i + 1)
                    for m in (2 * j, 2 * j + 1):
                        w = FM[m][1]
                        ins = v.tensor_tensor(WDL[0:w, m, :], r_wd[0:w, m, :], WDH[0:w, m, :], ALU.subtract)
                    ins.then_inc(prep_lo, 1)
            v.memset(stats[:, :, :], 0.0).then_inc(prep_done, 1)
            dve.wait_ge(prep_done, 1)

            def add_output(n, t):
                dve.wait_ge(S["o_ready"], n * TPC + t + 1)
                v.tensor_tensor(xg[:, n % NC, t], xg[:, n % NC, t], ps[:, output_bank(n, t), 0:D],
                                ALU.add) \
                    .then_inc(S["out_added"], 1)

            def layer0(n, prev):
                def output(t):
                    if prev is not None:
                        add_output(prev, t)

                c = n % NC
                if prev is None:
                    normalise_rows(n, 0)
                    dve.wait_ge(ld["wg"], 16)
                    v.tensor_copy(wg8[:, :, :, :], r_wg, saturate=True)
                dve.wait_ge(S["xnT_ready"], 2 * n + 1)
                v.tensor_copy(xq8, xnT, saturate=True).then_inc(S["xq8_ready"], 1)
                if prev is None:
                    dve.wait_ge(ld["wl"], 16)
                    v.tensor_copy(wl8[:, :, :], r_wl, saturate=True)
                for g in range(KD):
                    dve.wait_ge(S["e_ready"], KD * n + g + 1)
                    linked(v.tensor_scalar(ex[:, g], ex[:, g], 1.0, None, ALU.min))
                    ins = v.scalar_tensor_tensor(sig[:, g], ps[:, 6 + g, :], 1.0, ex[:, g], ALU.add, ALU.max)
                ins.then_inc(S["sig_ready"], 1)

                def gelu_inner(q):
                    dve.wait_ge(S["sq_ready"], n * 4 + q + 1)
                    t = inner[:, q % 2]
                    linked(v.tensor_tensor(t, t, gcp[:, q], ALU.mult))
                    linked(v.tensor_scalar(t, t, GELU_C, None, ALU.mult))
                    linked(v.tensor_tensor(t, t, gcp[:, q], ALU.add))
                    v.tensor_scalar(t, t, GELU_S, None, ALU.mult).then_inc(S["inner_ready"], 1)

                def gelu_outer(*qs):

                    def step_of(ins):
                        k_link[0] += 1
                        ins.then_inc(link, 1)

                    for q in qs:
                        t = tanhg[:, q % 2]
                        dve.wait_ge(S["tanh_ready"], n * 4 + q + 1)
                        step_of(v.tensor_scalar(t, t, 1.0, 0.5, ALU.add, ALU.mult))
                    for factor in (gcp, ucp):
                        for q in qs:
                            t = tanhg[:, q % 2]
                            dve.wait_ge(link, k_link[0] - len(qs) + 1)
                            step_of(v.tensor_tensor(t, t, factor[:, q], ALU.mult))
                    for q in qs:
                        dve.wait_ge(link, k_link[0] - len(qs) + 1 + q - qs[0])
                        v.tensor_copy(act8[:, 2 * q:2 * q + 2], tanhg[:, q % 2], saturate=True) \
                            .then_inc(S["act8_ready"], 1)

                def weigh(j):
                    i = n * 8 + j
                    dve.wait_ge(S["rbc_ready"], i + 1)
                    if j >= 4:
                        dve.wait_ge(S["comb_done"], i - 3)
                    v.tensor_tensor(sn[:, j % 4], sig[:, j // 4], ps[:, 2 + j % 4, :], ALU.mult) \
                        .then_inc(S["sn_ready"], 1)

                gelu_inner(0)
                output(0)
                dve.wait_ge(S["norm_ready"], n + 1)
                linked(v.tensor_scalar(rnorm, ps[:, 6, 0:CH // 2], MEM_EPS, None, ALU.max))
                linked(v.reciprocal(rnorm, rnorm))
                linked(v.tensor_scalar(rnorm, rnorm, bankw[:, :], None, ALU.mult))
                for r in range(2):
                    ins = v.tensor_copy(rsplit[0:64, r * CH // 2:(r + 1) * CH // 2], rnorm[64 * r:64 * r + 64, :])
                linked(ins)
                for r in range(2):
                    tok = slice(r * CH // 2, (r + 1) * CH // 2)
                    ins = v.tensor_tensor(rsplit[64:128, tok], rnorm[64 * r:64 * r + 64, :], rsplit[0:64, tok],
                                          ALU.subtract)
                ins.then_inc(S["r_ready"], 1)
                output(1)
                for j in range(4):
                    weigh(j)
                gelu_inner(1)
                for j in range(4, 8):
                    weigh(j)
                gelu_outer(0, 1)
                gelu_inner(2)
                gelu_inner(3)
                dve.wait_ge(S["y1_ready"], n + 1)
                v.tensor_tensor(xg[:, c], xg[:, c], token_major_all(6), ALU.add).then_inc(S["y1_added"], 1)
                output(2)
                gelu_outer(2)
                gelu_outer(3)
                dve.wait_ge(S["y1_added"], n + 1)

                def add_feed_forward(g):
                    dve.wait_ge(S["fb_ready"], 2 * n + g + 1)
                    ts = slice(2 * g, 2 * g + 2)
                    linked(v.tensor_tensor(xg[:, c, ts], xg[:, c, ts], fb[:, ts], ALU.add))

                row_stats(n, 1, add_feed_forward)
                normalise_rows(n, 1)
                output(3)

            def layer1(n):
                b, c = n // NC, n % NC
                dve.wait_ge(S["xnT_ready"], 2 * n + 2)
                linked(v.tensor_copy(XH[:, :, :], xnT))
                v.tensor_tensor(XL[:, :, :], xnT, XH[:, :, :], ALU.subtract) \
                    .then_inc(S["xsplit_ready"], 1)
                dve.wait_ge(S["th_ready"], n + 1)
                linked(v.tensor_scalar(th, th, 1.0, 0.5, ALU.add, ALU.mult))
                linked(v.tensor_tensor(bi, th, ebias[:, :].unsqueeze(1).broadcast_to([128, TPC, E]), ALU.add))
                mine = bi.unsqueeze(3).broadcast_to([128, TPC, E, E])
                other = bi.unsqueeze(2).broadcast_to([128, TPC, E, E])
                v.tensor_tensor(cmp1, other, mine, ALU.is_gt)
                linked(v.tensor_tensor(cmp2, other, mine, ALU.is_equal))
                linked(v.tensor_tensor(cmp2, cmp2, tri.unsqueeze(1).broadcast_to([128, TPC, E, E]), ALU.mult))
                linked(v.tensor_tensor(cmp1, cmp1, cmp2, ALU.add))
                linked(v.tensor_reduce(rank, cmp1, AX.X, ALU.add))
                linked(v.scalar_tensor_tensor(wex, rank, 2.0, th, ALU.is_lt, ALU.mult))
                linked(v.tensor_reduce(den, wex, AX.X, ALU.add))
                linked(v.tensor_scalar(den, den, 1e-8, None, ALU.add))
                linked(v.reciprocal(den, den))
                linked(v.scalar_tensor_tensor(wex, wex, 1.0 / RANK,
                                              den.unsqueeze(2).broadcast_to([128, TPC, E]), ALU.mult, ALU.mult))
                by_rank = wex.unsqueeze(3).broadcast_to([128, TPC, E, RANK])
                for g in range(2):
                    a = token_major_all(0)[:, :, E + 64 * g:E + 64 * g + 64]
                    ins = v.tensor_tensor(xaw[:, :, 64 * g:64 * g + 64].rearrange("p t (e r) -> p t e r", e=E),
                                          a.rearrange("p t (e r) -> p t e r", e=E), by_rank, ALU.mult)
                ins.then_inc(S["xaw_ready"], 1)
                dve.wait_ge(S["kvs_ready"], n + 1)
                linked(v.tensor_tensor(ksq, kvs[:, :, 0:64], kvs[:, :, 0:64], ALU.mult))
                linked(v.tensor_reduce(kss, ksq, AX.X, ALU.add))
                v.tensor_scalar(kss, kss, 1.0 / KVR, RMS_EPS, ALU.mult, ALU.add).then_inc(S["kss_ready"], 1)
                cs, sn_t = cos[:, TPC * c:TPC * c + TPC, :], sin[:, TPC * c:TPC * c + TPC, :]
                v.tensor_tensor(kr1, kvs[:, :, 64:128], cs, ALU.mult)
                v.tensor_tensor(kr2[:, :, 0:32], kvs[:, :, 96:128], sn_t[:, :, 0:32], ALU.mult)
                linked(v.tensor_tensor(kr2[:, :, 32:64], kvs[:, :, 64:96], sn_t[:, :, 32:64], ALU.mult))
                v.tensor_tensor(ktok[:, :, 64:128], kr1, kr2, ALU.add)
                dve.wait_ge(S["zh_ready"], n + 1)
                v.tensor_tensor(ZL, ps[:, 1, :], ZH, ALU.subtract).then_inc(S["zl_ready"], 1)
                dve.wait_ge(S["knr_ready"], n + 1)
                linked(v.tensor_tensor(ktok[:, :, 0:64], kvs[:, :, 0:64],
                                       knr.unsqueeze(2).broadcast_to([128, TPC, 64]), ALU.mult))
                v.tensor_tensor(ktok[:, :, 0:64], ktok[:, :, 0:64],
                                kvw[:, :].unsqueeze(1).broadcast_to([128, TPC, 64]), ALU.mult) \
                    .then_inc(S["ktok_ready"], 1)
                dve.wait_ge(S["ktok_ready"], n + 1)

                def hidden(m):
                    i, p, w = n * NM + m, m % 2, FM[m][1]
                    dve.wait_ge(S["tt_ready"], i + 1)
                    linked(v.scalar_tensor_tensor(a1[0:w, p], tt[0:w, p], 1.0, ps[0:w, 2 + 2 * p, :],
                                                  ALU.add, ALU.mult))
                    v.scalar_tensor_tensor(hf[0:w, p], a1[0:w, p], 0.5, ps[0:w, 3 + 2 * p, :],
                                           ALU.mult, ALU.mult).then_inc(S["hf_ready"], 1)

                def hidden_low(m):
                    w = FM[m][1]
                    dve.wait_ge(S["hh_ready"], n * NM + m + 1)
                    v.tensor_tensor(HL[0:w, m], hf[0:w, m % 2], HH[0:w, m], ALU.subtract) \
                        .then_inc(S["hs_ready"], 1)

                hidden(0)
                hidden(1)
                lat = LAT[:, TPC * c:TPC * c + TPC, 0:128]
                linked(v.tensor_copy(lat[:, :, 0:64], ktok[:, :, 0:64]))
                linked(v.tensor_tensor(lat[:, :, 64:128], ktok[:, :, 0:64], lat[:, :, 0:64], ALU.subtract))
                dve.wait_ge(S["kth_ready"], n + 1)
                v.tensor_tensor(KTL[:, row(c)], ps[:, 7, :], KTH[:, row(c)], ALU.subtract) \
                    .then_inc(S["ktl_ready"], 1)
                hidden_low(0)
                hidden_low(1)
                for m in range(2, NM):
                    hidden(m)
                    hidden_low(m)
                dve.wait_ge(S["z_ready"], n + 1)
                v.tensor_tensor(zw.rearrange("p t (e r) -> p t e r", e=E),
                                ps[:, 1, 0:TPC * 64].rearrange("p (t e r) -> p t e r", t=TPC, e=E),
                                by_rank, ALU.mult).then_inc(S["zw_ready"], 1)
                dve.wait_ge(S["z2h_ready"], n + 1)
                v.tensor_tensor(Z2L[0:64, :], ps[0:64, 0, :], Z2H[0:64, :], ALU.subtract) \
                    .then_inc(S["z2l_ready"], 1)
                dve.wait_ge(S["y2_ready"], n + 1)
                linked(v.tensor_tensor(xg[:, c], xg[:, c], token_major_all(6), ALU.add))

                def rope_sin(i):
                    u, (q, t) = n * 16 + i, query_step(i)
                    src, p = qtok[:, i % 4], i % 2
                    sa = sin[:, TPC * c + t, 0:32].unsqueeze(1).broadcast_to([128, 4, 32])
                    sb_ = sin[:, TPC * c + t, 32:64].unsqueeze(1).broadcast_to([128, 4, 32])
                    dve.wait_ge(S["qn_ready"], u + 1)
                    if i >= 2:
                        dve.wait_ge(S["qr_ready"], u - 1)
                    v.tensor_tensor(qr2[:, p, :, 0:32], src[:, :, 96:128], sa, ALU.mult)
                    v.tensor_tensor(qr2[:, p, :, 32:64], src[:, :, 64:96], sb_, ALU.mult) \
                        .then_inc(S["qrope_parts"], 1)

                def rope_add(i):
                    u, p = n * 16 + i, i % 2
                    dve.wait_ge(S["qc_ready"], u + 1)
                    dve.wait_ge(S["qrope_parts"], u + 1)
                    v.tensor_tensor(qtok[:, i % 4, :, 64:128], qr1[:, p], qr2[:, p], ALU.add) \
                        .then_inc(S["qr_ready"], 1)

                def q_low(i):
                    u, (q, t) = n * 16 + i, query_step(i)
                    dve.wait_ge(S["qth_ready"], u + 1)
                    v.tensor_tensor(QTL[:, 4 * q:4 * q + 4, t * 128:t * 128 + 128],
                                    ps[:, 2 + i % 2, :].rearrange("p (h c) -> p h c", h=4),
                                    QTH[:, 4 * q:4 * q + 4, t * 128:t * 128 + 128], ALU.subtract) \
                        .then_inc(S["qtl_ready"], 1)

                NJ = TPC * (c + 1)

                def jn(h, j):
                    return b * (3 * TPC * H) + c * (TPC * H) + h * NJ + j

                def units(j):
                    return (0, 1) if j == 0 else (j + 1,) if j + 1 < NJ else ()

                def row_max(h, par, j):
                    w = (j // (c + 1) + 1) * 128 if j % (c + 1) == c else 512
                    dve.wait_ge(S["rough_ready"], jn(h, j) + 1)
                    bank = j % 2 + (4 if isinstance(h, int) and h == 0 else 0)
                    v.tensor_reduce(pm[:, par, j:j + 1], ps[:, bank, 0:w], AX.X, ALU.max, negate=True) \
                        .then_inc(S["max_ready"], 1)

                def join_max(h, par):
                    two = pm[:, par, :].rearrange("p (t a) -> p t a", a=2)
                    dve.wait_ge(S["max_ready"], jn(h, NJ - 1) + 1)
                    v.tensor_tensor(nm[:, :], two[:, :, 0], two[:, :, 1], ALU.min).then_inc(S["nm_ready"], 1)

                def copy_max(h):
                    dve.wait_ge(S["maxT_made"], n * H + h + 1)
                    v.tensor_copy(maxT[:, :], ps[0:2 * TPC, 2, 0:128]).then_inc(S["maxT_ready"], 1)

                def p_low(h, j):
                    w0 = max(0, j - TPC * c) * 128
                    p = j % RING
                    dve.wait_ge(S["ph_ready"], jn(h, j) + 1)
                    v.tensor_tensor(PL[:, p, w0:CH], P[:, p, w0:CH], PH[:, p, w0:CH], ALU.subtract) \
                        .then_inc(S["pl_ready"], 1)

                def invert(h, g):
                    dve.wait_ge(S["cv_ready"], (n * H + h) * 2 + g + 1)
                    v.reciprocal(linv[:, 2 * g:2 * g + 2], cv[:, 2 * g:2 * g + 2, 128]) \
                        .then_inc(S["linv_ready"], 1)

                def context_low(pair):
                    dve.wait_ge(S["cth_ready"], n * (H // 2) + pair + 1)
                    at = (lambda q: q[:, pair, :]) if isinstance(pair, int) else \
                        (lambda q: q[:, bass.ds(pair, 1), :].rearrange("p a n -> p (a n)"))
                    v.tensor_tensor(at(QTL), ps[:, 3, :], at(QTH), ALU.subtract).then_inc(S["ctl_ready"], 1)

                def step(h, par, pair=None, first=False, last=False):
                    for j in range(NJ):
                        if j == 0:
                            copy_max(h)
                        if not last:
                            for u in units(j):
                                row_max(h + 1, 1 - par, u)
                        if c and not last and j == NJ - 2:
                            join_max(h + 1, 1 - par)
                        if j in (1, 3) and not first:
                            invert(h - 1, j // 2)
                        if j >= 1:
                            p_low(h, j - 1)
                        elif not first:
                            p_low(h - 1, NJ - 1)
                        if pair is not None and j == 2:
                            context_low(pair)
                        if first and n + 1 < B * NC and j == 0:
                            dve.wait_ge(x_loaded[(n + 1) % NC], ((n + 1) // NC) * 16 + 16)
                            row_stats(n + 1, 0)
                        if last and n + 1 < B * NC and j == ROWS_SLOT[c]:
                            normalise_rows(n + 1, 0)

                for i in range(18):
                    if i < 16:
                        rope_sin(i)
                    if 1 <= i <= 16:
                        rope_add(i - 1)
                    if i >= 2:
                        q_low(i - 2)
                    for j in first_unit(i, NJ):
                        row_max(0, 0, j)
                if c:
                    join_max(0, 0)
                step(0, 0, first=True)
                step(1, 1)
                with dve.Fori(1, H // 2 - 1) as hp:
                    step(hp * 2, 0)
                    step(hp * 2 + 1, 1, pair=hp - 1)
                step(H - 2, 0)
                step(H - 1, 1, pair=H // 2 - 2, last=True)
                p_low(H - 1, NJ - 1)
                invert(H - 1, 0)
                invert(H - 1, 1)
                context_low(H // 2 - 1)

            layer0(0, None)
            for n in range(B * NC):
                layer1(n)
                if n + 1 < B * NC:
                    layer0(n + 1, n)
            for t in range(TPC):
                add_output(B * NC - 1, t)

        @block.tensor
        def _(pe):
            mm = nc.tensor.matmul

            waited = {"wq": ("wq", 32), "g": ("wv", 32), "gu": ("gu", 32), "wd": ("wd", 32)}
            for i, (kind, j) in enumerate(BANKS):
                name, value = waited[kind]
                pe.wait_ge(ld[name], value)
                if i == H // 4 + 1:
                    pe.wait_ge(ld["const"], 16)
                    pe.wait_ge(prep_dve, 2)
                    mm(ps[0:64, 7, 0:1], blk[0:64, :], bsm[:, 1:2], start=True, stop=True).then_inc(sums_ready, 1)
                if i == H // 4 + 7:
                    pe.wait_ge(prep_dve, 6)
                if i >= 4:
                    if i - 4 >= SUMS:
                        pe.wait_ge(prep_sum, i - 4 - SUMS + 1)
                    else:
                        pe.wait_ge(prep_lo, i - 4 + 1)
                dst = ps[:, bank_of(i), :]
                if kind == "wq":
                    k, hh = j // 2, j % 2
                    for a in range(8):
                        h = 8 * hh + a
                        last = mm(dst[:, 64 * a:64 * a + 64], r_wqT[:, h, 128 * k:128 * k + 128], r_wkT[:, h, :],
                                  start=True, stop=True)
                elif kind == "g":
                    for a in range(2):
                        for r in range(2):
                            h = 2 * (2 * j + a) + r
                            last = mm(ps[64 * r:64 * r + 64, bank_of(i), a * D:a * D + D], r_wvT[:, h, :],
                                      r_wo[:, h, :], start=True, stop=True)
                elif kind == "gu":
                    k, g = j // 2, j % 2
                    sa = r_lora[32 * g:32 * g + RANK, 128 * k:128 * k + 128]
                    for n0, n1 in ((0, 512), (512, DFF)):
                        last = mm(ps[:, bank_of(i) + n0 // 512, 0:n1 - n0], sa,
                                  r_lora[32 * g:32 * g + RANK, D + n0:D + n1], start=True, stop=True)
                else:
                    for a in range(2):
                        m0, w = FM[2 * j + a]
                        last = mm(dst[0:w, a * D:a * D + D], r_lora[64:64 + RANK, m0:m0 + w],
                                  r_lora[64:64 + RANK, DFF:DFF + D], start=True, stop=True)
                last.then_inc(prep_mm, 1)
            pe.wait_ge(prep_done, 1)
            pe.wait_ge(ld["l0"], 64)
            pe.wait_ge(ld["kva"], 64)

            def split3(ps_out, pairs, start=True, stop=True):
                for i, ((lh, ll), (rh, rl_)) in enumerate(pairs):
                    mm(ps_out, lh, rh, start=start and i == 0, stop=False)
                    mm(ps_out, lh, rl_, start=False, stop=False)
                    last = mm(ps_out, ll, rh, start=False, stop=stop and i == len(pairs) - 1)
                return last

            def transposes(i):
                for g in range(2):
                    pe.wait_ge(S["xn_ready"], 2 * i + g + 1)
                    for k in range(KD):
                        for t in (2 * g, 2 * g + 1):
                            last = nc.tensor.transpose(ps[:, 6 + k, t * 128:t * 128 + 128],
                                                       xn[:, t, k * 128:k * 128 + 128], ident)
                last.then_inc(S["xT_ready"], 1)

            def output_half(n, i):
                t, half = i // 2, i % 2
                tok = slice(t * 128, t * 128 + 128)
                if n == B * NC - 1 and i == 0:
                    pe.wait_ge(S["ctl_ready"], n * H // 2 + H // 4)
                elif i == 0 or n == B * NC - 1 and i == 1:
                    pe.wait_ge(S["ctl_ready"], (n + 1) * H // 2)
                if half == 0 and t >= 2 and n < B * NC - 1:
                    pe.wait_ge(S["out_added"], n * TPC + t - 1)
                last = split3(ps[:, output_bank(n, t), 0:D], [((QTH[:, h, tok], QTL[:, h, tok]), (GH[:, h, :], GL[:, h, :]))
                                                  for h in range(half * H // 4, (half + 1) * H // 4)],
                              start=half == 0, stop=half == 1)
                if half:
                    last.then_inc(S["o_ready"], 1)

            def layer0(n, prev):
                def output(*halves):
                    if prev is not None:
                        for i in halves:
                            output_half(prev, i)

                if prev is None:
                    transposes(2 * n)
                pe.wait_ge(S["xnT_ready"], 2 * n + 1)
                for g in range(KD):
                    for k in range(KD):
                        last = mm(ps[:, 6 + g, :], wq0[:, k, g * 128:g * 128 + 128], xnT[:, k, :],
                                  start=k == 0, stop=k == KD - 1)
                    last.then_inc(S["q_ready"], 1)

                def ffn0(q):
                    i = n * 4 + q
                    if q >= 1:
                        pe.wait_ge(S["up_copied"], i)
                    if q == 2:
                        pe.wait_ge(S["sn_ready"], n * 8 + 8)
                    for g in range(2):
                        for a in range(2):
                            h = 2 * q + a
                            for k in range(KD):
                                last = mm(ps[:, 2 + 2 * g + a, :], wg8[:, k, g, h * 128:h * 128 + 128],
                                          xq8[:, k, :], start=k == 0, stop=k == KD - 1)
                    last.then_inc(S["gu_ready"], 1)

                pe.wait_ge(S["xq8_ready"], n + 1)
                ffn0(0)
                output(0)
                pe.wait_ge(S["sig_ready"], n + 1)
                for r in range(2):
                    for k in range(KD):
                        last = mm(ps[64 * r:64 * r + 64, 6, 0:CH // 2], mnorm[:, k, :],
                                  sig[:, k, r * CH // 2:(r + 1) * CH // 2], start=k == 0, stop=k == KD - 1)
                last.then_inc(S["norm_ready"], 1)
                output(1)
                ffn0(1)
                output(2, 3, 4)

                def spread(j):
                    if j >= 4:
                        pe.wait_ge(S["sn_ready"], n * 8 + j - 3)
                    mm(ps[:, 2 + j % 4, :], selb[:, j, :], rsplit[:, :], start=True, stop=True) \
                        .then_inc(S["rbc_ready"], 1)

                def combine(j):
                    g, bank = j // 4, j % 4
                    pe.wait_ge(S["sn_ready"], n * 8 + j + 1)
                    mm(ps[:, 6 + g, :], mem[:, j, :], sn[:, j % 4], start=bank == 0, stop=bank == 3) \
                        .then_inc(S["comb_done"], 1)

                pe.wait_ge(S["r_ready"], n + 1)
                pe.wait_ge(S["up_copied"], n * 4 + 2)
                for j in range(4):
                    spread(j)
                for j in range(8):
                    if j == 6:
                        ffn0(2)
                    combine(j)
                    if j + 4 < 8:
                        spread(j + 4)
                ffn0(3)
                pe.wait_ge(S["combT_ready"], n + 1)
                for t in range(TPC):
                    for k in range(KD):
                        last = mm(token_major(6, t), combT[:, k, t * 128:t * 128 + 128], wo0[:, k, :],
                                  start=k == 0, stop=k == KD - 1)
                last.then_inc(S["y1_ready"], 1)
                output(5, 6)
                pe.wait_ge(S["y1_added"], n + 1)
                for q in range(4):
                    pe.wait_ge(S["act8_ready"], n * 4 + q + 1)
                    for g in range(2):
                        for k in (2 * q, 2 * q + 1):
                            for t in (2 * g, 2 * g + 1):
                                last = mm(token_major(6, t), act8[:, k, t * 128:t * 128 + 128], wl8[:, k, :],
                                          start=k == 0 and t % 2 == 0, stop=k == 7 and t % 2 == 1)
                        if q == 3:
                            last.then_inc(S["y0_ready"], 1)
                output(7)

            def layer1(n):
                b, c = n // NC, n % NC
                transposes(2 * n + 1)
                pe.wait_ge(S["xnT_ready"], 2 * n + 2)
                if n:
                    pe.wait_ge(S["out_added"], n * TPC)
                for t in range(TPC):
                    for k in range(KD):
                        last = mm(token_major(0, t)[:, 0:136], xnT[:, k, t * 128:t * 128 + 128], ra[:, k, :],
                                  start=k == 0, stop=k == KD - 1)
                last.then_inc(S["ra_ready"], 1)
                pe.wait_ge(S["xsplit_ready"], n + 1)
                for t in range(TPC):
                    tok = slice(t * 128, t * 128 + 128)
                    last = split3(ps[:, 6, tok], [((XH[:, k, tok], XL[:, k, tok]), (KVH[:, k, :], KVL[:, k, :]))
                                                  for k in range(KD)])
                last.then_inc(S["kvc_ready"], 1)

                def gate_up(m):
                    m0, w = FM[m]
                    if m >= 2:
                        pe.wait_ge(S["hf_ready"], n * NM + m - 1)
                    for g in range(2):
                        split3(ps[0:w, 2 + 2 * (m % 2) + g, :],
                               [((GUH[:, k, g, m0:m0 + w], GUL[:, k, g, m0:m0 + w]), (XH[:, k, :], XL[:, k, :]))
                                for k in range(KD)], stop=False)

                def gate_up_experts(m):
                    m0, w = FM[m]
                    for g in range(2):
                        r = slice(64 * g, 64 * g + 64)
                        last = split3(ps[0:w, 2 + 2 * (m % 2) + g, :],
                                      [((BGH[r, m0:m0 + w], BGL[r, m0:m0 + w]), (ZH[r, :], ZL[r, :]))], start=False)
                    last.then_inc(S["m_ready"], 1)

                gate_up(0)
                pe.wait_ge(S["xaw_ready"], n + 1)
                for t in range(TPC):
                    last = nc.tensor.transpose(ps[:, 1, t * 128:t * 128 + 128], xaw[:, t, :], ident)
                last.then_inc(S["xawT_ready"], 1)
                gate_up(1)
                pe.wait_ge(S["zl_ready"], n + 1)
                gate_up_experts(0)
                gate_up_experts(1)
                pe.wait_ge(S["ktok_ready"], n + 1)
                for t in range(TPC):
                    last = nc.tensor.transpose(ps[:, 7, t * 128:t * 128 + 128], ktok[:, t, :], ident)
                last.then_inc(S["kT_ready"], 1)
                for m in range(2, NM):
                    gate_up(m)
                    gate_up_experts(m)
                pe.wait_ge(S["ktl_ready"], n + 1)

                def down(ms):
                    for m in ms:
                        w = FM[m][1]
                        pe.wait_ge(S["hs_ready"], n * NM + m + 1)
                        for t in range(TPC):
                            tok = slice(t * 128, t * 128 + 128)
                            split3(token_major(6, t), [((HH[0:w, m, tok], HL[0:w, m, tok]),
                                                        (WDH[0:w, m, :], WDL[0:w, m, :]))],
                                   start=m == 0 and t % 2 == 0, stop=False)

                down((0, 1, 2))
                pe.wait_ge(S["hs_ready"], n * NM + NM)
                for t in range(TPC):
                    tok = slice(t * 128, t * 128 + 128)
                    last = split3(ps[:, 1, t * 64:t * 64 + 64],
                                  [((HH[0:w, m, tok], HL[0:w, m, tok]), (ADH[0:w, m, :], ADL[0:w, m, :]))
                                   for m, (_, w) in enumerate(FM)])
                last.then_inc(S["z_ready"], 1)
                down((3,))
                pe.wait_ge(S["zw_ready"], n + 1)
                for t in range(TPC):
                    last = nc.tensor.transpose(ps[0:64, 0, t * 128:t * 128 + 128], zw[:, t, :], ident)
                last.then_inc(S["z2T_ready"], 1)
                down(range(4, NM))
                pe.wait_ge(S["z2l_ready"], n + 1)
                for t in range(TPC):
                    tok = slice(t * 128, t * 128 + 128)
                    last = split3(token_major(6, t),
                                  [((Z2H[0:64, tok], Z2L[0:64, tok]), (BDH[:, :], BDL[:, :]))], start=False,
                                  stop=t % 2 == 1)
                last.then_inc(S["y2_ready"], 1)

                def project(i):
                    u, (q, t) = n * 16 + i, query_step(i)
                    tok = slice(t * 128, t * 128 + 128)
                    if i >= 2:
                        pe.wait_ge(S["qn_ready"], u - 1)
                    split3(ps[:, i % 2, :],
                           [((XH[:, k, tok], XL[:, k, tok]),
                             (WQH[:, k, 4 * q:4 * q + 4, :].rearrange("p h c -> p (h c)"),
                              WQL[:, k, 4 * q:4 * q + 4, :].rearrange("p h c -> p (h c)")))
                            for k in range(KD)]).then_inc(S["qp_ready"], 1)

                def turn(i):
                    u = n * 16 + i
                    pe.wait_ge(S["qr_ready"], u + 1)
                    if i >= 2:
                        pe.wait_ge(S["qtl_ready"], u - 1)
                    for a in range(4):
                        last = nc.tensor.transpose(ps[:, 2 + i % 2, a * 128:a * 128 + 128], qtok[:, i % 4, a, :],
                                                   ident)
                    last.then_inc(S["qt_ready"], 1)

                NJ = TPC * (c + 1)

                def jn(h, j):
                    return b * (3 * TPC * H) + c * (TPC * H) + h * NJ + j

                def query(q, h, t0, t1):
                    if isinstance(h, int):
                        return q[:, h, t0 * 128:t1 * 128]
                    return q[:, bass.ds(h, 1), t0 * 128:t1 * 128].rearrange("p a n -> p (a n)")

                def units(j):
                    return (0, 1) if j == 0 else (j + 1,) if j + 1 < NJ else ()

                def rough_scores(h, j):
                    t, half = j // (c + 1), j % (c + 1)
                    w = (t + 1) * 128 if half == c else 512
                    first = isinstance(h, int) and h == 0
                    bank = j % 2 + (4 if first else 0)
                    if not (first and j < 2):
                        pe.wait_ge(S["max_ready"], jn(h, j) - 1)
                    elif j == 0:
                        pe.wait_ge(S["qth_ready"], n * 16 + TPC)
                    last = mm(ps[:, bank, 0:w], query(QTH, h, t, t + 1), KTH[:, half * 512:half * 512 + w],
                              start=True, stop=half < c)
                    if half == c:
                        last = mm(ps[:, bank, w - 128:w], identb[:, :], maskb[:, :], start=False, stop=True)
                    last.then_inc(S["rough_ready"], 1)

                def scores(h, j):
                    t0 = max(0, j - TPC * c)
                    if not (isinstance(h, int) and h == 0 and j < 2):
                        pe.wait_ge(S["ph_ready"], jn(h, j) - 1)
                    dst, key = ps[:, 4 + j % 2, t0 * 128:CH], slice(j * 128, j * 128 + 128)
                    qh, ql = query(QTH, h, t0, TPC), query(QTL, h, t0, TPC)
                    mm(dst, KTH[:, key], qh, start=True, stop=False)
                    mm(dst, KTH[:, key], ql, start=False, stop=False)
                    mm(dst, KTL[:, key], qh, start=False, stop=False)

                def turn_max(h):
                    if isinstance(h, int) and h == 0:
                        pe.wait_ge(S["qtl_ready"], n * 16 + 15)
                    pe.wait_ge(S["nms_ready"], n * H + h + 1)
                    mm(ps[0:2 * TPC, 2, 0:128], nms[:, :], identb[:, :], start=True, stop=True) \
                        .then_inc(S["maxT_made"], 1)

                def less_max(h, j):
                    t0 = max(0, j - TPC * c)
                    if j == 0:
                        pe.wait_ge(S["maxT_ready"], n * H + h + 1)
                    if j >= TPC * c:
                        mm(ps[:, 4 + j % 2, t0 * 128:t0 * 128 + 128], maskb[:, :], identb[:, :],
                           start=False, stop=False)
                    for t in range(t0, TPC):
                        last = mm(ps[:, 4 + j % 2, t * 128:t * 128 + 128], tilesel[:, t, :], maxT[:, :],
                                  start=False, stop=t == TPC - 1)
                    last.then_inc(S["st_ready"], 1)

                def values(h, j):
                    if j == 0 and not (isinstance(h, int) and h == 0):
                        pe.wait_ge(S["cv_ready"], (n * H + h) * 2)
                    pe.wait_ge(S["pl_ready"], jn(h, j) + 1)
                    for t in range(max(0, j - TPC * c), TPC):
                        dst, tok = token_major(6, t)[:, 0:129], slice(t * 128, t * 128 + 128)
                        mm(dst, PH[:, j % RING, tok], LAT[:, j, 0:129],
                           start=j == 0 and t % 2 == 0, stop=False)
                        last = mm(dst, PL[:, j % RING, tok], LAT[:, j, 0:129], start=False,
                                  stop=j == TPC * c + t and t % 2 == 1)
                    last.then_inc(S["pv_done"], 1)

                def turn_context(pair):
                    pe.wait_ge(S["ctok_ready"], (n * H + pair * 2 + 2) * 2)
                    if not isinstance(pair, int) or pair:
                        pe.wait_ge(S["ctl_ready"], n * (H // 2) + pair)
                    for t in range(TPC):
                        last = nc.tensor.transpose(ps[:, 3, t * 128:t * 128 + 128], ctok[:, t, :], ident)
                    last.then_inc(S["ct_ready"], 1)

                def step(h, pair=None, first=False, last=False):
                    for j in range(NJ):
                        if not last:
                            for u in units(j):
                                rough_scores(h + 1, u)
                        if j == 0:
                            turn_max(h)
                        scores(h, j)
                        if j >= LAG:
                            values(h, j - LAG)
                        elif not first:
                            values(h - 1, NJ - LAG + j)
                        less_max(h, j)
                        if pair is not None and j == 0:
                            turn_context(pair)

                for i in range(18):
                    if i < 16:
                        project(i)
                    if i >= 2:
                        turn(i - 2)
                    for j in first_unit(i, NJ):
                        rough_scores(0, j)
                step(0, first=True)
                step(1)
                with pe.Fori(1, H // 2 - 1) as hp:
                    step(hp * 2)
                    step(hp * 2 + 1, pair=hp - 1)
                step(H - 2)
                step(H - 1, pair=H // 2 - 2, last=True)
                for j in range(NJ - LAG, NJ):
                    values(H - 1, j)
                if n + 1 < B * NC:
                    pe.wait_ge(S["cv_ready"], (n + 1) * H * 2)
                    transposes(2 * n + 2)
                else:
                    output_half(n, 0)
                turn_context(H // 2 - 1)
                if n + 1 == B * NC:
                    for t in range(1, TPC):
                        output_half(n, 2 * t)

            layer0(0, None)
            for n in range(B * NC):
                layer1(n)
                if n + 1 < B * NC:
                    layer0(n + 1, n)
            for t in range(TPC):
                output_half(B * NC - 1, 2 * t + 1)


def _constants(np):
    k = np.zeros((128, C_END), np.float32)
    k[:, C_ID:C_ID + 128] = np.eye(128, dtype=np.float32)
    q, key = np.arange(128)[:, None], np.arange(128)[None, :]
    k[:, C_MASK:C_MASK + 128] = np.where(key > q, np.float32(MASKED), np.float32(0))
    sel = np.zeros((64, KD, NB, 128), np.float32)
    for g in range(KD):
        for n in range(NB):
            for h in range(8):
                sel[n * H0 + g * 8 + h, g, n, h * D0:(h + 1) * D0] = 1
    k[:, C_SEL:C_TRI] = np.tile(sel.reshape(64, -1), (2, 1))
    e = np.arange(E)
    k[:, C_TRI:C_BLK] = (e[None, :] < e[:, None]).astype(np.float32).reshape(1, 64)
    r = np.arange(64) // H0
    k[0:64, C_BLK:C_COS] = (r[:, None] == r[None, :]).astype(np.float32)
    inv = (np.float32(1) / np.float32(10000.0) ** (np.arange(0, ROPE, 2, dtype=np.float32) / np.float32(ROPE)))
    f = np.outer(np.arange(T, dtype=np.float32), inv.astype(np.float32)).astype(np.float32)
    cos = np.cos(f.astype(np.float64)).astype(np.float32)
    sin = np.sin(f.astype(np.float64)).astype(np.float32)
    cos = np.concatenate([cos, cos], 1).reshape(T // 128, 128, ROPE).transpose(1, 0, 2)
    sin = np.concatenate([-sin, sin], 1).reshape(T // 128, 128, ROPE).transpose(1, 0, 2)
    k[:, C_COS:C_SIN] = cos.reshape(128, -1)
    k[:, C_SIN:C_END] = sin.reshape(128, -1)
    return k


def kernel(**inputs):
    import numpy as np
    import concourse.bacc as bacc
    from concourse.bass_utils import run_bass_kernel_spmd

    i = {n: np.asarray(a) for n, a in inputs.items()}
    mems, norms = i["L0_attn_memories"], i["L0_attn_memory_norms"]
    mem = np.zeros((128, KD, NB, 128), np.float32)
    mnorm = np.zeros((128, KD, NB, H0), np.float32)
    for g in range(KD):
        for n in range(NB):
            for h in range(8):
                r = slice(h * D0, (h + 1) * D0)
                mem[r, g, n, r] = mems[n, g * 8 + h]
                mnorm[r, g, n, g * 8 + h] = norms[n, g * 8 + h]
    bank = i["L0_attn_bank_weights"]
    wq = i["L1_attn_wq"].reshape(D, H, NOPE + ROPE)
    wkv = i["L1_attn_wkv_b"].reshape(KVR, H, NOPE + VD)
    a_gate = i["L1_ffn_A_gate"].transpose(1, 0, 2).reshape(D, E * RANK)
    a_up = i["L1_ffn_A_up"].transpose(1, 0, 2).reshape(D, E * RANK)
    lora = np.zeros((72, DFF + D), np.float32)
    for g, (a, bm) in enumerate((("sA_gate", "sB_gate"), ("sA_up", "sB_up"), ("sA_down", "sB_down"))):
        a, bm = i["L1_ffn_" + a].T, i["L1_ffn_" + bm]
        lora[32 * g:32 * g + RANK, 0:a.shape[1]] = a
        lora[32 * g:32 * g + RANK, a.shape[1]:] = bm
    arrays = {
        "x": i["L0_attn_hidden_states"],
        "const": _constants(np),
        "wq0": i["L0_attn_Wq"].T,
        "wo0": i["L0_attn_Wo"].T,
        "mem": mem.reshape(128, 8, 128),
        "mnorm": mnorm.reshape(128, KD, 64),
        "mrow": norms.reshape(64, D0),
        "bw": np.tile(bank, (NB, 1)),
        "bwself": bank.T.reshape(64, 1),
        "wg": i["L0_ffn_w_gating"].transpose(1, 0, 2),
        "wl": i["L0_ffn_w_linear"],
        "wqT": wq[:, :, 0:NOPE].transpose(2, 1, 0),
        "wkT": wkv[:, :, 0:NOPE].transpose(2, 1, 0),
        "wqr": wq[:, :, NOPE:],
        "wvT": wkv[:, :, NOPE:].transpose(2, 1, 0),
        "wo": i["L1_attn_wo"],
        "wkva": i["L1_attn_wkv_a"],
        "kvw": i["L1_attn_kv_norm_w"],
        "ra": np.concatenate([i["L1_ffn_W_router"], a_gate, a_up], 1),
        "wgu": np.stack([i["L1_ffn_W_gate"], i["L1_ffn_W_up"]], 1),
        "wd": i["L1_ffn_W_down"],
        "lora": lora,
        "bgu": np.concatenate([i["L1_ffn_B_gate"].reshape(64, DFF), i["L1_ffn_B_up"].reshape(64, DFF)], 0),
        "ad": i["L1_ffn_A_down"].transpose(1, 0, 2).reshape(DFF, 64),
        "bd": i["L1_ffn_B_down"].reshape(64, D),
        "ebias": i["L1_ffn_expert_bias"],
    }
    nc = bacc.Bacc("TRN2", target_bir_lowering=False, num_devices=1)
    ins, args = {}, []
    for name, a in arrays.items():
        a = np.ascontiguousarray(a)
        ins[name + "_dram"] = a
        args.append(nc.dram_tensor(name + "_dram", a.shape, mybir.dt.from_np(a.dtype), kind="ExternalInput").ap())
    args.append(nc.dram_tensor("out_dram", (B, T, D), mybir.dt.float32, kind="ExternalOutput").ap())
    fused_two_layers(nc, *args)
    r = run_bass_kernel_spmd(nc, [ins], core_ids=[0])
    return r.results[0]["out_dram"]
```
